# Optimizing a Trainium2 kernel written in Bass

```python
import numpy as np
import jax
import jax.numpy as jnp

def _softmax(x, axis=-1):
    return jax.nn.softmax(x, axis=axis)

def _gelu(x):
    return jax.nn.gelu(x, approximate=True)

def _silu(x):
    return jax.nn.silu(x)

def _sigmoid(x):
    return jax.nn.sigmoid(x)

def _layernorm(x, axis=-1, eps=1e-05):
    m = jnp.mean(x, axis=axis, keepdims=True)
    v = jnp.var(x, axis=axis, keepdims=True)
    return (x - m) / jnp.sqrt(v + eps)

def _scatter_add(tgt, idx, src, axis=0):
    return tgt.at[idx].add(src)

def _segment_sum(src, seg, n):
    return jax.ops.segment_sum(src, seg, n)
kernel_name = 'mk_gps_d1_gnn_r8_ee9f48'

def setup_inputs(seed: int=0):
    np.random.seed(seed)
    _w = jnp.asarray

    def _rec_inputs():
        import jax
        import jax.numpy as jnp
        _gk = jax.random.key(seed)
        x = -0.0003713 + 1 * jax.random.normal(jax.random.fold_in(_gk, 1), (6250, 256), jnp.float32)
        _s = jax.random.randint(jax.random.fold_in(_gk, 2), (50000,), 0, 6250, jnp.int32)
        _d = jax.random.randint(jax.random.fold_in(_gk, 3), (50000,), 0, 6250, jnp.int32)
        _loop = jnp.arange(6250, dtype=jnp.int32)
        src = jnp.concatenate([_s, _d, _loop])
        dst = jnp.concatenate([_d, _s, _loop])
        _o = jnp.argsort(dst, stable=True)
        src = src[_o]
        dst = dst[_o]
        return (x, src, dst)
    x, src, dst = _rec_inputs()

    def _L0_gnn_setup():
        import jax, jax.numpy as jnp
        import numpy as np
        N_NODES = 6250
        N_EDGES = 200000
        IN_FEATS = 256
        HIDDEN = 512
        OUT_FEATS = 256
        EPS = 0.0
        key = jax.random.key(seed)
        ks = jax.random.split(key, 6)
        x = jax.random.normal(ks[0], (N_NODES, IN_FEATS), dtype=jnp.float32)
        edge_row = jax.random.randint(ks[1], (N_EDGES,), 0, N_NODES, dtype=jnp.int32)
        edge_col = jax.random.randint(ks[2], (N_EDGES,), 0, N_NODES, dtype=jnp.int32)
        W1 = jax.random.uniform(ks[3], (IN_FEATS, HIDDEN), dtype=jnp.float32, minval=-1.0 / np.sqrt(IN_FEATS), maxval=1.0 / np.sqrt(IN_FEATS))
        b1 = jnp.zeros((HIDDEN,), dtype=jnp.float32)
        W2 = jax.random.uniform(ks[4], (HIDDEN, OUT_FEATS), dtype=jnp.float32, minval=-1.0 / np.sqrt(HIDDEN), maxval=1.0 / np.sqrt(HIDDEN))
        b2 = jnp.zeros((OUT_FEATS,), dtype=jnp.float32)
        return {'x': x, 'edge_row': edge_row, 'edge_col': edge_col, 'W1': W1, 'b1': b1, 'W2': W2, 'b2': b2}
    _L0_gnn_all = _L0_gnn_setup()
    _L0_gnn_in = {k: v for k, v in _L0_gnn_all.items() if k in ('W1', 'b1', 'W2', 'b2')}
    del _L0_gnn_all

    def _L0_mix_setup():
        import jax, jax.numpy as jnp
        import numpy as np
        B, N, C = (8, 1024, 256)
        H, D, S = (8, 32, 32)
        HID = 4 * C

        def layernorm(x, w, b, eps=1e-05):
            mu = jnp.mean(x, axis=-1, keepdims=True)
            var = jnp.mean(jnp.square(x - mu), axis=-1, keepdims=True)
            return (x - mu) * jax.lax.rsqrt(var + eps) * w + b

        def linear_no_attn(x, Wx, bx, Wq, Wk, Wv, Wo, bo):
            x_mid = x @ Wx.T + bx
            x_mid = x_mid.reshape(x.shape[0], x.shape[1], H, D).transpose(0, 2, 1, 3)
            q = jax.nn.softmax(x_mid @ Wq.T, axis=-1)
            k = jax.nn.softmax(x_mid @ Wk.T, axis=-2)
            v = x_mid @ Wv.T
            kv = jnp.einsum('bhns,bhnd->bhsd', k, v)
            qkv = jnp.einsum('bhns,bhsd->bhnd', q, kv)
            qkv = qkv.transpose(0, 2, 1, 3).reshape(x.shape[0], x.shape[1], H * D)
            return qkv @ Wo.T + bo
        key = jax.random.key(seed)
        ks = jax.random.split(key, 16)
        s = lambda fan: 1.0 / np.sqrt(fan)
        return {'fx': jax.random.normal(ks[0], (B, N, C), jnp.float32), 'ln1_w': jnp.ones((C,), jnp.float32), 'ln1_b': jnp.zeros((C,), jnp.float32), 'Wx': jax.random.uniform(ks[1], (C, C), jnp.float32, -s(C), s(C)), 'bx': jax.random.uniform(ks[2], (C,), jnp.float32, -s(C), s(C)), 'Wq': jax.random.uniform(ks[3], (S, D), jnp.float32, -s(D), s(D)), 'Wk': jax.random.uniform(ks[4], (S, D), jnp.float32, -s(D), s(D)), 'Wv': jax.random.uniform(ks[5], (D, D), jnp.float32, -s(D), s(D)), 'Wo': jax.random.uniform(ks[6], (C, C), jnp.float32, -s(C), s(C)), 'bo': jax.random.uniform(ks[7], (C,), jnp.float32, -s(C), s(C)), 'ln2_w': jnp.ones((C,), jnp.float32), 'ln2_b': jnp.zeros((C,), jnp.float32), 'W1': jax.random.uniform(ks[8], (HID, C), jnp.float32, -s(C), s(C)), 'b1': jax.random.uniform(ks[9], (HID,), jnp.float32, -s(C), s(C)), 'W2': jax.random.uniform(ks[10], (C, HID), jnp.float32, -s(HID), s(HID)), 'b2': jax.random.uniform(ks[11], (C,), jnp.float32, -s(HID), s(HID))}
    _L0_mix_all = _L0_mix_setup()
    _L0_mix_in = {k: v for k, v in _L0_mix_all.items() if k in ('ln1_w', 'ln1_b', 'Wx', 'bx', 'Wq', 'Wk', 'Wv', 'Wo', 'bo', 'ln2_w', 'ln2_b', 'W1', 'b1', 'W2', 'b2')}
    del _L0_mix_all

    def _L0_ffn_setup():
        import jax, jax.numpy as jnp
        import numpy as np
        TOP_K = 2
        LN_EPS = 1e-05
        key = jax.random.key(seed)
        ks = jax.random.split(key, 8)
        B, S, D, E, H = (16, 1024, 256, 8, 1024)
        x = jax.random.normal(ks[0], (B, S, D), dtype=jnp.float32)
        Wr = jax.random.normal(ks[1], (D, E), dtype=jnp.float32) * 0.1
        br = jnp.zeros((E,), dtype=jnp.float32)
        ln_g = jnp.ones((E, D), dtype=jnp.float32)
        ln_b = jnp.zeros((E, D), dtype=jnp.float32)
        W1 = jax.random.normal(ks[2], (E, D, H), dtype=jnp.float32) * (1.0 / np.sqrt(D))
        b1 = jnp.zeros((E, H), dtype=jnp.float32)
        W2 = jax.random.normal(ks[3], (E, H, D), dtype=jnp.float32) * (1.0 / np.sqrt(H))
        b2 = jnp.zeros((E, D), dtype=jnp.float32)
        return {'x': x, 'Wr': Wr, 'br': br, 'ln_g': ln_g, 'ln_b': ln_b, 'W1': W1, 'b1': b1, 'W2': W2, 'b2': b2}
    _L0_ffn_all = _L0_ffn_setup()
    _L0_ffn_in = {k: v for k, v in _L0_ffn_all.items() if k in ('Wr', 'br', 'ln_g', 'ln_b', 'W1', 'b1', 'W2', 'b2')}
    del _L0_ffn_all
    return {'x': x, 'src': src, 'dst': dst, 'L0_gnn_W1': _L0_gnn_in['W1'], 'L0_gnn_b1': _L0_gnn_in['b1'], 'L0_gnn_W2': _L0_gnn_in['W2'], 'L0_gnn_b2': _L0_gnn_in['b2'], 'L0_mix_ln1_w': _L0_mix_in['ln1_w'], 'L0_mix_ln1_b': _L0_mix_in['ln1_b'], 'L0_mix_Wx': _L0_mix_in['Wx'], 'L0_mix_bx': _L0_mix_in['bx'], 'L0_mix_Wq': _L0_mix_in['Wq'], 'L0_mix_Wk': _L0_mix_in['Wk'], 'L0_mix_Wv': _L0_mix_in['Wv'], 'L0_mix_Wo': _L0_mix_in['Wo'], 'L0_mix_bo': _L0_mix_in['bo'], 'L0_mix_ln2_w': _L0_mix_in['ln2_w'], 'L0_mix_ln2_b': _L0_mix_in['ln2_b'], 'L0_mix_W1': _L0_mix_in['W1'], 'L0_mix_b1': _L0_mix_in['b1'], 'L0_mix_W2': _L0_mix_in['W2'], 'L0_mix_b2': _L0_mix_in['b2'], 'L0_ffn_Wr': _L0_ffn_in['Wr'], 'L0_ffn_br': _L0_ffn_in['br'], 'L0_ffn_ln_g': _L0_ffn_in['ln_g'], 'L0_ffn_ln_b': _L0_ffn_in['ln_b'], 'L0_ffn_W1': _L0_ffn_in['W1'], 'L0_ffn_b1': _L0_ffn_in['b1'], 'L0_ffn_W2': _L0_ffn_in['W2'], 'L0_ffn_b2': _L0_ffn_in['b2']}

def reference(x, src, dst, L0_gnn_W1, L0_gnn_b1, L0_gnn_W2, L0_gnn_b2, L0_mix_ln1_w, L0_mix_ln1_b, L0_mix_Wx, L0_mix_bx, L0_mix_Wq, L0_mix_Wk, L0_mix_Wv, L0_mix_Wo, L0_mix_bo, L0_mix_ln2_w, L0_mix_ln2_b, L0_mix_W1, L0_mix_b1, L0_mix_W2, L0_mix_b2, L0_ffn_Wr, L0_ffn_br, L0_ffn_ln_g, L0_ffn_ln_b, L0_ffn_W1, L0_ffn_b1, L0_ffn_W2, L0_ffn_b2):
    import jax
    import jax.numpy as jnp

    def _L0_gnn_ref(x, edge_row, edge_col, W1, b1, W2, b2):
        import jax, jax.numpy as jnp
        import numpy as np
        N_NODES = 6250
        N_EDGES = 200000
        IN_FEATS = 256
        HIDDEN = 512
        OUT_FEATS = 256
        EPS = 0.0
        agg = jax.ops.segment_sum(x[edge_col], edge_row, num_segments=N_NODES)
        h = agg + (1.0 + EPS) * x
        h = h @ W1 + b1
        out = h @ W2 + b2
        return out

    def _L0_mix_ref(fx, ln1_w, ln1_b, Wx, bx, Wq, Wk, Wv, Wo, bo, ln2_w, ln2_b, W1, b1, W2, b2):
        import jax, jax.numpy as jnp
        import numpy as np
        B, N, C = (8, 1024, 256)
        H, D, S = (8, 32, 32)
        HID = 4 * C

        def layernorm(x, w, b, eps=1e-05):
            mu = jnp.mean(x, axis=-1, keepdims=True)
            var = jnp.mean(jnp.square(x - mu), axis=-1, keepdims=True)
            return (x - mu) * jax.lax.rsqrt(var + eps) * w + b

        def linear_no_attn(x, Wx, bx, Wq, Wk, Wv, Wo, bo):
            x_mid = x @ Wx.T + bx
            x_mid = x_mid.reshape(x.shape[0], x.shape[1], H, D).transpose(0, 2, 1, 3)
            q = jax.nn.softmax(x_mid @ Wq.T, axis=-1)
            k = jax.nn.softmax(x_mid @ Wk.T, axis=-2)
            v = x_mid @ Wv.T
            kv = jnp.einsum('bhns,bhnd->bhsd', k, v)
            qkv = jnp.einsum('bhns,bhsd->bhnd', q, kv)
            qkv = qkv.transpose(0, 2, 1, 3).reshape(x.shape[0], x.shape[1], H * D)
            return qkv @ Wo.T + bo
        h = linear_no_attn(layernorm(fx, ln1_w, ln1_b), Wx, bx, Wq, Wk, Wv, Wo, bo) + fx
        y = layernorm(h, ln2_w, ln2_b)
        y = jax.nn.gelu(y @ W1.T + b1, approximate=False)
        y = y @ W2.T + b2
        return y + h

    def _L0_ffn_ref(x, Wr, br, ln_g, ln_b, W1, b1, W2, b2):
        import jax, jax.numpy as jnp
        import numpy as np
        TOP_K = 2
        LN_EPS = 1e-05
        B, S, D = x.shape
        N = B * S
        xt = x.reshape(N, D)
        logits = xt @ Wr + br
        probs = jax.nn.softmax(logits, axis=-1)
        top_p, top_idx = jax.lax.top_k(probs, TOP_K)
        weights = top_p / top_p.sum(axis=-1, keepdims=True)
        mu = xt.mean(axis=-1, keepdims=True)
        var = ((xt - mu) ** 2).mean(axis=-1, keepdims=True)
        xn = (xt - mu) * jax.lax.rsqrt(var + LN_EPS)
        xe = xn[None, :, :] * ln_g[:, None, :] + ln_b[:, None, :]
        h = jax.nn.gelu(jnp.einsum('end,edh->enh', xe, W1) + b1[:, None, :], approximate=False)
        y = jnp.einsum('enh,ehd->end', h, W2) + b2[:, None, :]
        y_tok = jnp.transpose(y, (1, 0, 2))
        sel = jnp.take_along_axis(y_tok, top_idx[:, :, None], axis=1)
        out = (weights[:, :, None] * sel).sum(axis=1)
        return out.reshape(B, S, D)
    xn = _layernorm(x, axis=-1)
    x = x + _L0_gnn_ref(xn, src, dst, L0_gnn_W1, L0_gnn_b1, L0_gnn_W2, L0_gnn_b2) + _L0_mix_ref(xn[None], L0_mix_ln1_w, L0_mix_ln1_b, L0_mix_Wx, L0_mix_bx, L0_mix_Wq, L0_mix_Wk, L0_mix_Wv, L0_mix_Wo, L0_mix_bo, L0_mix_ln2_w, L0_mix_ln2_b, L0_mix_W1, L0_mix_b1, L0_mix_W2, L0_mix_b2)[0]
    x = x + _L0_ffn_ref(_layernorm(x, axis=-1)[None], L0_ffn_Wr, L0_ffn_br, L0_ffn_ln_g, L0_ffn_ln_b, L0_ffn_W1, L0_ffn_b1, L0_ffn_W2, L0_ffn_b2)[0]
    return x

_drawn_inputs = setup_inputs


def setup_inputs(seed=0):
    import zlib

    import numpy as np

    out = dict(_drawn_inputs(seed))
    spreads = {'L0_gnn_b1': (0.0, 2.0),
     'L0_gnn_b2': (0.0, 0.8),
     'L0_mix_ln1_w': (1.0, 0.6),
     'L0_mix_ln1_b': (0.0, 0.522),
     'L0_mix_ln2_w': (1.0, 0.6),
     'L0_mix_ln2_b': (0.0, 2.0),
     'L0_ffn_br': (0.0, 0.8),
     'L0_ffn_ln_g': (1.0, 0.6),
     'L0_ffn_ln_b': (0.0, 2.0),
     'L0_ffn_b1': (0.0, 2.0),
     'L0_ffn_b2': (0.0, 2.0)}
    factors = {'L0_mix_Wx': 4.212,
     'L0_mix_bx': 7.28,
     'L0_mix_Wq': 8.0,
     'L0_mix_Wk': 8.0,
     'L0_mix_Wv': 3.475,
     'L0_mix_Wo': 3.525,
     'L0_mix_bo': 23.024,
     'L0_mix_b1': 51.104,
     'L0_mix_b2': 33.816,
     'L0_mix_W1': 7.025,
     'L0_mix_W2': 5.986,
     'L0_ffn_Wr': 3.251,
     'L0_ffn_W1': 3.537,
     'L0_ffn_W2': 3.064}
    for name, (base, spread) in spreads.items():
        noise = np.random.default_rng([zlib.crc32(name.encode()), seed]).standard_normal(out[name].shape)
        drawn = base * np.exp(spread * noise) if base else spread * noise
        out[name] = jnp.asarray(drawn.astype(out[name].dtype))
    for name, factor in factors.items():
        out[name] = (out[name] * factor).astype(out[name].dtype)
    return out
```

```python
from contextlib import ExitStack

import concourse.bass as bass
from concourse import mybir

P = 128
C = 256
KC = C // P
F32 = mybir.dt.float32
I32 = mybir.dt.int32
U32 = mybir.dt.uint32
ALU = mybir.AluOpType
ACT = mybir.ActivationFunctionType
AX = mybir.AxisListType.X
LN_EPS = 1e-5
HEADS, HD = 8, 32
EXPERTS = 8
TILE_TOKENS = 256
RSQRT_SEED = 1597463007.0


class Chain:

    def __init__(self, eng, sem):
        self.eng, self.sem, self.base, self.k, self.i, self.per = eng, sem, 0, 0, None, 0

    def link(self, ins):
        ins.then_inc(self.sem, 1)
        self.k += 1
        at = self.base + self.k
        self.eng.wait_ge(self.sem, at if self.i is None else self.i * self.per + at)

    def enter(self, i, per):
        self.base += self.k
        self.k, self.i, self.per = 0, i, per

    def leave(self, times):
        assert self.k == self.per, (self.k, self.per)
        self.base += times * self.per
        self.k, self.i = 0, None


def rsqrt(v, link, y, x, t):
    link(v.tensor_scalar(t.bitcast(I32), x.bitcast(I32), 1, None, ALU.logical_shift_right))
    link(v.tensor_scalar(y.bitcast(I32), t.bitcast(I32), -1.0, RSQRT_SEED, ALU.mult, ALU.add))
    for _ in range(3):
        link(v.tensor_tensor(t, y, y, ALU.mult))
        link(v.scalar_tensor_tensor(t, t, -0.5, x, ALU.mult, ALU.mult))
        link(v.scalar_tensor_tensor(y, t, 1.5, y, ALU.add, ALU.mult))


RSQRT_LINKS = 11


def mean_var(v, link, st, mean, var, t):
    link(v.tensor_tensor(mean, st[:, :, 1], st[:, :, 4], ALU.add))
    link(v.tensor_scalar(mean, mean, 0.5, None, ALU.mult))
    link(v.tensor_tensor(t, st[:, :, 1], st[:, :, 4], ALU.subtract))
    link(v.tensor_tensor(t, t, t, ALU.mult))
    link(v.tensor_tensor(var, st[:, :, 2], st[:, :, 5], ALU.add))
    link(v.tensor_scalar(var, var, 1.0 / C, None, ALU.mult))
    link(v.scalar_tensor_tensor(var, t, 0.25, var, ALU.mult, ALU.add))


MEAN_VAR_LINKS = 7


def double_norm(v, link, var, rstd, rstd2, a, t):
    link(v.tensor_scalar(a, var, LN_EPS, None, ALU.add))
    rsqrt(v, link, rstd, a, t)
    link(v.tensor_tensor(a, rstd, rstd, ALU.mult))
    link(v.tensor_tensor(a, a, var, ALU.mult))
    link(v.tensor_scalar(a, a, LN_EPS, None, ALU.add))
    rsqrt(v, link, rstd2, a, t)
    link(v.tensor_tensor(rstd2, rstd2, rstd, ALU.mult))


def count_keys(v, ch, key, mask, ids, counts, n):
    with v.Fori(0, n) as b:
        ch.enter(b, 1)
        ch.link(v.tensor_scalar(mask, key, ids[:, bass.ds(b, 1)], 0.0, ALU.is_equal, ALU.add,
                                accum_out=counts[:, bass.ds(b, 1)]))
        ch.leave(n)


def bucket_starts(v, ch, base_total, n, align, cum, size, off, t_int, ones_row):
    shift = align.bit_length() - 1
    link = ch.link
    link(v.tensor_scalar(size, base_total[:, n:2 * n], float(align - 1), None, ALU.add))
    link(v.tensor_copy(t_int, size))
    link(v.tensor_scalar(t_int, t_int, shift, None, ALU.logical_shift_right))
    link(v.tensor_copy(size, t_int))
    link(v.tensor_tensor_scan(cum, ones_row, size, 0.0, ALU.mult, ALU.add))
    link(v.tensor_tensor(off, cum, size, ALU.subtract))
    link(v.scalar_tensor_tensor(off, off, float(align), base_total[:, 0:n], ALU.mult, ALU.add))


def place_keys(v, ch, key, mask, scan, pos, ids, off, n, idle):
    with v.Fori(0, n) as b:
        ch.enter(b, 3)
        ch.link(v.tensor_scalar(mask, key, ids[:, bass.ds(b, 1)], None, ALU.is_equal))
        ch.link(v.tensor_tensor_scan(scan, mask, mask, off[:, bass.ds(b, 1)], ALU.add, ALU.max))
        v.sem_inc(idle, 1)
        ch.link(v.copy_predicated(pos, mask.bitcast(I32), scan))
        ch.leave(n)


def tile_owner(v, ch, cum, n, unit_ids, ge, owner, owner_int, cols):
    link = ch.link
    link(v.tensor_tensor(ge, unit_ids.unsqueeze(2).broadcast_to([P, cols, n]),
                         cum.unsqueeze(1).broadcast_to([P, cols, n]), ALU.is_ge))
    link(v.tensor_reduce(owner, ge, AX, ALU.add))
    link(v.tensor_scalar(owner, owner, float(n - 1), None, ALU.min))
    link(v.tensor_copy(owner_int, owner))


def gps_layer(nc, w, out, NODES, ECOLS):
    NT = w["x"].shape[0] // P
    LAST = NODES - (NT - 1) * P
    PAIRS = NT // 2
    assert NT == 2 * PAIRS + 1 and PAIRS % 2 == 0 and NT % 7 == 0
    NCH = (ECOLS * P + NT * (P - 1)) // P
    NCH += -NCH % 16
    NCHP = NCH + 16
    CCOLS = -(-NCH // P)
    SCAT = 32
    assert ECOLS % SCAT == 0
    ACOLS = 2 * NT
    ETILES = (ACOLS * P + EXPERTS * (TILE_TOKENS - 1)) // TILE_TOKENS
    ETILES += ETILES % 2
    assert ETILES <= P
    HID = w["mix_W1T"].shape[1]
    HB = HID // P
    GH = w["gnn_W2"].shape[0] // P
    QK = 2 * C
    INV_P = 1.0 / P

    def dram(name, shape, dt=F32):
        return nc.dram_tensor(name, shape, dt, kind="Internal").ap()

    xn_d = dram("xn_d", (NT * P, C))
    q_d = dram("q_d", (NT * P, C))
    k_d = dram("k_d", (NT * P, C))
    xm_d = dram("xm_d", (NT * P, C))
    part_d = dram("part_d", (NT * P, C))
    elist_d = dram("elist_d", (P * NCH, 1), I32)
    chunk_d = dram("chunk_d", (CCOLS * P, 1), I32)
    etile_d = dram("etile_d", (P, 1), I32)
    xs_d = dram("xs_d", (ETILES * TILE_TOKENS, C))
    ys_d = dram("ys_d", (ETILES * TILE_TOKENS, C))

    outer = ExitStack()
    with outer:
        def tools(ctx, tag):
            sb = lambda name, shape, dt=F32: ctx.enter_context(nc.sbuf_tensor(f"{tag}_{name}", shape, dt))
            ps = lambda name, shape: ctx.enter_context(nc.psum_tensor(f"{tag}_{name}", shape, F32))
            sem = lambda name: ctx.enter_context(nc.semaphore(f"{tag}_{name}"))
            return sb, ps, sem

        sb, _, _ = tools(outer, "g")
        ident = sb("ident", [P, P])
        ones = sb("ones", [P, P])
        tri = sb("tri", [P, P])
        iota_b = sb("iota_b", [P, max(P, NT)])
        ids = iota_b[:, 0:NT]
        node_ids = iota_b[:, 0:P]
        unit_ids = sb("unit_ids", [P, CCOLS])
        part_ids = sb("part_ids", [P, 1])
        W12 = sb("W12", [P, KC, C])
        stat_mean = sb("mean", [P, NT])
        stat_a = sb("stat_a", [P, NT])
        stat_b = sb("stat_b", [P, NT])
        stats = sb("stats", [P, NT, 6])
        var = sb("var", [P, NT])
        rstd = sb("rstd", [P, NT])
        rstd2 = sb("rstd2", [P, NT])
        WR = sb("WR", [P, KC, EXPERTS])
        br = sb("br", [1, EXPERTS])
        chunk_owner = sb("chunk_owner", [P, CCOLS], I32)

        mixctx = ExitStack()
        with mixctx:
            sb, _, _ = tools(mixctx, "m")
            RA = sb("RA", [P, KC, 3 * C])
            RB = sb("RB", [1, 3 * C])
            G = sb("G", [P, KC, C])
            M = sb("M", [P, KC, C])
            bo = sb("bo", [1, C])
            bsum = sb("bsum", [1, C])
            W1f = sb("W1f", [P, KC, HID])
            b1f = sb("b1f", [P, HB])
            W2 = sb("W2", [P, HB, C])
            addr = sb("addr", [P, ECOLS], I32)
            rec = sb("rec", [P, ECOLS], I32)

            c1 = ExitStack()
            with c1:
                sb, ps, sem = tools(c1, "b1")
                xg = sb("xg", [P, 2, 7, C])
                src = sb("src", [P, ECOLS], I32)
                key = sb("key", [P, ECOLS])
                mask = sb("mask", [P, ECOLS])
                scan = sb("scan", [P, ECOLS])
                pos = sb("pos", [P, ECOLS])
                posi = src
                fill = sb("fill", [P, NCH], I32)
                counts = sb("counts", [P, NT])
                size = sb("size", [P, NT])
                cum = sb("cum", [P, NT])
                off = sb("off", [P, NT])
                t_int = sb("t_int", [P, NT], I32)
                ge = sb("ge", [P, CCOLS, NT])
                own_f = sb("own_f", [P, CCOLS])
                WxT = sb("WxT", [P, KC, C])
                Wx = sb("Wx", [P, KC, C])
                BD = sb("BD", [P, KC, QK])
                WvBD = sb("WvBD", [P, KC, C])
                WoT = sb("WoT", [P, KC, C])
                gW1T = sb("gW1T", [P, GH, C])
                gW2 = sb("gW2", [P, GH, C])
                cols = sb("cols", [P, 5 * KC + HB + GH])
                ln1w, ln1b, bxc, ln2w, ln2b = (cols[:, KC * n:KC * n + KC] for n in range(5))
                b1c = cols[:, 5 * KC:5 * KC + HB]
                gb1c = cols[:, 5 * KC + HB:]
                rows = sb("rows", [1, 3 * C])
                bxp = sb("bxp", [P, KC])
                fold = [ps(f"fold{n}", [P, QK]) for n in range(2)]
                cnt_ps = ps("cnt", [P, 2 * NT])

                const_done = sem("const_done")
                zero_done = sem("zero_done")
                edges_in = sem("edges_in")
                xg_in = [sem(f"xg_in{n}") for n in range(2)]
                xg_used = sem("xg_used")
                weights_in = sem("weights_in")
                diag_in = sem("diag_in")
                fold_mm = sem("fold_mm")
                fold_out = sem("fold_out")
                counted = sem("counted")
                summed = sem("summed")
                owners = sem("owners")
                dve = sem("dve")
                idle = sem("idle")
                act = sem("act")
                stored = sem("stored")
                filled = sem("filled")
                block = c1.enter_context(nc.Block())

                NG = NT // 7
                assert NG * 7 == NT

                @block.gpsimd
                def _(pool):
                    pool.memset(ones[:], 1.0).then_inc(const_done, 1)
                    pool.memset(ident[:], 0.0).then_inc(const_done, 1)
                    pool.memset(tri[:], 1.0).then_inc(const_done, 1)
                    pool.memset(BD[:], 0.0).then_inc(zero_done, 1)
                    pool.memset(WvBD[:], 0.0).then_inc(zero_done, 1)
                    pool.wait_ge(const_done, 3)
                    pool.affine_select(out=ident[:], in_=ident[:], compare_op=ALU.not_equal, fill=1.0, base=0,
                                       pattern=[[-1, P]], channel_multiplier=1).then_inc(const_done, 1)
                    pool.affine_select(out=tri[:], in_=tri[:], compare_op=ALU.is_gt, fill=0.0, base=0,
                                       pattern=[[1, P]], channel_multiplier=-1).then_inc(const_done, 1)
                    pool.iota(iota_b[:], [[1, max(P, NT)]], base=0, channel_multiplier=0,
                              allow_small_or_imprecise_dtypes=True).then_inc(const_done, 1)
                    pool.iota(unit_ids[:], [[1, CCOLS]], base=0, channel_multiplier=CCOLS,
                              allow_small_or_imprecise_dtypes=True).then_inc(const_done, 1)
                    pool.iota(part_ids[:], [[1, 1]], base=0, channel_multiplier=1,
                              allow_small_or_imprecise_dtypes=True).then_inc(const_done, 1)
                    pool.memset(fill[:], P).then_inc(const_done, 1)

                CONSTS = 9

                @block.sync
                def _(sp):
                    sp.dma_start(src[:], w["src"]).then_inc(edges_in, 16)
                    sp.dma_start(rec[:], w["dst"]).then_inc(edges_in, 16)
                    xt = w["x"].rearrange("(g t p) c -> g p t c", p=P, t=7)
                    for g in range(NG):
                        if g >= 2:
                            sp.wait_ge(xg_used, g - 1)
                        sp.dma_start(xg[:, g % 2], xt[g]).then_inc(xg_in[g % 2], 16)
                    sp.wait_ge(const_done, CONSTS)
                    sp.dma_start(elist_d.rearrange("(p n) a -> p (n a)", p=P), fill[:]).then_inc(filled, 16)
                    sp.wait_ge(owners, 1)
                    sp.dma_start(chunk_d.rearrange("(p n) a -> p (n a)", p=P), chunk_owner[:]).then_inc(stored, 16)
                    sp.wait_ge(filled, 16)
                    sp.wait_ge(stored, 16)

                NW = 15

                @block.scalar
                def _(a):
                    for dst, name in ((WxT, "mix_WxT"), (Wx, "mix_Wx"), (WoT, "mix_WoT"), (gW1T, "gnn_W1T"),
                                      (gW2, "gnn_W2"), (W1f, "mix_W1T"), (W2, "mix_W2T"), (WR, "ffn_Wr")):
                        a.dma_start(dst[:], w[name].rearrange("(k p) c -> p k c", p=P)).then_inc(weights_in, 16)
                    a.dma_start(cols[:], w["cols"]).then_inc(weights_in, 16)
                    a.dma_start(rows[0:1, 0:C], w["mix_bx"]).then_inc(weights_in, 16)
                    a.dma_start(rows[0:1, C:2 * C], w["gnn_b2"]).then_inc(weights_in, 16)
                    a.dma_start(rows[0:1, 2 * C:3 * C], w["mix_b2"]).then_inc(weights_in, 16)
                    a.dma_start(bo[:], w["mix_bo"]).then_inc(weights_in, 16)
                    a.dma_start(br[:], w["ffn_br"]).then_inc(weights_in, 16)
                    a.wait_ge(zero_done, 2)
                    n_diag = 0
                    for h in range(HEADS):
                        r, k = h * HD % P, h * HD // P
                        for dst, at, name in ((BD, 0, "mix_WqT"), (BD, C, "mix_WkT"), (WvBD, 0, "mix_Wv")):
                            a.dma_start(dst[r:r + HD, k, at + h * HD:at + h * HD + HD], w[name]).then_inc(diag_in, 16)
                            n_diag += 1
                    a.wait_ge(weights_in, 14 * 16)

                    def take(n):
                        a.wait_ge(fold_mm, n + 1)
                        return fold[n % 2]

                    for m in range(KC):
                        f = take(m)
                        a.activation(RA[:, m, 0:QK], f[:, 0:QK], ACT.Identity, scale=ln1w[:, m:m + 1]).then_inc(fold_out, 1)
                    for m in range(KC):
                        a.activation(RA[:, m, QK:], WxT[:, m, :], ACT.Identity, scale=ln1w[:, m:m + 1]).then_inc(act, 1)
                    f = take(2)
                    a.activation(bxp[:], f[:, 0:KC], ACT.Copy).then_inc(fold_out, 1)
                    f = take(3)
                    a.activation(RB[0:1, 0:QK], f[0:1, 0:QK], ACT.Copy).then_inc(fold_out, 1)
                    f = take(4)
                    a.activation(RB[0:1, QK:], f[0:1, 0:C], ACT.Copy).then_inc(fold_out, 1)
                    f = take(5)
                    a.activation(G[:, :, :].rearrange("p k c -> p (k c)"), f[:, 0:KC * C], ACT.Copy).then_inc(fold_out, 1)
                    f = take(6)
                    a.activation(W12[:, :, :].rearrange("p k c -> p (k c)"), f[:, 0:KC * C], ACT.Copy).then_inc(fold_out, 1)
                    f = take(7)
                    a.activation(bsum[:], f[0:1, 0:C], ACT.Copy).then_inc(fold_out, 1)
                    f = take(8)
                    a.activation(b1f[:], f[:, 0:HB], ACT.Copy).then_inc(fold_out, 1)
                    for m in range(KC):
                        a.activation(W1f[:, m, :], W1f[:, m, :], ACT.Identity, scale=ln2w[:, m:m + 1]).then_inc(act, 1)

                @block.tensor
                def _(pe):
                    pe.wait_ge(weights_in, 14 * 16)
                    pe.wait_ge(diag_in, 3 * HEADS * 16)
                    pe.wait_ge(const_done, CONSTS)

                    def room(n):
                        if n >= 2:
                            pe.wait_ge(fold_out, n - 1)
                        return fold[n % 2]

                    for m in range(KC):
                        f = room(m)
                        for k in range(KC):
                            mm = pe.matmul(f[:, 0:QK], Wx[:, k, m * P:m * P + P], BD[:, k, :], start=(k == 0), stop=(k == KC - 1))
                        mm.then_inc(fold_mm, 1)
                    f = room(2)
                    pe.matmul(f[:, 0:KC], ident[:], bxc, start=True, stop=False)
                    for m in range(KC):
                        for k in range(KC):
                            mm = pe.matmul(f[:, m:m + 1], WxT[:, k, m * P:m * P + P], ln1b[:, k:k + 1],
                                           start=False, stop=(m == KC - 1 and k == KC - 1))
                    mm.then_inc(fold_mm, 1)
                    f = room(3)
                    pe.wait_ge(fold_out, 3)
                    for k in range(KC):
                        mm = pe.matmul(f[0:1, 0:QK], bxp[:, k:k + 1], BD[:, k, :], start=(k == 0), stop=(k == KC - 1))
                    mm.then_inc(fold_mm, 1)
                    f = room(4)
                    pe.matmul(f[0:1, 0:C], ones[0:1, 0:1], rows[0:1, 0:C], start=True, stop=False)
                    for k in range(KC):
                        mm = pe.matmul(f[0:1, 0:C], ln1b[:, k:k + 1], WxT[:, k, :], start=False, stop=(k == KC - 1))
                    mm.then_inc(fold_mm, 1)
                    f = room(5)
                    for m in range(KC):
                        for k in range(KC):
                            mm = pe.matmul(f[:, m * C:m * C + C], WvBD[:, k, m * P:m * P + P], WoT[:, k, :],
                                           start=(k == 0), stop=(k == KC - 1))
                    mm.then_inc(fold_mm, 1)
                    f = room(6)
                    for m in range(KC):
                        for k in range(GH):
                            mm = pe.matmul(f[:, m * C:m * C + C], gW1T[:, k, m * P:m * P + P], gW2[:, k, :],
                                           start=(k == 0), stop=(k == GH - 1))
                    mm.then_inc(fold_mm, 1)
                    f = room(7)
                    pe.matmul(f[0:1, 0:C], ones[0:1, 0:1], rows[0:1, C:2 * C], start=True, stop=False)
                    pe.matmul(f[0:1, 0:C], ones[0:1, 0:1], rows[0:1, 2 * C:3 * C], start=False, stop=False)
                    for k in range(GH):
                        mm = pe.matmul(f[0:1, 0:C], gb1c[:, k:k + 1], gW2[:, k, :], start=False, stop=(k == GH - 1))
                    mm.then_inc(fold_mm, 1)
                    f = room(8)
                    pe.matmul(f[:, 0:HB], ident[:], b1c, start=True, stop=False)
                    for j in range(HB):
                        for k in range(KC):
                            mm = pe.matmul(f[:, j:j + 1], W1f[:, k, j * P:j * P + P], ln2b[:, k:k + 1],
                                           start=False, stop=(j == HB - 1 and k == KC - 1))
                    mm.then_inc(fold_mm, 1)
                    pe.wait_ge(counted, 1)
                    pe.matmul(cnt_ps[:, 0:NT], tri[:], counts[:], start=True, stop=True)
                    pe.matmul(cnt_ps[:, NT:2 * NT], ones[:], counts[:], start=True, stop=True).then_inc(summed, 1)

                @block.vector
                def _(v):
                    ch = Chain(v, dve)
                    link = ch.link
                    v.wait_ge(edges_in, 32)
                    v.wait_ge(const_done, CONSTS)
                    link(v.tensor_scalar(rec[:], rec[:], 8, None, ALU.logical_shift_left))
                    link(v.tensor_scalar(scan[:].bitcast(I32), src[:], P - 1, None, ALU.bitwise_and))
                    link(v.tensor_tensor(rec[:], rec[:], scan[:].bitcast(I32), ALU.bitwise_or))
                    link(v.tensor_scalar(src[:], src[:], 7, None, ALU.logical_shift_right))
                    link(v.tensor_copy(key[:], src[:]))
                    link(v.memset(pos[:], 0.0))
                    count_keys(v, ch, key[:], mask[:], ids, counts[:], NT)
                    v.sem_inc(counted, 1)
                    v.wait_ge(summed, 1)
                    bucket_starts(v, ch, cnt_ps, NT, P, cum[:], size[:], off[:], t_int[:], ones[:, 0:NT])
                    tile_owner(v, ch, cum[:], NT, unit_ids[:], ge[:], own_f[:], chunk_owner[:], CCOLS)
                    v.sem_inc(owners, 1)
                    place_keys(v, ch, key[:], mask[:], scan[:], pos[:], ids, off[:], NT, idle)
                    link(v.tensor_scalar(pos[:], pos[:], -1.0, None, ALU.add))
                    link(v.tensor_copy(posi[:], pos[:]))
                    link(v.tensor_scalar(addr[:], posi[:], P - 1, None, ALU.bitwise_and))
                    link(v.tensor_scalar(posi[:], posi[:], 7, None, ALU.logical_shift_right))
                    link(v.tensor_copy(pos[:], addr[:]))
                    link(v.tensor_copy(scan[:], posi[:]))
                    link(v.scalar_tensor_tensor(pos[:], pos[:], float(NCH), scan[:], ALU.mult, ALU.add))
                    link(v.tensor_copy(addr[:], pos[:]))
                    for g in range(NG):
                        v.wait_ge(xg_in[g % 2], 16 * (g // 2 + 1))
                        for t in range(7):
                            ins = v.bn_stats(stats[:, 7 * g + t, :], xg[:, g % 2, t, :])
                            if t == 6:
                                ins.then_inc(xg_used, 1)
                    v.wait_ge(xg_used, NG)
                    mean_var(v, link, stats, stat_mean[:], var[:], stat_a[:])
                    double_norm(v, link, var[:], rstd[:], rstd2[:], stat_a[:], stat_b[:])
                    link(v.scalar_tensor_tensor(stat_a[:], stat_mean[:], -1.0, rstd[:], ALU.mult, ALU.mult))

            c2 = ExitStack()
            with c2:
                sb, ps, sem = tools(c2, "b2")
                xt = sb("xt", [P, 2, C])
                z = sb("z", [P, 2, C])
                xn = sb("xn", [P, 2, C])
                zT = sb("zT", [P, 2, C])
                q = sb("q", [P, 2, C])
                k_s = sb("k_s", [P, 2, C])
                xm = sb("xm", [P, 2, C])
                mx = sb("mx", [P, HEADS])
                kmax = sb("kmax", [P, C])
                kmax_c = sb("kmax_c", [P, KC])
                diag = sb("diag", [P, KC, P])
                kmax_b = sb("kmax_b", [P, C])
                ke = sb("ke", [P, 2, C])
                KV = sb("KV", [P, KC, P])
                KVm = sb("KVm", [P, KC, P])
                hmask = sb("hmask", [P, P])
                rden = sb("rden", [P, KC])
                qx = sb("qx", [P, 2, 2, C])
                xnp = sb("xnp", [P, 2, 2, C])
                xp = sb("xp", [P, 2, 2, C])
                qT = sb("qT", [P, KC, C])
                h = sb("h", [P, 2, C])
                z2 = sb("z2", [P, 2, C])
                z2T = sb("z2T", [P, KC, C])
                hT = sb("hT", [P, HB, C])
                part = sb("part", [P, 2, C])
                pst = sb("pst", [P, 2, 6])
                pm, pv, pr, pa, pb = (sb(f"pair{n}", [P, 2]) for n in range(5))
                ring_a = sb("ring_a", [P, 2, SCAT // 2], I32)
                ring_r = sb("ring_r", [P, 2, SCAT // 2], I32)
                bank = [ps(f"bank{n}", [P, 512]) for n in range(8)]

                x_in = [sem(f"x_in{n}") for n in range(2)]
                z_ready = sem("z_ready")
                xn_ready = sem("xn_ready")
                xn_out = [sem(f"xn_out{n}") for n in range(2)]
                zT_mm = sem("zT_mm")
                zT_ready = sem("zT_ready")
                qkx_mm = sem("qkx_mm")
                q_shift = sem("q_shift")
                q_exp = sem("q_exp")
                kx_ready = sem("kx_ready")
                k_seen = sem("k_seen")
                q_ready = sem("q_ready")
                kx_out = [sem(f"kx_out{n}") for n in range(2)]
                q_out = [sem(f"q_out{n}") for n in range(2)]
                kT_mm = sem("kT_mm")
                kdiag = sem("kdiag")
                kmax_mm = sem("kmax_mm")
                kmax_ready = sem("kmax_ready")
                kx_in = [sem(f"kx_in{n}") for n in range(2)]
                k_sub = sem("k_sub")
                k_exp = sem("k_exp")
                kv_mm = sem("kv_mm")
                kv_ready = sem("kv_ready")
                M_mm = sem("M_mm")
                M_ready = sem("M_ready")
                pair_in = [sem(f"pair_in{n}") for n in range(2)]
                qT_mm = sem("qT_mm")
                qT_ready = sem("qT_ready")
                h_mm = sem("h_mm")
                z2_ready = sem("z2_ready")
                z2T_mm = sem("z2T_mm")
                z2T_ready = sem("z2T_ready")
                up_mm = sem("up_mm")
                gelu = sem("gelu")
                y_mm = sem("y_mm")
                part_ready = sem("part_ready")
                part_out = sem("part_out")
                dve = sem("dve")
                hm = sem("hm")
                idle = sem("idle")
                ring_ready = sem("ring_ready")
                sent = [sem(f"sent{n}") for n in range(2)]
                block = c2.enter_context(nc.Block())

                rows_of = lambda d, i, n=1: d[bass.ds(i * P, n * P), :]
                half = SCAT // 2

                @block.gpsimd
                def _(pool):
                    pool.memset(hmask[:], 0.0).then_inc(hm, 1)
                    pool.wait_ge(hm, 1)
                    for g in range(P // HD):
                        pool.memset(hmask[g * HD:g * HD + HD, g * HD:g * HD + HD], 1.0).then_inc(hm, 1)
                        pool.wait_ge(hm, g + 2)
                    with pool.Fori(0, ECOLS // SCAT) as i:
                        for s in range(2):
                            pool.wait_ge(sent[s], i * (16 * half))
                            pool.sem_inc(idle, 1)
                            at = i * SCAT + s * half
                            pool.tensor_copy(ring_a[:, s, :], addr[:, bass.ds(at, half)]).then_inc(ring_ready, 1)
                            pool.tensor_copy(ring_r[:, s, :], rec[:, bass.ds(at, half)]).then_inc(ring_ready, 1)
                            pool.wait_ge(ring_ready, i * 4 + 2 * s + 2)
                            pool.sem_inc(idle, 1)
                            for c in range(half):
                                pool.indirect_dma_start(
                                    out=elist_d, out_offset=bass.IndirectOffsetOnAxis(ap=ring_a[:, s, c:c + 1], axis=0),
                                    in_=ring_r[:, s, c:c + 1], in_offset=None).then_inc(sent[s], 16)
                    for s in range(2):
                        pool.wait_ge(sent[s], ECOLS // SCAT * 16 * half)

                @block.sync
                def _(sp):
                    def load_x(i, t, s, free):
                        if free is not None:
                            sp.wait_ge(z_ready, free)
                            sp.wait_ge(xn_ready, free)
                        sp.dma_start(xt[:, s], rows_of(w["x"], t)).then_inc(x_in[s], 16)

                    def store(t, n, s):
                        sp.wait_ge(xn_ready, n + 1)
                        sp.dma_start(rows_of(xn_d, t), xn[:, s]).then_inc(xn_out[s], 16)
                        sp.wait_ge(kx_ready, n * 2 + 2)
                        sp.dma_start(rows_of(k_d, t), k_s[:, s]).then_inc(kx_out[s], 16)
                        sp.dma_start(rows_of(xm_d, t), xm[:, s]).then_inc(kx_out[s], 16)
                        sp.wait_ge(q_ready, n + 1)
                        sp.dma_start(rows_of(q_d, t), q[:, s]).then_inc(q_out[s], 16)

                    load_x(0, 0, 0, None)
                    load_x(0, 1, 1, None)
                    with sp.Fori(0, PAIRS - 1) as i:
                        for s in range(2):
                            store(2 * i + s, 2 * i + s, s)
                            load_x(i, 2 * i + s + 2, s, 2 * i + s + 1)
                    for s in range(2):
                        store(NT - 3 + s, NT - 3 + s, s)
                        if s == 0:
                            load_x(0, NT - 1, 0, NT - 2)
                    store(NT - 1, NT - 1, 0)
                    halves = (PAIRS + 1, PAIRS)
                    for s in range(2):
                        sp.wait_ge(kx_out[s], 32 * halves[s])
                        sp.wait_ge(q_out[s], 16 * halves[s])
                        sp.wait_ge(xn_out[s], 16 * halves[s])

                    def load_kx(t, s, free):
                        if free is not None:
                            sp.wait_ge(kv_mm, free)
                        sp.dma_start(k_s[:, s], rows_of(k_d, t)).then_inc(kx_in[s], 16)
                        sp.dma_start(xm[:, s], rows_of(xm_d, t)).then_inc(kx_in[s], 16)

                    load_kx(0, 0, None)
                    load_kx(1, 1, None)
                    with sp.Fori(0, PAIRS - 1) as i:
                        for s in range(2):
                            load_kx(2 * i + s + 2, s, 2 * i + s + 1)
                    load_kx(NT - 1, 0, NT - 2)

                    def load_pair(i, s, n, free):
                        if free is not None:
                            sp.wait_ge(part_ready, free)
                        for dst, d in ((qx, q_d), (xnp, xn_d), (xp, w["x"])):
                            sp.dma_start(dst[:, s, 0:n, :], d[bass.ds(i * 2 * P, n * P), :].rearrange("(t p) c -> p t c", p=P))\
                              .then_inc(pair_in[s], 16)

                    def store_pair(i, n):
                        sp.wait_ge(part_ready, i + 1)
                        sp.dma_start(part_d[bass.ds(i * 2 * P, n * P), :].rearrange("(t p) c -> p t c", p=P), part[:, 0:n, :])\
                          .then_inc(part_out, 16)

                    load_pair(0, 0, 2, None)
                    load_pair(1, 1, 2, None)
                    with sp.Fori(0, PAIRS // 2 - 1) as i:
                        for s in range(2):
                            store_pair(2 * i + s, 2)
                            load_pair(2 * i + s + 2, s, 2, 2 * i + s + 1)
                    store_pair(PAIRS - 2, 2)
                    load_pair(PAIRS, 0, 1, PAIRS - 1)
                    store_pair(PAIRS - 1, 2)
                    store_pair(PAIRS, 1)
                    sp.wait_ge(part_out, 16 * (PAIRS + 1))

                @block.vector
                def _(v):
                    ch = Chain(v, dve)
                    v.wait_ge(hm, 1 + P // HD)
                    ch.link(v.memset(kmax[:], -3.0e38))

                    def project(n, xin, s, rows, prev):
                        v.wait_ge(x_in[s], xin)
                        if prev is not None:
                            v.wait_ge(zT_mm, prev)
                        v.tensor_scalar(z[:, s], xt[:, s], stat_mean[:, bass.ds(n, 1)], rstd2[:, bass.ds(n, 1)],
                                        ALU.subtract, ALU.mult).then_inc(z_ready, 1)
                        v.wait_ge(qkx_mm, n + 1)
                        lg = bank[4 + s]
                        lq = lg[:, 0:C].rearrange("p (h s) -> p h s", s=HD)
                        qh = q[:, s].rearrange("p (h s) -> p h s", s=HD)
                        ch.link(v.tensor_reduce(mx[:], lq, AX, ALU.max))
                        if prev is not None:
                            v.wait_ge(q_out[s], prev_out(n))
                        v.tensor_tensor(qh, lq, mx[:].unsqueeze(2).broadcast_to([P, HEADS, HD]), ALU.subtract)\
                         .then_inc(q_shift, 1)
                        ch.link(v.tensor_tensor(kmax[0:rows, :], kmax[0:rows, :], lg[0:rows, C:QK], ALU.max))
                        v.sem_inc(k_seen, 1)
                        v.wait_ge(q_exp, n + 1)
                        ch.link(v.tensor_reduce(mx[:], qh, AX, ALU.add))
                        ch.link(v.reciprocal(mx[:], mx[:]))
                        v.tensor_tensor(qh, qh, mx[:].unsqueeze(2).broadcast_to([P, HEADS, HD]), ALU.mult)\
                         .then_inc(q_ready, 1)

                    def prev_out(n):
                        return prev_out.value

                    for s in range(2):
                        project(s, 16, s, P, None)
                    with v.Fori(1, PAIRS) as i:
                        ch.enter(i - 1, 8)
                        for s in range(2):
                            prev_out.value = i * 16
                            project(2 * i + s, i * 16 + 16, s, P, 2 * i + s - 1)
                        ch.leave(PAIRS - 1)
                    prev_out.value = PAIRS * 16
                    project(NT - 1, PAIRS * 16 + 16, 0, LAST, NT - 2)

                    v.sem_inc(k_seen, 1)
                    v.wait_ge(kT_mm, 1)
                    for m in range(KC):
                        ch.link(v.tensor_reduce(kmax_c[:, m:m + 1], bank[6][:, m * P:m * P + P], AX, ALU.max))
                    for m in range(KC):
                        ch.link(v.tensor_scalar(diag[:, m], ident[:], kmax_c[:, m:m + 1], None, ALU.mult))
                    v.sem_inc(kdiag, 1)
                    v.wait_ge(kmax_mm, 1)
                    ch.link(v.tensor_copy(kmax_b[:], bank[7][:, 0:C]))

                    def shift_k(n, xin, s, prev):
                        v.wait_ge(kx_in[s], xin)
                        if prev is not None:
                            v.wait_ge(kv_mm, prev)
                        v.tensor_tensor(ke[:, s], k_s[:, s], kmax_b[:], ALU.subtract).then_inc(k_sub, 1)

                    for s in range(2):
                        shift_k(s, 32, s, None)
                    with v.Fori(1, PAIRS) as i:
                        for s in range(2):
                            shift_k(2 * i + s, i * 32 + 32, s, 2 * i + s - 1)
                    shift_k(NT - 1, PAIRS * 32 + 32, 0, NT - 2)

                    v.wait_ge(kv_mm, NT)
                    for m in range(KC):
                        ch.link(v.tensor_tensor(KVm[:, m], bank[m][:, 0:P], hmask[:], ALU.mult))
                        ch.link(v.reciprocal(rden[:, m:m + 1], bank[2 + m][:, 0:1]))
                    v.sem_inc(kv_ready, 1)
                    for m in range(KC):
                        v.wait_ge(M_mm, m + 1)
                        ch.link(v.tensor_scalar(M[:, m, :], bank[4 + m][:, 0:C], rden[:, m:m + 1], None, ALU.mult))
                    v.sem_inc(M_ready, 1)

                    def pair(n, pin, s, nt):
                        v.wait_ge(part_ready, n)
                        v.wait_ge(h_mm, n + 1)
                        v.wait_ge(pair_in[s], pin)
                        ph = bank[1][:, 0:nt * C].rearrange("p (t c) -> p t c", c=C)
                        ch.link(v.tensor_tensor(h[:, 0:nt], ph, xnp[:, s, 0:nt], ALU.add))
                        for t in range(2):
                            ch.link(v.bn_stats(pst[:, t, :], h[:, t % nt, :]))
                        mean_var(v, ch.link, pst, pm[:], pv[:], pa[:])
                        ch.link(v.tensor_scalar(pa[:], pv[:], LN_EPS, None, ALU.add))
                        rsqrt(v, ch.link, pr[:], pa[:], pb[:])
                        for t in range(2):
                            ch.link(v.tensor_scalar(z2[:, t % nt], h[:, t % nt], pm[:, t:t + 1], pr[:, t:t + 1],
                                                    ALU.subtract, ALU.mult))
                        v.sem_inc(z2_ready, 1)
                        ch.link(v.tensor_tensor(h[:, 0:nt], h[:, 0:nt], xp[:, s, 0:nt], ALU.add))
                        v.wait_ge(y_mm, n + 1)
                        v.wait_ge(part_out, n * 16)
                        py = bank[5][:, 0:nt * C].rearrange("p (t c) -> p t c", c=C)
                        v.tensor_tensor(part[:, 0:nt], py, h[:, 0:nt], ALU.add).then_inc(part_ready, 1)

                    per = 1 + 2 + MEAN_VAR_LINKS + 1 + RSQRT_LINKS + 2 + 1
                    with v.Fori(0, PAIRS // 2) as i:
                        ch.enter(i, 2 * per)
                        for s in range(2):
                            pair(2 * i + s, i * 48 + 48, s, 2)
                        ch.leave(PAIRS // 2)
                    pair(PAIRS, (PAIRS // 2) * 48 + 48, 0, 1)

                @block.scalar
                def _(a):
                    def project(n, xin, s, prev):
                        a.wait_ge(x_in[s], xin)
                        if prev is not None:
                            a.wait_ge(xn_out[s], prev * 16)
                        a.activation(xn[:, s], xt[:, s], ACT.Identity, bias=stat_a[:, bass.ds(n, 1)],
                                     scale=rstd[:, bass.ds(n, 1)]).then_inc(xn_ready, 1)
                        a.wait_ge(zT_mm, n + 1)
                        a.activation(zT[:, s], bank[s][:, 0:C], ACT.Copy).then_inc(zT_ready, 1)
                        a.wait_ge(q_shift, n + 1)
                        a.activation(q[:, s], q[:, s], ACT.Exp).then_inc(q_exp, 1)
                        a.wait_ge(k_seen, n + 1)
                        if prev is not None:
                            a.wait_ge(kx_out[s], prev * 32)
                        a.activation(k_s[:, s], bank[4 + s][:, C:QK], ACT.Copy).then_inc(kx_ready, 1)
                        a.activation(xm[:, s], bank[6 + s][:, 0:C], ACT.Copy).then_inc(kx_ready, 1)

                    for s in range(2):
                        project(s, 16, s, None)
                    with a.Fori(1, PAIRS) as i:
                        for s in range(2):
                            project(2 * i + s, i * 16 + 16, s, i)
                    project(NT - 1, PAIRS * 16 + 16, 0, PAIRS)

                    def exp_k(n, s):
                        a.wait_ge(k_sub, n + 1)
                        a.activation(ke[:, s], ke[:, s], ACT.Exp).then_inc(k_exp, 1)

                    with a.Fori(0, PAIRS) as i:
                        for s in range(2):
                            exp_k(2 * i + s, s)
                    exp_k(NT - 1, 0)

                    def pair(n, nt):
                        a.wait_ge(qT_mm, n + 1)
                        pq = bank[0][:, 0:KC * nt * P].rearrange("p (k c) -> p k c", k=KC)
                        a.activation(qT[:, :, 0:nt * P], pq, ACT.Copy).then_inc(qT_ready, 1)
                        a.wait_ge(z2T_mm, n + 1)
                        pz = bank[2][:, 0:KC * nt * P].rearrange("p (k c) -> p k c", k=KC)
                        a.activation(z2T[:, :, 0:nt * P], pz, ACT.Copy).then_inc(z2T_ready, 1)
                        for j in range(HB):
                            a.wait_ge(up_mm, n * HB + j + 1)
                            a.activation(hT[:, j, 0:nt * P], bank[3 + j % 2 * 3][:, 0:nt * P], ACT.Gelu, bias=b1f[:, j:j + 1])\
                             .then_inc(gelu, 1)

                    with a.Fori(0, PAIRS) as i:
                        pair(i, 2)
                    pair(PAIRS, 1)

                @block.tensor
                def _(pe):
                    def project(n, s, prev):
                        pe.wait_ge(z_ready, n + 1)
                        if prev is not None:
                            pe.wait_ge(zT_ready, prev)
                        for k in range(KC):
                            mm = pe.transpose(bank[s][:, k * P:k * P + P], z[:, s, k * P:k * P + P], ident[:])
                        mm.then_inc(zT_mm, 1)
                        pe.wait_ge(zT_ready, n + 1)
                        if prev is not None:
                            pe.wait_ge(kx_ready, prev * 2)
                            pe.wait_ge(q_shift, prev)
                        for o, lo, hi in ((4 + s, 0, QK), (6 + s, QK, 3 * C)):
                            for k in range(KC):
                                pe.matmul(bank[o][:, 0:hi - lo], zT[:, s, k * P:k * P + P], RA[:, k, lo:hi],
                                          start=(k == 0), stop=False)
                            mm = pe.matmul(bank[o][:, 0:hi - lo], ones[0:1, :], RB[0:1, lo:hi], start=False, stop=True)
                        mm.then_inc(qkx_mm, 1)

                    for s in range(2):
                        project(s, s, None)
                    with pe.Fori(1, PAIRS) as i:
                        for s in range(2):
                            project(2 * i + s, s, 2 * i + s - 1)
                    project(NT - 1, 0, NT - 2)

                    pe.wait_ge(k_seen, NT + 1)
                    pe.wait_ge(kx_ready, 2 * NT)
                    for m in range(KC):
                        mm = pe.transpose(bank[6][:, m * P:m * P + P], kmax[:, m * P:m * P + P], ident[:])
                    mm.then_inc(kT_mm, 1)
                    pe.wait_ge(kdiag, 1)
                    for m in range(KC):
                        mm = pe.matmul(bank[7][:, m * P:m * P + P], ones[:], diag[:, m], start=True, stop=True)
                    mm.then_inc(kmax_mm, 1)

                    def kv(n, s, rows, first, last):
                        pe.wait_ge(k_exp, n + 1)
                        for m in range(KC):
                            pe.matmul(bank[m][:, 0:P], xm[0:rows, s, m * P:m * P + P], ke[0:rows, s, m * P:m * P + P],
                                      start=first, stop=last)
                            mm = pe.matmul(bank[2 + m][:, 0:1], ke[0:rows, s, m * P:m * P + P], ones[0:rows, 0:1],
                                           start=first, stop=last)
                        mm.then_inc(kv_mm, 1)

                    kv(0, 0, P, True, False)
                    kv(1, 1, P, False, False)
                    with pe.Fori(1, PAIRS) as i:
                        for s in range(2):
                            kv(2 * i + s, s, P, False, False)
                    kv(NT - 1, 0, LAST, False, True)
                    pe.wait_ge(kv_ready, 1)
                    for m in range(KC):
                        pe.matmul(bank[4 + m][:, 0:C], KVm[:, m], G[:, m, :], start=True, stop=True).then_inc(M_mm, 1)
                    pe.wait_ge(M_ready, 1)

                    def pair(n, pin, s, nt):
                        N = nt * P
                        pe.wait_ge(pair_in[s], pin)
                        pe.wait_ge(qT_ready, n)
                        for k in range(KC):
                            for t in range(nt):
                                mm = pe.transpose(bank[0][:, k * N + t * P:k * N + t * P + P],
                                                  qx[:, s, t, k * P:k * P + P], ident[:])
                        mm.then_inc(qT_mm, 1)
                        pe.wait_ge(qT_ready, n + 1)
                        pe.wait_ge(z2_ready, n)
                        for t in range(nt):
                            for k in range(KC):
                                pe.matmul(bank[1][:, t * C:t * C + C], qT[:, k, t * P:t * P + P], M[:, k, :],
                                          start=(k == 0), stop=False)
                            mm = pe.matmul(bank[1][:, t * C:t * C + C], ones[0:1, :], bo[:], start=False, stop=True)
                        mm.then_inc(h_mm, 1)
                        pe.wait_ge(z2_ready, n + 1)
                        for k in range(KC):
                            for t in range(nt):
                                mm = pe.transpose(bank[2][:, k * N + t * P:k * N + t * P + P],
                                                  z2[:, t, k * P:k * P + P], ident[:])
                        mm.then_inc(z2T_mm, 1)
                        pe.wait_ge(z2T_ready, n + 1)
                        for j in range(HB):
                            if j >= 2:
                                pe.wait_ge(gelu, n * HB + j - 1)
                            for k in range(KC):
                                mm = pe.matmul(bank[3 + j % 2 * 3][:, 0:N], W1f[:, k, j * P:j * P + P], z2T[:, k, 0:N],
                                               start=(k == 0), stop=(k == KC - 1))
                            mm.then_inc(up_mm, 1)
                        pe.wait_ge(gelu, n * HB + HB)
                        pe.wait_ge(part_ready, n)
                        for t in range(nt):
                            for j in range(HB):
                                pe.matmul(bank[5][:, t * C:t * C + C], hT[:, j, t * P:t * P + P], W2[:, j, :],
                                          start=(j == 0), stop=False)
                            mm = pe.matmul(bank[5][:, t * C:t * C + C], ones[0:1, :], bsum[:], start=False, stop=True)
                        mm.then_inc(y_mm, 1)

                    with pe.Fori(0, PAIRS // 2) as i:
                        for s in range(2):
                            pair(2 * i + s, i * 48 + 48, s, 2)
                    pair(PAIRS, (PAIRS // 2) * 48 + 48, 0, 1)

        sb, _, _ = tools(outer, "r")
        acc = sb("acc", [P, NT, C])
        idx = sb("idx", [P, 2 * NT, 1], I32)
        top = sb("top", [P, NT, 8])
        wgt = sb("wgt", [P, 2, NT])
        key2 = sb("key2", [P, ACOLS])
        owner_row = sb("owner_row", [1, P], I32)

        c3 = ExitStack()
        with c3:
            sb, ps, sem = tools(c3, "b3")
            elist = sb("elist", [P, NCHP], I32)
            low = sb("low", [P, NCHP])
            crow = sb("crow", [1, CCOLS * P], I32)
            hot = sb("hot", [P, 2, 8, P])
            src_ring = sb("src_ring", [P, 2, 8], I32)
            rows16 = sb("rows16", [P, 16, C])
            bank = [ps(f"bank{n}", [P, 512]) for n in range(8)]
            list_in = sem("list_in")
            acc_in = sem("acc_in")
            zero = sem("zero")
            ready = sem("ready")
            gathered = [sem(f"gathered{n}") for n in range(16)]
            free = sem("free")
            added = sem("added")
            idle = sem("idle")
            dve = sem("dve")
            block = c3.enter_context(nc.Block())

            @block.sync
            def _(sp):
                sp.dma_start(elist[:, 0:NCH], elist_d.rearrange("(p n) a -> p (n a)", p=P)).then_inc(list_in, 16)
                sp.dma_start(crow[:], chunk_d.rearrange("n a -> a n")).then_inc(list_in, 16)
                sp.dma_start(acc[:], xn_d.rearrange("(t p) c -> p t c", p=P)).then_inc(acc_in, 16)

            @block.vector
            def _(v):
                ch = Chain(v, dve)
                ch.link(v.memset(elist[:, NCH:], P))
                v.wait_ge(list_in, 32)
                low_i = rows16[:].rearrange("p a b -> p (a b)")[:, 0:NCHP].bitcast(I32)
                ch.link(v.tensor_scalar(low_i, elist[:], 255, None, ALU.bitwise_and))
                ch.link(v.tensor_copy(low[:], low_i))
                ch.link(v.tensor_scalar(elist[:], elist[:], 8, None, ALU.logical_shift_right))

                def prepare(at, s):
                    v.tensor_tensor(hot[:, s], low[:, bass.ds(at, 8)].unsqueeze(2).broadcast_to([P, 8, P]),
                                    node_ids.unsqueeze(1).broadcast_to([P, 8, P]), ALU.is_equal).then_inc(ready, 1)
                    v.tensor_copy(src_ring[:, s], elist[:, bass.ds(at, 8)]).then_inc(ready, 1)

                def add(i, s):
                    _, owner = nc.values_load_multi_w_load_instructions(
                        crow[0:1, bass.ds(i * 16 + s * 8, 8)], engines=[mybir.EngineType.DVE], min_val=0, max_val=NT - 1,
                        skip_runtime_bounds_check_because="the owners were clamped to the last tile")
                    for c in range(8):
                        v.wait_ge(free, i * 16 + s * 8 + c + 17)
                        v.wait_ge(added, i * 16 + s * 8 + c + 8)
                        tile = acc[:, bass.ds(owner[c], 1), :].rearrange("p a c -> p (a c)")
                        v.tensor_tensor(tile, tile, bank[c][:, 0:C], ALU.add).then_inc(added, 1)

                v.sem_inc(added, 8)
                prepare(0, 0)
                v.wait_ge(acc_in, 16)
                with v.Fori(0, NCH // 16) as i:
                    v.wait_ge(free, i * 16 + 16)
                    prepare(i * 16 + 8, 1)
                    add(i, 0)
                    v.wait_ge(free, i * 16 + 24)
                    prepare(i * 16 + 16, 0)
                    add(i, 1)

            @block.gpsimd
            def _(pool):
                with pool.Fori(0, NCH // 16) as i:
                    for s in range(2):
                        pool.wait_ge(ready, i * 4 + 2 * s + 2)
                        pool.sem_inc(idle, 1)
                        for c in range(8):
                            n = 8 * s + c
                            pool.wait_ge(free, i * 16 + n + 1)
                            pool.sem_inc(idle, 1)
                            pool.indirect_dma_start(
                                out=rows16[:, n, :], out_offset=None, in_=xn_d,
                                in_offset=bass.IndirectOffsetOnAxis(ap=src_ring[:, s, c:c + 1], axis=0))\
                                .then_inc(gathered[n], 16)

            @block.tensor
            def _(pe):
                pe.sem_inc(free, 16)
                with pe.Fori(0, NCH // 16) as i:
                    for s in range(2):
                        pe.wait_ge(ready, i * 4 + 2 * s + 2)
                        for c in range(8):
                            n = 8 * s + c
                            pe.wait_ge(gathered[n], i * 16 + 16)
                            pe.wait_ge(added, i * 16 + n + 1)
                            pe.matmul(bank[c][:, 0:C], hot[:, s, c], rows16[:, n, :], start=True, stop=True).then_inc(free, 1)

        c4 = ExitStack()
        with c4:
            sb, ps, sem = tools(c4, "b4")
            a_s = sb("a_s", [P, 2, C])
            aT = sb("aT", [P, 2, C])
            pt = sb("pt", [P, 2, C])
            u = sb("u", [P, 2, C])
            uT = sb("uT", [P, 2, C])
            lg = sb("lg", [P, 2, 8])
            mi = sb("mi", [P, 2, 8], U32)
            mv8 = sb("mv8", [P, 2, 8])
            topi = sb("topi", [P, NT, 8])
            mask = sb("mask", [P, ACOLS])
            scan = sb("scan", [P, ACOLS])
            pos = sb("pos", [P, ACOLS])
            counts, size, cum, off = (sb(f"e{n}", [P, EXPERTS]) for n in range(4))
            t_int = sb("t_int", [P, EXPERTS], I32)
            ge = sb("ge", [P, 1, EXPERTS])
            own_f = sb("own_f", [P, 1])
            own_i = sb("own_i", [P, 1], I32)
            zrow = sb("zrow", [P, 8, C])
            z3 = sb("z3", [P, 4, C])
            ring = sb("ring", [P, 4, 2], I32)
            bank = [ps(f"bank{n}", [P, 512]) for n in range(8)]
            a_ready = sem("a_ready")
            aT_mm = sem("aT_mm")
            aT_ready = sem("aT_ready")
            gnn_mm = sem("gnn_mm")
            part_in = [sem(f"part_in{n}") for n in range(2)]
            x1_ready = sem("x1_ready")
            u_ready = sem("u_ready")
            uT_mm = sem("uT_mm")
            uT_ready = sem("uT_ready")
            lg_mm = sem("lg_mm")
            lg_ready = sem("lg_ready")
            zeroed = sem("zeroed")
            xs_zero = sem("xs_zero")
            counted = sem("counted")
            summed = sem("summed")
            owners = sem("owners")
            own_out = sem("own_out")
            own_in = sem("own_in")
            z3_ready = sem("z3_ready")
            sent = [sem(f"sent{n}") for n in range(4)]
            placed = sem("placed")
            own_in2 = sem("slots_ready")
            stat_ok = sem("stat_ok")
            dve = sem("dve")
            idle = sem("idle")
            block = c4.enter_context(nc.Block())

            @block.sync
            def _(sp):
                def load_part(t, s, free_at):
                    if free_at is not None:
                        sp.wait_ge(x1_ready, free_at)
                    sp.dma_start(pt[:, s], part_d[bass.ds(t * P, P), :]).then_inc(part_in[s], 16)

                load_part(0, 0, None)
                load_part(1, 1, None)
                with sp.Fori(1, PAIRS) as i:
                    for s in range(2):
                        load_part(2 * i + s, s, 2 * i + s - 1)
                load_part(NT - 1, 0, NT - 2)
                sp.wait_ge(zeroed, 1)
                for g in range(ETILES // 4):
                    sp.dma_start(xs_d[g * 8 * P:(g + 1) * 8 * P, :].rearrange("(t p) c -> p t c", p=P), zrow[:])\
                      .then_inc(xs_zero, 16)
                sp.wait_ge(owners, 1)
                sp.dma_start(etile_d, own_i[:]).then_inc(own_out, 16)
                sp.wait_ge(own_out, 16)
                sp.dma_start(owner_row[:], etile_d.rearrange("n a -> a n")).then_inc(own_in, 16)
                sp.wait_ge(own_in, 16)
                sp.wait_ge(xs_zero, 16 * (ETILES // 4))

            @block.tensor
            def _(pe):
                def gnn(n, s, prev):
                    pe.wait_ge(a_ready, n + 1)
                    for k in range(KC):
                        mm = pe.transpose(bank[s][:, k * P:k * P + P], a_s[:, s, k * P:k * P + P], ident[:])
                    mm.then_inc(aT_mm, 1)
                    pe.wait_ge(aT_ready, n + 1)
                    if prev is not None:
                        pe.wait_ge(x1_ready, prev)
                    for k in range(KC):
                        mm = pe.matmul(bank[2 + s][:, 0:C], aT[:, s, k * P:k * P + P], W12[:, k, :],
                                       start=(k == 0), stop=(k == KC - 1))
                    mm.then_inc(gnn_mm, 1)

                for s in range(2):
                    gnn(s, s, None)
                with pe.Fori(1, PAIRS) as i:
                    for s in range(2):
                        gnn(2 * i + s, s, 2 * i + s - 1)
                gnn(NT - 1, 0, NT - 2)

                def route(n, s):
                    pe.wait_ge(u_ready, n + 1)
                    for k in range(KC):
                        mm = pe.transpose(bank[s][:, k * P:k * P + P], u[:, s, k * P:k * P + P], ident[:])
                    mm.then_inc(uT_mm, 1)
                    pe.wait_ge(uT_ready, n + 1)
                    for k in range(KC):
                        pe.matmul(bank[4 + s][:, 0:EXPERTS], uT[:, s, k * P:k * P + P], WR[:, k, :], start=(k == 0), stop=False)
                    pe.matmul(bank[4 + s][:, 0:EXPERTS], ones[0:1, :], br[:], start=False, stop=True).then_inc(lg_mm, 1)

                with pe.Fori(0, PAIRS) as i:
                    for s in range(2):
                        route(2 * i + s, s)
                route(NT - 1, 0)
                pe.wait_ge(counted, 1)
                pe.matmul(bank[6][:, 0:EXPERTS], tri[:], counts[:], start=True, stop=True)
                pe.matmul(bank[6][:, EXPERTS:2 * EXPERTS], ones[:], counts[:], start=True, stop=True).then_inc(summed, 1)

            @block.scalar
            def _(a):
                def gnn(n, s, prev):
                    if prev is not None:
                        a.wait_ge(aT_mm, prev)
                    a.activation(a_s[:, s], acc[:, bass.ds(n, 1), :].rearrange("p a c -> p (a c)"), ACT.Copy).then_inc(a_ready, 1)
                    a.wait_ge(aT_mm, n + 1)
                    if prev is not None:
                        a.wait_ge(gnn_mm, prev)
                    a.activation(aT[:, s], bank[s][:, 0:C], ACT.Copy).then_inc(aT_ready, 1)

                for s in range(2):
                    gnn(s, s, None)
                with a.Fori(1, PAIRS) as i:
                    for s in range(2):
                        gnn(2 * i + s, s, 2 * i + s - 1)
                gnn(NT - 1, 0, NT - 2)

                def route(n, s):
                    a.wait_ge(uT_mm, n + 1)
                    a.activation(uT[:, s], bank[s][:, 0:C], ACT.Copy).then_inc(uT_ready, 1)

                with a.Fori(0, PAIRS) as i:
                    for s in range(2):
                        route(2 * i + s, s)
                route(NT - 1, 0)
                a.wait_ge(lg_ready, NT + 1)
                a.activation(top[:, :, 1], top[:, :, 1], ACT.Exp).then_inc(placed, 1)

                def rows(n, c):
                    a.wait_ge(sent[c], rows.sent * 32)
                    a.activation(z3[:, c], acc[:, bass.ds(n, 1), :].rearrange("p a c -> p (a c)"), ACT.Identity,
                                 bias=var[:, bass.ds(n, 1)], scale=rstd2[:, bass.ds(n, 1)]).then_inc(z3_ready, 1)

                with a.Fori(0, NT // 4) as i:
                    for c in range(4):
                        rows.sent = i
                        rows(4 * i + c, c)
                rows.sent = NT // 4
                rows(NT - 1, 0)

            @block.vector
            def _(v):
                ch = Chain(v, dve)
                v.memset(zrow[:], 0.0).then_inc(zeroed, 1)

                def gnn(n, s, pin):
                    v.wait_ge(gnn_mm, n + 1)
                    v.wait_ge(part_in[s], pin)
                    tile = acc[:, bass.ds(n, 1), :].rearrange("p a c -> p (a c)")
                    v.tensor_tensor(tile, bank[2 + s][:, 0:C], pt[:, s], ALU.add).then_inc(x1_ready, 1)
                    v.wait_ge(x1_ready, n + 1)
                    v.sem_inc(idle, 1)
                    v.bn_stats(stats[:, bass.ds(n, 1), :].rearrange("p a c -> p (a c)"), tile).then_inc(stat_ok, 1)

                with v.Fori(0, PAIRS) as i:
                    for s in range(2):
                        gnn(2 * i + s, s, i * 16 + 16)
                gnn(NT - 1, 0, PAIRS * 16 + 16)
                v.wait_ge(stat_ok, NT)
                mean_var(v, ch.link, stats, stat_mean[:], var[:], stat_a[:])
                double_norm(v, ch.link, var[:], rstd[:], rstd2[:], stat_a[:], stat_b[:])
                ch.link(v.scalar_tensor_tensor(var[:], stat_mean[:], -1.0, rstd2[:], ALU.mult, ALU.mult))

                def route(n, s, prev):
                    if prev is not None:
                        v.wait_ge(uT_mm, prev)
                    v.tensor_scalar(u[:, s], acc[:, bass.ds(n, 1), :].rearrange("p a c -> p (a c)"),
                                    stat_mean[:, bass.ds(n, 1)], rstd[:, bass.ds(n, 1)],
                                    ALU.subtract, ALU.mult).then_inc(u_ready, 1)
                    v.wait_ge(lg_mm, n + 1)
                    ch.link(v.tensor_copy(lg[:, s], bank[4 + s][:, 0:EXPERTS]))
                    v.sem_inc(idle, 1)
                    ch.link(v.max(mv8[:, s], lg[:, s]))
                    v.sem_inc(idle, 1)
                    ch.link(v.max_index(mi[:, s], mv8[:, s], lg[:, s]))
                    ch.link(v.tensor_copy(top[:, bass.ds(n, 1), :].rearrange("p a c -> p (a c)"), mv8[:, s]))
                    ch.link(v.tensor_copy(topi[:, bass.ds(n, 1), :].rearrange("p a c -> p (a c)"), mi[:, s]))
                    v.sem_inc(lg_ready, 1)

                for s in range(2):
                    route(s, s, None)
                with v.Fori(1, PAIRS) as i:
                    ch.enter(i - 1, 10)
                    for s in range(2):
                        route(2 * i + s, s, 2 * i + s - 1)
                    ch.leave(PAIRS - 1)
                route(NT - 1, 0, NT - 2)
                ch.link(v.tensor_tensor(top[:, :, 1], top[:, :, 1], top[:, :, 0], ALU.subtract))
                v.sem_inc(lg_ready, 1)
                ch.link(v.tensor_copy(key2[:, 0:NT], topi[:, :, 0]))
                ch.link(v.tensor_copy(key2[:, NT:], topi[:, :, 1]))
                ch.link(v.memset(pos[:], 0.0))
                count_keys(v, ch, key2[:], mask[:], ids, counts[:], EXPERTS)
                v.sem_inc(counted, 1)
                v.wait_ge(summed, 1)
                bucket_starts(v, ch, bank[6], EXPERTS, TILE_TOKENS, cum[:], size[:], off[:], t_int[:], ones[:, 0:EXPERTS])
                tile_owner(v, ch, cum[:], EXPERTS, part_ids[:], ge[:], own_f[:], own_i[:], 1)
                v.sem_inc(owners, 1)
                place_keys(v, ch, key2[:], mask[:], scan[:], pos[:], ids, off[:], EXPERTS, idle)
                ch.link(v.tensor_scalar(pos[:], pos[:], -1.0, None, ALU.add))
                ch.link(v.tensor_copy(idx[:].rearrange("p n a -> p (n a)"), pos[:]))
                v.sem_inc(placed, 1)
                v.wait_ge(placed, 2)
                ch.link(v.tensor_scalar(top[:, :, 0], top[:, :, 1], 1.0, None, ALU.add))
                ch.link(v.reciprocal(wgt[:, 0, :], top[:, :, 0]))
                ch.link(v.tensor_tensor(wgt[:, 1, :], wgt[:, 0, :], top[:, :, 1], ALU.mult))

            @block.gpsimd
            def _(pool):
                pool.wait_ge(placed, 2)
                pool.wait_ge(xs_zero, 16 * (ETILES // 4))

                def send(n, c, k, done):
                    pool.wait_ge(sent[c], done * 32)
                    pool.sem_inc(idle, 1)
                    pool.tensor_copy(ring[:, c, 0:1], idx[:, bass.ds(n, 1), :].rearrange("p n a -> p (n a)")).then_inc(own_in2, 1)
                    pool.tensor_copy(ring[:, c, 1:2], idx[:, bass.ds(n + NT, 1), :].rearrange("p n a -> p (n a)")).then_inc(own_in2, 1)
                    pool.wait_ge(own_in2, n * 2 + 2)
                    pool.sem_inc(idle, 1)
                    pool.wait_ge(z3_ready, n + 1)
                    pool.sem_inc(idle, 1)
                    for j in range(2):
                        pool.indirect_dma_start(
                            out=xs_d, out_offset=bass.IndirectOffsetOnAxis(ap=ring[:, c, j:j + 1], axis=0),
                            in_=z3[:, c, :], in_offset=None).then_inc(sent[c], 16)

                with pool.Fori(0, NT // 4) as i:
                    for c in range(4):
                        send(4 * i + c, c, c, i)
                send(NT - 1, 0, 0, NT // 4)
                for c in range(4):
                    pool.wait_ge(sent[c], 32 * (NT // 4 + (c == 0)))

        c5 = ExitStack()
        with c5:
            sb, ps, sem = tools(c5, "b5")
            E1 = sb("E1", [P, 2, KC, HID])
            E2 = sb("E2", [P, 2, HB, C])
            vec = sb("vec", [P, 2, 2 * KC + HB])
            b2e = sb("b2e", [1, 2, C])
            xs = sb("xs", [P, 2, 2, C])
            xeT = sb("xeT", [P, 2, KC, TILE_TOKENS])
            hT = sb("hT", [P, 2, HB, TILE_TOKENS])
            ys = sb("ys", [P, 2, 2, C])
            bank = [ps(f"bank{n}", [P, 512]) for n in range(8)]
            w_in = [sem(f"w_in{n}") for n in range(2)]
            xsT_mm = sem("xsT_mm")
            xeT_ready = sem("xeT_ready")
            up_mm = sem("up_mm")
            gelu = sem("gelu")
            y_mm = sem("y_mm")
            y_ready = sem("y_ready")
            idle5 = sem("half_taken")
            y_out = [sem(f"y_out{n}") for n in range(2)]
            block = c5.enter_context(nc.Block())
            LOADS = 5
            w1_d = w["ffn_W1"].rearrange("(e k p) h -> e p k h", p=P, k=KC)
            w2_d = w["ffn_W2"].rearrange("(e j p) c -> e p j c", p=P, j=HB)
            HALF = ETILES // 2

            @block.sync
            def _(sp):
                def load(t, s, free_at):
                    if free_at is not None:
                        sp.wait_ge(y_mm, free_at)
                    e = nc.values_load(owner_row[0:1, bass.ds(t, 1)], engines=[mybir.EngineType.SP],
                                       min_val=0, max_val=EXPERTS - 1,
                                       skip_runtime_bounds_check_because="the owners were clamped to the last expert")
                    one = lambda a: a[bass.ds(e, 1)]
                    sp.dma_start(E1[:, s], one(w1_d).rearrange("a p k h -> p (a k) h")).then_inc(w_in[s], 16)
                    sp.dma_start(E2[:, s], one(w2_d).rearrange("a p k h -> p (a k) h")).then_inc(w_in[s], 16)
                    sp.dma_start(vec[:, s], one(w["ffn_vec"]).rearrange("a p k -> p (a k)")).then_inc(w_in[s], 16)
                    sp.dma_start(b2e[:, s], one(w["ffn_b2"])).then_inc(w_in[s], 16)
                    sp.dma_start(xs[:, s], xs_d[bass.ds(t * TILE_TOKENS, TILE_TOKENS), :].rearrange("(t p) c -> p t c", p=P))\
                      .then_inc(w_in[s], 16)

                def store(t, s):
                    sp.wait_ge(y_ready, t + 1)
                    sp.dma_start(ys_d[bass.ds(t * TILE_TOKENS, TILE_TOKENS), :].rearrange("(t p) c -> p t c", p=P), ys[:, s])\
                      .then_inc(y_out[s], 16)

                load(0, 0, None)
                load(1, 1, None)
                with sp.Fori(0, HALF - 1) as i:
                    for s in range(2):
                        load(2 * i + s + 2, s, 2 * i + s + 1)
                        store(2 * i + s, s)
                for s in range(2):
                    store(ETILES - 2 + s, s)
                for s in range(2):
                    sp.wait_ge(y_out[s], 16 * HALF)

            @block.tensor
            def _(pe):
                def turn(t, s, win):
                    pe.wait_ge(w_in[s], win)
                    pe.wait_ge(xeT_ready, 2 * t)
                    for k in range(KC):
                        for j in range(2):
                            mm = pe.transpose(bank[0][:, k * C + j * P:k * C + j * P + P], xs[:, s, j, k * P:k * P + P], ident[:])
                    mm.then_inc(xsT_mm, 1)

                def up(t, s):
                    pe.wait_ge(xeT_ready, 2 * t + 2)
                    for j in range(HB):
                        if j >= 4:
                            pe.wait_ge(gelu, t * HB + j - 3)
                        else:
                            pe.wait_ge(gelu, t * HB)
                        for k in range(KC):
                            mm = pe.matmul(bank[1 + j % 4][:, 0:TILE_TOKENS], E1[:, s, k, j * P:j * P + P], xeT[:, s, k, :],
                                           start=(k == 0), stop=(k == KC - 1))
                        mm.then_inc(up_mm, 1)

                def down(t, s):
                    pe.wait_ge(gelu, t * HB + HB)
                    pe.wait_ge(y_ready, t)
                    for i in range(2):
                        for j in range(HB):
                            pe.matmul(bank[5 + i][:, 0:C], hT[:, s, j, i * P:i * P + P], E2[:, s, j, :], start=(j == 0), stop=False)
                        mm = pe.matmul(bank[5 + i][:, 0:C], ones[0:1, :], b2e[0:1, s, :], start=False, stop=True)
                    mm.then_inc(y_mm, 1)

                W = 16 * LOADS
                turn(0, 0, W)
                with pe.Fori(0, HALF - 1) as i:
                    up(2 * i, 0)
                    turn(2 * i + 1, 1, i * W + W)
                    down(2 * i, 0)
                    up(2 * i + 1, 1)
                    turn(2 * i + 2, 0, i * W + 2 * W)
                    down(2 * i + 1, 1)
                up(ETILES - 2, 0)
                turn(ETILES - 1, 1, HALF * W)
                down(ETILES - 2, 0)
                up(ETILES - 1, 1)
                down(ETILES - 1, 1)

            @block.scalar
            def _(a):
                def scale(t, s):
                    a.wait_ge(xsT_mm, t + 1)
                    for k in range(KC):
                        a.activation(xeT[:, s, k, :], bank[0][:, k * C:k * C + TILE_TOKENS], ACT.Identity,
                                     bias=vec[:, s, KC + k:KC + k + 1], scale=vec[:, s, k:k + 1]).then_inc(xeT_ready, 1)

                def act_up(t, s):
                    for j in range(HB):
                        a.wait_ge(up_mm, t * HB + j + 1)
                        a.activation(hT[:, s, j, :], bank[1 + j % 4][:, 0:TILE_TOKENS], ACT.Gelu,
                                     bias=vec[:, s, 2 * KC + j:2 * KC + j + 1]).then_inc(gelu, 1)

                scale(0, 0)
                with a.Fori(0, HALF - 1) as i:
                    act_up(2 * i, 0)
                    scale(2 * i + 1, 1)
                    act_up(2 * i + 1, 1)
                    scale(2 * i + 2, 0)
                act_up(ETILES - 2, 0)
                scale(ETILES - 1, 1)
                act_up(ETILES - 1, 1)

            @block.vector
            def _(v):
                def take(t, s, out_at):
                    v.wait_ge(y_mm, t + 1)
                    v.wait_ge(y_out[s], out_at)
                    v.tensor_copy(ys[:, s, 0, :], bank[5][:, 0:C]).then_inc(idle5, 1)
                    v.tensor_copy(ys[:, s, 1, :], bank[6][:, 0:C]).then_inc(idle5, 1)
                    v.wait_ge(idle5, t * 2 + 2)
                    v.sem_inc(y_ready, 1)

                with v.Fori(0, HALF) as i:
                    for s in range(2):
                        take(2 * i + s, s, i * 16)

        c6 = ExitStack()
        with c6:
            sb, ps, sem = tools(c6, "b6")
            y1 = sb("y1", [P, 4, 2, C])
            o = sb("o", [P, 4, C])
            ring = sb("ring", [P, 4, 2], I32)
            got = [sem(f"got{n}") for n in range(4)]
            ring_ok = sem("ring_ok")
            idle = sem("idle")
            used = sem("used")
            dve = sem("dve")
            out_done = [sem(f"out_done{n}") for n in range(4)]
            block = c6.enter_context(nc.Block())

            @block.gpsimd
            def _(pool):
                def fetch(n, c):
                    pool.wait_ge(used, n + 1)
                    pool.sem_inc(idle, 1)
                    pool.tensor_copy(ring[:, c, 0:1], idx[:, bass.ds(n, 1), :].rearrange("p n a -> p (n a)")).then_inc(ring_ok, 1)
                    pool.tensor_copy(ring[:, c, 1:2], idx[:, bass.ds(n + NT, 1), :].rearrange("p n a -> p (n a)")).then_inc(ring_ok, 1)
                    pool.wait_ge(ring_ok, n * 2 + 2)
                    pool.sem_inc(idle, 1)
                    for j in range(2):
                        pool.indirect_dma_start(
                            out=y1[:, c, j, :], out_offset=None, in_=ys_d,
                            in_offset=bass.IndirectOffsetOnAxis(ap=ring[:, c, j:j + 1], axis=0)).then_inc(got[c], 16)

                with pool.Fori(0, NT // 4) as i:
                    for c in range(4):
                        fetch(4 * i + c, c)
                fetch(NT - 1, 0)

            @block.vector
            def _(v):
                v.sem_inc(used, 4)
                ch = Chain(v, dve)

                def combine(n, c, lap):
                    v.wait_ge(got[c], lap * 32 + 32)
                    v.wait_ge(out_done[c], lap * 16)
                    tile = acc[:, bass.ds(n, 1), :].rearrange("p a c -> p (a c)")
                    ch.link(v.scalar_tensor_tensor(o[:, c], y1[:, c, 0], wgt[:, 0, bass.ds(n, 1)], tile, ALU.mult, ALU.add))
                    v.scalar_tensor_tensor(o[:, c], y1[:, c, 1], wgt[:, 1, bass.ds(n, 1)], o[:, c], ALU.mult, ALU.add)\
                     .then_inc(used, 1)

                with v.Fori(0, NT // 4) as i:
                    ch.enter(i, 4)
                    for c in range(4):
                        combine(4 * i + c, c, i)
                    ch.leave(NT // 4)
                combine(NT - 1, 0, NT // 4)

            @block.sync
            def _(sp):
                def store(n, c):
                    sp.wait_ge(used, n + 5)
                    sp.dma_start(out[bass.ds(n * P, P), :], o[:, c]).then_inc(out_done[c], 16)

                with sp.Fori(0, NT // 4) as i:
                    for c in range(4):
                        store(4 * i + c, c)
                store(NT - 1, 0)
                for c in range(4):
                    sp.wait_ge(out_done[c], 16 * (NT // 4 + (c == 0)))


def kernel(x, src, dst, **weights):
    import numpy as np
    from concourse import bacc
    from concourse.bass_utils import run_bass_kernel_spmd

    x, src, dst = np.asarray(x), np.asarray(src), np.asarray(dst)
    g = {k: np.asarray(a) for k, a in weights.items()}
    nodes = x.shape[0]
    tiles = -(-nodes // P)
    xp = np.zeros((tiles * P, C), x.dtype)
    xp[:nodes] = x
    ecols = -(-src.shape[0] // P)
    ecols += -ecols % 32
    sp = np.full(ecols * P, tiles * P - 1, src.dtype)
    sp[:src.shape[0]] = src
    dp = np.zeros(ecols * P, dst.dtype)
    dp[:dst.shape[0]] = dst
    T = lambda a: np.ascontiguousarray(a.T)
    col = lambda a: a.reshape(-1, P).T
    row = lambda a: a.reshape(1, -1)
    m = lambda n: g["L0_mix_" + n]
    f = lambda n: g["L0_ffn_" + n]
    arrays = {
        "x": xp, "src": sp.reshape(P, ecols), "dst": dp.reshape(P, ecols),
        "mix_WxT": T(m("Wx")), "mix_Wx": m("Wx"), "mix_WoT": T(m("Wo")), "mix_WqT": T(m("Wq")), "mix_WkT": T(m("Wk")),
        "mix_Wv": m("Wv"), "mix_W1T": T(m("W1")), "mix_W2T": T(m("W2")),
        "gnn_W1T": T(g["L0_gnn_W1"]), "gnn_W2": g["L0_gnn_W2"],
        "cols": np.concatenate([col(a) for a in (m("ln1_w"), m("ln1_b"), m("bx"), m("ln2_w"), m("ln2_b"), m("b1"),
                                                 g["L0_gnn_b1"])], axis=1),
        "mix_bx": row(m("bx")), "gnn_b2": row(g["L0_gnn_b2"]), "mix_b2": row(m("b2")), "mix_bo": row(m("bo")),
        "ffn_Wr": f("Wr"), "ffn_br": row(f("br")),
        "ffn_W1": f("W1").reshape(-1, f("W1").shape[2]), "ffn_W2": f("W2").reshape(-1, C),
        "ffn_vec": np.concatenate([f(n).reshape(EXPERTS, -1, P).transpose(0, 2, 1) for n in ("ln_g", "ln_b", "b1")], axis=2),
        "ffn_b2": f("b2"),
    }
    nc = bacc.Bacc("TRN2", target_bir_lowering=False, num_devices=1)
    aps, maps = {}, {}
    for name, a in arrays.items():
        a = np.ascontiguousarray(a)
        maps[f"in_{name}"] = a
        aps[name] = nc.dram_tensor(f"in_{name}", a.shape, mybir.dt.from_np(a.dtype), kind="ExternalInput").ap()
    out = nc.dram_tensor("out", xp.shape, F32, kind="ExternalOutput").ap()
    gps_layer(nc, aps, out, nodes, ecols)
    r = run_bass_kernel_spmd(nc, [maps], core_ids=[0])
    return r.results[0]["out"][:nodes]
```

```python
from contextlib import ExitStack

import concourse.bass as bass
from concourse import mybir

P = 128
C = 256
KC = C // P
F32 = mybir.dt.float32
I32 = mybir.dt.int32
U32 = mybir.dt.uint32
ALU = mybir.AluOpType
ACT = mybir.ActivationFunctionType
AX = mybir.AxisListType.X
LN_EPS = 1e-5
HEADS, HD = 8, 32
EXPERTS = 8
TILE_TOKENS = 256
RSQRT_SEED = 1597463007.0


class Chain:

    def __init__(self, eng, sem):
        self.eng, self.sem, self.base, self.k, self.i, self.per = eng, sem, 0, 0, None, 0

    def link(self, ins):
        ins.then_inc(self.sem, 1)
        self.k += 1
        at = self.base + self.k
        self.eng.wait_ge(self.sem, at if self.i is None else self.i * self.per + at)

    def enter(self, i, per):
        self.base += self.k
        self.k, self.i, self.per = 0, i, per

    def leave(self, times):
        assert self.k == self.per, (self.k, self.per)
        self.base += times * self.per
        self.k, self.i = 0, None


def at_least(eng, sem, value):
    if not isinstance(value, int) or value > 0:
        eng.wait_ge(sem, value)


def rsqrt(v, link, y, x, t):
    link(v.tensor_scalar(t.bitcast(I32), x.bitcast(I32), 1, None, ALU.logical_shift_right))
    link(v.tensor_scalar(y.bitcast(I32), t.bitcast(I32), -1.0, RSQRT_SEED, ALU.mult, ALU.add))
    for _ in range(3):
        link(v.tensor_tensor(t, y, y, ALU.mult))
        link(v.scalar_tensor_tensor(t, t, -0.5, x, ALU.mult, ALU.mult))
        link(v.scalar_tensor_tensor(y, t, 1.5, y, ALU.add, ALU.mult))


RSQRT_LINKS = 11


def mean_var(v, link, st, mean, var, t):
    link(v.tensor_tensor(mean, st[:, :, 1], st[:, :, 4], ALU.add))
    link(v.tensor_scalar(mean, mean, 0.5, None, ALU.mult))
    link(v.tensor_tensor(t, st[:, :, 1], st[:, :, 4], ALU.subtract))
    link(v.tensor_tensor(t, t, t, ALU.mult))
    link(v.tensor_tensor(var, st[:, :, 2], st[:, :, 5], ALU.add))
    link(v.tensor_scalar(var, var, 1.0 / C, None, ALU.mult))
    link(v.scalar_tensor_tensor(var, t, 0.25, var, ALU.mult, ALU.add))


MEAN_VAR_LINKS = 7


def double_norm(v, link, var, rstd, rstd2, a, t):
    link(v.tensor_scalar(a, var, LN_EPS, None, ALU.add))
    rsqrt(v, link, rstd, a, t)
    link(v.tensor_tensor(a, rstd, rstd, ALU.mult))
    link(v.tensor_tensor(a, a, var, ALU.mult))
    link(v.tensor_scalar(a, a, LN_EPS, None, ALU.add))
    rsqrt(v, link, rstd2, a, t)
    link(v.tensor_tensor(rstd2, rstd2, rstd, ALU.mult))


def count_keys(v, ch, key, mask, ids, counts, n):
    with v.Fori(0, n) as b:
        ch.enter(b, 1)
        ch.link(v.tensor_scalar(mask, key, ids[:, bass.ds(b, 1)], 0.0, ALU.is_equal, ALU.add,
                                accum_out=counts[:, bass.ds(b, 1)]))
        ch.leave(n)


def bucket_starts(v, ch, base_total, n, align, cum, size, off, t_int, ones_row):
    shift = align.bit_length() - 1
    link = ch.link
    link(v.tensor_scalar(size, base_total[:, n:2 * n], float(align - 1), None, ALU.add))
    link(v.tensor_copy(t_int, size))
    link(v.tensor_scalar(t_int, t_int, shift, None, ALU.logical_shift_right))
    link(v.tensor_copy(size, t_int))
    link(v.tensor_tensor_scan(cum, ones_row, size, 0.0, ALU.mult, ALU.add))
    link(v.tensor_tensor(off, cum, size, ALU.subtract))
    link(v.scalar_tensor_tensor(off, off, float(align), base_total[:, 0:n], ALU.mult, ALU.add))


def place_keys(v, ch, key, mask, scan, pos, ids, off, n, hold, more=False):
    with v.Fori(0, n) as b:
        ch.enter(b, 4 if more else 3)
        ch.link(v.tensor_scalar(mask, key, ids[:, bass.ds(b, 1)], None, ALU.is_equal))
        ch.link(v.tensor_tensor_scan(scan, mask, mask, off[:, bass.ds(b, 1)], ALU.add, ALU.max))
        v.sem_inc(hold, 1)
        ch.link(v.copy_predicated(pos, mask.bitcast(I32), scan))
        if more:
            v.sem_inc(hold, 1)
            ch.link(v.tensor_copy(off[:, bass.ds(b, 1)], scan[:, scan.shape[1] - 1:scan.shape[1]]))
        ch.leave(n)


def tile_owner(v, ch, cum, n, unit_ids, ge, owner, owner_int, cols):
    link = ch.link
    link(v.tensor_tensor(ge, unit_ids.unsqueeze(2).broadcast_to([P, cols, n]),
                         cum.unsqueeze(1).broadcast_to([P, cols, n]), ALU.is_ge))
    link(v.tensor_reduce(owner, ge, AX, ALU.add))
    link(v.tensor_scalar(owner, owner, float(n - 1), None, ALU.min))
    link(v.tensor_copy(owner_int, owner))


def gps_layer(nc, w, out, NODES, ECOLS):
    NT = w["x"].shape[0] // P
    LAST = NODES - (NT - 1) * P
    PAIRS = NT // 2
    assert NT == 2 * PAIRS + 1 and PAIRS % 2 == 0 and NT % 7 == 0
    NCH = (ECOLS * P + NT * (P - 1)) // P
    NCH += -NCH % 16
    NCHP = NCH + 16
    CCOLS = -(-NCH // P)
    SCAT = 32
    assert ECOLS % SCAT == 0
    ACOLS = 2 * NT
    ETILES = (ACOLS * P + EXPERTS * (TILE_TOKENS - 1)) // TILE_TOKENS
    ETILES += ETILES % 2
    assert ETILES <= P
    HID = w["mix_W1T"].shape[1]
    HB = HID // P
    GH = w["gnn_W2"].shape[0] // P
    QK = 2 * C
    INV_P = 1.0 / P

    def dram(name, shape, dt=F32):
        return nc.dram_tensor(name, shape, dt, kind="Internal").ap()

    xn_d = dram("xn_d", (NT * P, C))
    q_d = dram("q_d", (NT * P, C))
    k_d = dram("k_d", (NT * P, C))
    xm_d = dram("xm_d", (NT * P, C))
    part_d = dram("part_d", (NT * P, C))
    elist_d = dram("elist_d", (P * NCH, 1), I32)
    chunk_d = dram("chunk_d", (CCOLS * P, 1), I32)
    etile_d = dram("etile_d", (P, 1), I32)
    xs_d = dram("xs_d", (ETILES * TILE_TOKENS, C))
    ys_d = dram("ys_d", (ETILES * TILE_TOKENS, C))

    outer = ExitStack()
    with outer:
        def tools(ctx, tag):
            sb = lambda name, shape, dt=F32: ctx.enter_context(nc.sbuf_tensor(f"{tag}_{name}", shape, dt))
            ps = lambda name, shape: ctx.enter_context(nc.psum_tensor(f"{tag}_{name}", shape, F32))
            sem = lambda name: ctx.enter_context(nc.semaphore(f"{tag}_{name}"))
            return sb, ps, sem

        sb, _, _ = tools(outer, "g")
        ident = sb("ident", [P, P])
        ones = sb("ones", [P, P])
        tri = sb("tri", [P, P])
        iota_b = sb("iota_b", [P, max(P, NT)])
        ids = iota_b[:, 0:NT]
        node_ids = iota_b[:, 0:P]
        unit_ids = sb("unit_ids", [P, CCOLS])
        part_ids = sb("part_ids", [P, 1])
        W12 = sb("W12", [P, KC, C])
        stat_mean = sb("mean", [P, NT])
        stat_a = sb("stat_a", [P, NT])
        stat_b = sb("stat_b", [P, NT])
        stats = sb("stats", [P, NT, 6])
        var = sb("var", [P, NT])
        rstd = sb("rstd", [P, NT])
        rstd2 = sb("rstd2", [P, NT])
        WR = sb("WR", [P, KC, EXPERTS])
        br = sb("br", [1, EXPERTS])
        brb = sb("brb", [P, EXPERTS])
        chunk_owner = sb("chunk_owner", [P, CCOLS], I32)

        mixctx = ExitStack()
        with mixctx:
            sb, _, _ = tools(mixctx, "m")
            RA = sb("RA", [P, KC, 3 * C])
            RB = sb("RB", [1, 3 * C])
            RBb = sb("RBb", [P, 3 * C])
            bob = sb("bob", [P, C])
            bsumb = sb("bsumb", [P, C])
            G = sb("G", [P, KC, C])
            M = sb("M", [P, KC, C])
            bo = sb("bo", [1, C])
            bsum = sb("bsum", [1, C])
            W1f = sb("W1f", [P, KC, HID])
            b1f = sb("b1f", [P, HB])
            W2 = sb("W2", [P, HB, C])
            addr = sb("addr", [P, ECOLS], I32)
            rec = sb("rec", [P, ECOLS], I32)

            c1 = ExitStack()
            with c1:
                sb, ps, sem = tools(c1, "b1")
                xg = sb("xg", [P, 2, 7, C])
                xg2 = sb("xg2", [P, 2, 7, C])
                src = sb("src", [P, ECOLS], I32)
                key = sb("key", [P, ECOLS])
                mask = sb("mask", [P, ECOLS])
                scan = sb("scan", [P, ECOLS])
                pos = sb("pos", [P, ECOLS])
                posi = src
                fill = sb("fill", [P, NCH], I32)
                counts = sb("counts", [P, NT])
                size = sb("size", [P, NT])
                cum = sb("cum", [P, NT])
                off = sb("off", [P, NT])
                t_int = sb("t_int", [P, NT], I32)
                ge = sb("ge", [P, CCOLS, NT])
                own_f = sb("own_f", [P, CCOLS])
                WxT = sb("WxT", [P, KC, C])
                Wx = sb("Wx", [P, KC, C])
                BD = sb("BD", [P, KC, QK])
                WvBD = sb("WvBD", [P, KC, C])
                WoT = sb("WoT", [P, KC, C])
                gW1T = sb("gW1T", [P, GH, C])
                gW2 = sb("gW2", [P, GH, C])
                cols = sb("cols", [P, 5 * KC + HB + GH])
                ln1w, ln1b, bxc, ln2w, ln2b = (cols[:, KC * n:KC * n + KC] for n in range(5))
                b1c = cols[:, 5 * KC:5 * KC + HB]
                gb1c = cols[:, 5 * KC + HB:]
                rows = sb("rows", [1, 3 * C])
                bxp = sb("bxp", [P, KC])
                xt = sb("xt", [P, 4, C])
                z = sb("z", [P, 2, C])
                xn = sb("xn", [P, 2, C])
                zT = sb("zT", [P, 2, C])
                q = sb("q", [P, 2, C])
                lg = sb("lg", [P, 2, QK])
                xm = sb("xm", [P, 2, C])
                mx = sb("mx", [P, HEADS])
                kmax = sb("kmax", [P, C])
                kmax_c = sb("kmax_c", [P, KC])
                diag = sb("diag", [P, KC, P])
                kmax_b = sb("kmax_b", [P, C])
                ksum = sb("ksum", [P, 8, C])
                KVm = sb("KVm", [P, KC, P])
                hmask = sb("hmask", [P, P])
                rden = sb("rden", [P, KC])
                qx = sb("qx", [P, 2, 2, C])
                xnp = sb("xnp", [P, 2, 2, C])
                xp = sb("xp", [P, 2, 2, C])
                qT = sb("qT", [P, KC, C])
                h = sb("h", [P, 2, 2, C])
                z2 = sb("z2", [P, 2, C])
                z2T = sb("z2T", [P, KC, C])
                hT = sb("hT", [P, HB, C])
                part = sb("part", [P, 2, C])
                pst = sb("pst", [P, 2, 6])
                pm, pv, pr, pa, pb = (sb(f"pair{n}", [P, 2]) for n in range(5))
                half = SCAT // 2
                ring_a = sb("ring_a", [P, 2, half], I32)
                ring_r = sb("ring_r", [P, 2, half], I32)
                bank = [ps(f"bank{n}", [P, 512]) for n in range(8)]
                cnt_ps = bank[2]

                const_done = sem("const_done")
                zero_done = sem("zero_done")
                edges_in = sem("edges_in")
                xg_in = [sem(f"xg_in{n}") for n in range(2)]
                xg_used = sem("xg_used")
                weights_in = sem("weights_in")
                diag_in = sem("diag_in")
                fold_mm = sem("fold_mm")
                fold_out = sem("fold_out")
                scaled = sem("scaled")
                counted = sem("counted")
                summed = sem("summed")
                owners = sem("owners")
                placed = sem("placed")
                stats_ready = sem("stats_ready")
                filled = sem("filled")
                owners_out = sem("owners_out")
                ring_ready = sem("ring_ready")
                sent = [sem(f"sent{n}") for n in range(2)]
                hm = sem("hm")
                x_in = [sem(f"x_in{n}") for n in range(4)]
                z_ready = sem("z_ready")
                xn_ready = sem("xn_ready")
                xn_out = [sem(f"xn_out{n}") for n in range(2)]
                zT_mm = sem("zT_mm")
                zT_ready = sem("zT_ready")
                qkx_mm = sem("qkx_mm")
                q_shift = sem("q_shift")
                q_exp = sem("q_exp")
                kx_ready = sem("kx_ready")
                q_ready = sem("q_ready")
                kx_out = [sem(f"kx_out{n}") for n in range(2)]
                q_out = [sem(f"q_out{n}") for n in range(2)]
                kmax_done = sem("kmax_done")
                kT_mm = sem("kT_mm")
                kdiag = sem("kdiag")
                kmax_mm = sem("kmax_mm")
                kx_in = [sem(f"kx_in{n}") for n in range(2)]
                k_sub = sem("k_sub")
                k_exp = sem("k_exp")
                k_sum = sem("k_sum")
                kv_mm = sem("kv_mm")
                den_mm = sem("den_mm")
                kv_ready = sem("kv_ready")
                M_mm = sem("M_mm")
                M_ready = sem("M_ready")
                pair_in = [sem(f"pair_in{n}") for n in range(2)]
                qT_mm = sem("qT_mm")
                qT_ready = sem("qT_ready")
                h_mm = sem("h_mm")
                z2_ready = sem("z2_ready")
                front_done = sem("front_done")
                z2T_mm = sem("z2T_mm")
                z2T_ready = sem("z2T_ready")
                up_mm = sem("up_mm")
                gelu = sem("gelu")
                y_mm = sem("y_mm")
                part_ready = sem("part_ready")
                part_out = sem("part_out")
                dve = sem("dve")
                hold = sem("hold")
                block = c1.enter_context(nc.Block())

                NG = NT // 7
                FIRST = 160 if ECOLS > 320 else 64
                CONSTS = 9
                rows_of = lambda d, i, n=1: d[bass.ds(i * P, n * P), :]
                L4 = NT // 4
                L2 = PAIRS // 2

                @block.gpsimd
                def _(pool):
                    pool.memset(ones[:], 1.0).then_inc(const_done, 1)
                    pool.memset(ident[:], 0.0).then_inc(const_done, 1)
                    pool.memset(tri[:], 1.0).then_inc(const_done, 1)
                    pool.wait_ge(const_done, 3)
                    pool.affine_select(out=ident[:], in_=ident[:], compare_op=ALU.not_equal, fill=1.0, base=0,
                                       pattern=[[-1, P]], channel_multiplier=1).then_inc(const_done, 1)
                    pool.affine_select(out=tri[:], in_=tri[:], compare_op=ALU.is_gt, fill=0.0, base=0,
                                       pattern=[[1, P]], channel_multiplier=-1).then_inc(const_done, 1)
                    pool.iota(iota_b[:], [[1, max(P, NT)]], base=0, channel_multiplier=0,
                              allow_small_or_imprecise_dtypes=True).then_inc(const_done, 1)
                    pool.iota(unit_ids[:], [[1, CCOLS]], base=0, channel_multiplier=CCOLS,
                              allow_small_or_imprecise_dtypes=True).then_inc(const_done, 1)
                    pool.iota(part_ids[:], [[1, 1]], base=0, channel_multiplier=1,
                              allow_small_or_imprecise_dtypes=True).then_inc(const_done, 1)
                    pool.memset(fill[:], P).then_inc(const_done, 1)
                    pool.memset(BD[:], 0.0).then_inc(zero_done, 1)
                    pool.memset(WvBD[:], 0.0).then_inc(zero_done, 1)
                    pool.memset(hmask[:], 0.0).then_inc(hm, 1)
                    pool.wait_ge(hm, 1)
                    for g in range(P // HD):
                        pool.memset(hmask[g * HD:g * HD + HD, g * HD:g * HD + HD], 1.0).then_inc(hm, 1)
                        pool.wait_ge(hm, g + 2)

                    def scatter(i):
                        for s in range(2):
                            at_least(pool, sent[s], i * (16 * half))
                            pool.sem_inc(hold, 1)
                            at = i * SCAT + s * half
                            pool.tensor_copy(ring_a[:, s, :], addr[:, bass.ds(at, half)]).then_inc(ring_ready, 1)
                            pool.tensor_copy(ring_r[:, s, :], rec[:, bass.ds(at, half)]).then_inc(ring_ready, 1)
                            pool.wait_ge(ring_ready, i * 4 + 2 * s + 2)
                            pool.sem_inc(hold, 1)
                            for c in range(half):
                                pool.indirect_dma_start(
                                    out=elist_d, out_offset=bass.IndirectOffsetOnAxis(ap=ring_a[:, s, c:c + 1], axis=0),
                                    in_=ring_r[:, s, c:c + 1], in_offset=None).then_inc(sent[s], 16)

                    pool.wait_ge(filled, 16)
                    pool.wait_ge(placed, 1)
                    scatter(0)
                    with pool.Fori(1, FIRST // SCAT) as i:
                        scatter(i)
                    pool.wait_ge(placed, 2)
                    with pool.Fori(FIRST // SCAT, ECOLS // SCAT) as i:
                        scatter(i)
                    for s in range(2):
                        pool.wait_ge(sent[s], ECOLS // SCAT * 16 * half)

                @block.sync
                def _(sp):
                    sp.dma_start(src[:], w["src"]).then_inc(edges_in, 16)
                    sp.dma_start(rec[:], w["dst"]).then_inc(edges_in, 16)
                    xgt = w["x"].rearrange("(g t p) c -> g p t c", p=P, t=7)
                    sp.dma_start(xg[:, 0], xgt[0]).then_inc(xg_in[0], 16)
                    sp.dma_start(xg[:, 1], xgt[1]).then_inc(xg_in[1], 16)
                    sp.wait_ge(const_done, CONSTS)
                    sp.dma_start(elist_d.rearrange("(p n) a -> p (n a)", p=P), fill[:]).then_inc(filled, 16)
                    sp.wait_ge(owners, 1)
                    sp.dma_start(chunk_d.rearrange("(p n) a -> p (n a)", p=P), chunk_owner[:]).then_inc(owners_out, 16)
                    for g in range(2, NG):
                        sp.wait_ge(xg_used, g - 1)
                        sp.dma_start(xg[:, g % 2], xgt[g]).then_inc(xg_in[g % 2], 16)

                    def load_x(i, c):
                        n = 4 * i + c
                        at_least(sp, z_ready, n - 3)
                        at_least(sp, xn_ready, n - 3)
                        sp.dma_start(xt[:, c % 4], rows_of(w["x"], n)).then_inc(x_in[c % 4], 16)

                    def store(i, c):
                        n, s = 4 * i + c, c % 2
                        sp.wait_ge(xn_ready, n + 1)
                        sp.dma_start(rows_of(xn_d, n), xn[:, s]).then_inc(xn_out[s], 16)
                        sp.wait_ge(kx_ready, n + 1)
                        sp.dma_start(rows_of(k_d, n), lg[:, s, C:QK]).then_inc(kx_out[s], 16)
                        sp.dma_start(rows_of(xm_d, n), xm[:, s]).then_inc(kx_out[s], 16)
                        sp.wait_ge(q_ready, n + 1)
                        sp.dma_start(rows_of(q_d, n), q[:, s]).then_inc(q_out[s], 16)

                    for c in range(3):
                        load_x(0, c)
                    for c in range(4):
                        load_x(0, c + 3)
                        store(0, c)
                    with sp.Fori(1, L4 - 1) as i:
                        for c in range(4):
                            load_x(i, c + 3)
                            store(i, c)
                    for c in range(4):
                        if c < 2:
                            load_x(L4 - 1, c + 3)
                        store(L4 - 1, c)
                    store(L4, 0)
                    for s, n in ((0, PAIRS + 1), (1, PAIRS)):
                        sp.wait_ge(kx_out[s], 32 * n)
                        sp.wait_ge(q_out[s], 16 * n)
                        sp.wait_ge(xn_out[s], 16 * n)

                    for g in range(NG):
                        if g >= 2:
                            sp.wait_ge(kv_mm, g - 1)
                            sp.wait_ge(k_sum, g - 1)
                        for dst, d in ((xg, k_d), (xg2, xm_d)):
                            sp.dma_start(dst[:, g % 2], d.rearrange("(g t p) c -> g p t c", p=P, t=7)[g]).then_inc(kx_in[g % 2], 16)

                    def load_pair(n, s, tiles=2):
                        at_least(sp, front_done, n - 1)
                        for dst, d in ((qx, q_d), (xnp, xn_d), (xp, w["x"])):
                            sp.dma_start(dst[:, s, 0:tiles, :], d[bass.ds(n * 2 * P, tiles * P), :].rearrange("(t p) c -> p t c", p=P))\
                              .then_inc(pair_in[s], 16)

                    def store_pair(n, tiles=2):
                        sp.wait_ge(part_ready, n + 1)
                        sp.dma_start(part_d[bass.ds(n * 2 * P, tiles * P), :].rearrange("(t p) c -> p t c", p=P), part[:, 0:tiles, :])\
                          .then_inc(part_out, 16)

                    load_pair(0, 0)
                    load_pair(1, 1)
                    for n in range(2):
                        load_pair(n + 2, n)
                        store_pair(n)
                    with sp.Fori(1, L2 - 1) as i:
                        for s in range(2):
                            load_pair(2 * i + s + 2, s)
                            store_pair(2 * i + s)
                    load_pair(PAIRS, 0, 1)
                    store_pair(PAIRS - 2)
                    store_pair(PAIRS - 1)
                    store_pair(PAIRS, 1)
                    sp.wait_ge(part_out, 16 * (PAIRS + 1))
                    sp.wait_ge(owners_out, 16)

                @block.vector
                def _(v):
                    ch = Chain(v, dve)
                    link = ch.link
                    v.wait_ge(edges_in, 32)
                    v.wait_ge(const_done, CONSTS)
                    link(v.tensor_scalar(rec[:], rec[:], 8, None, ALU.logical_shift_left))
                    link(v.tensor_scalar(scan[:].bitcast(I32), src[:], P - 1, None, ALU.bitwise_and))
                    link(v.tensor_tensor(rec[:], rec[:], scan[:].bitcast(I32), ALU.bitwise_or))
                    link(v.tensor_scalar(src[:], src[:], 7, None, ALU.logical_shift_right))
                    link(v.tensor_copy(key[:], src[:]))
                    link(v.memset(pos[:], 0.0))
                    count_keys(v, ch, key[:], mask[:], ids, counts[:], NT)
                    v.sem_inc(counted, 1)
                    v.wait_ge(summed, 1)
                    bucket_starts(v, ch, cnt_ps, NT, P, cum[:], size[:], off[:], t_int[:], ones[:, 0:NT])
                    tile_owner(v, ch, cum[:], NT, unit_ids[:], ge[:], own_f[:], chunk_owner[:], CCOLS)
                    v.sem_inc(owners, 1)

                    def place(lo, hi, more):
                        c = slice(lo, hi)
                        place_keys(v, ch, key[:, c], mask[:, c], scan[:, c], pos[:, c], ids, off[:], NT, hold, more)
                        link(v.tensor_scalar(pos[:, c], pos[:, c], -1.0, None, ALU.add))
                        link(v.tensor_copy(posi[:, c], pos[:, c]))
                        link(v.tensor_scalar(addr[:, c], posi[:, c], P - 1, None, ALU.bitwise_and))
                        link(v.tensor_scalar(posi[:, c], posi[:, c], 7, None, ALU.logical_shift_right))
                        link(v.tensor_copy(pos[:, c], addr[:, c]))
                        link(v.tensor_copy(scan[:, c], posi[:, c]))
                        link(v.scalar_tensor_tensor(pos[:, c], pos[:, c], float(NCH), scan[:, c], ALU.mult, ALU.add))
                        link(v.tensor_copy(addr[:, c], pos[:, c]))
                        v.sem_inc(placed, 1)

                    place(0, FIRST, True)
                    place(FIRST, ECOLS, False)
                    for g in range(NG):
                        v.wait_ge(xg_in[g % 2], 16 * (g // 2 + 1))
                        for t in range(7):
                            ins = v.bn_stats(stats[:, 7 * g + t, :], xg[:, g % 2, t, :])
                        ins.then_inc(xg_used, 1)
                    v.wait_ge(xg_used, NG)
                    mean_var(v, link, stats, stat_mean[:], var[:], stat_a[:])
                    double_norm(v, link, var[:], rstd[:], rstd2[:], stat_a[:], stat_b[:])
                    link(v.scalar_tensor_tensor(stat_a[:], stat_mean[:], -1.0, rstd[:], ALU.mult, ALU.mult))
                    v.sem_inc(stats_ready, 1)

                    link(v.memset(kmax[:], -3.0e38))
                    v.wait_ge(fold_out, 12)

                    def norm(i, c):
                        n = 4 * i + c
                        v.wait_ge(x_in[c % 4], 16 * (i + c // 4 + 1))
                        at_least(v, zT_mm, n - 1)
                        v.tensor_scalar(z[:, c % 2], xt[:, c % 4], stat_mean[:, bass.ds(n, 1)], rstd2[:, bass.ds(n, 1)],
                                        ALU.subtract, ALU.mult).then_inc(z_ready, 1)

                    def soft(i, c, used=P):
                        n, s = 4 * i + c, c % 2
                        v.wait_ge(qkx_mm, n + 1)
                        at_least(v, kx_out[s], 32 * (2 * i + c // 2))
                        link(v.tensor_tensor(lg[:, s], bank[4 + s][:], RBb[:, 0:QK], ALU.add))
                        v.tensor_tensor(xm[:, s], bank[6 + s][:, 0:C], RBb[:, QK:], ALU.add).then_inc(kx_ready, 1)
                        lq = lg[:, s, 0:C].rearrange("p (h s) -> p h s", s=HD)
                        qh = q[:, s].rearrange("p (h s) -> p h s", s=HD)
                        link(v.tensor_reduce(mx[:], lq, AX, ALU.max))
                        at_least(v, q_out[s], 16 * (2 * i + c // 2))
                        v.tensor_tensor(qh, lq, mx[:].unsqueeze(2).broadcast_to([P, HEADS, HD]), ALU.subtract)\
                         .then_inc(q_shift, 1)
                        link(v.tensor_tensor(kmax[0:used, :], kmax[0:used, :], lg[0:used, s, C:QK], ALU.max))
                        v.wait_ge(q_exp, n + 1)
                        link(v.tensor_reduce(mx[:], qh, AX, ALU.add))
                        link(v.reciprocal(mx[:], mx[:]))
                        v.tensor_tensor(qh, qh, mx[:].unsqueeze(2).broadcast_to([P, HEADS, HD]), ALU.mult)\
                         .then_inc(q_ready, 1)
                        v.wait_ge(q_ready, n + 1)

                    def lap(i):
                        for c in range(4):
                            norm(i, c + 2)
                            soft(i, c)

                    norm(0, 0)
                    norm(0, 1)
                    lap(0)
                    with v.Fori(1, L4 - 1) as i:
                        ch.enter(i - 1, 4 * 5)
                        lap(i)
                        ch.leave(L4 - 2)
                    for c in range(4):
                        if c < 3:
                            norm(L4 - 1, c + 2)
                        soft(L4 - 1, c)
                    soft(L4, 0, LAST)

                    v.sem_inc(kmax_done, 1)
                    v.wait_ge(kT_mm, 1)
                    for m in range(KC):
                        link(v.tensor_reduce(kmax_c[:, m:m + 1], bank[0][:, m * P:m * P + P], AX, ALU.max))
                    for m in range(KC):
                        link(v.tensor_scalar(diag[:, m], ident[:], kmax_c[:, m:m + 1], None, ALU.mult))
                    v.sem_inc(kdiag, 1)
                    v.wait_ge(kmax_mm, 1)
                    link(v.tensor_copy(kmax_b[:], bank[1][:, 0:C]))

                    def shift_k(g):
                        v.wait_ge(kx_in[g % 2], 32 * (g // 2 + 1))
                        v.tensor_tensor(xg[:, g % 2], xg[:, g % 2], kmax_b[:].unsqueeze(1).broadcast_to([P, 7, C]),
                                        ALU.subtract).then_inc(k_sub, 1)

                    def sum_k(g, tiles):
                        v.wait_ge(k_exp, g + 1)
                        v.tensor_reduce(ksum[:, g], xg[:, g % 2, 0:tiles].rearrange("p t c -> p c t"), AX, ALU.add)\
                         .then_inc(k_sum, 1)

                    shift_k(0)
                    for g in range(NG - 1):
                        shift_k(g + 1)
                        sum_k(g, 7)
                    sum_k(NG - 1, 6)
                    v.wait_ge(k_sum, NG)
                    last = ksum[0:LAST, NG - 1]
                    link(v.tensor_tensor(last, last, xg[0:LAST, (NG - 1) % 2, 6], ALU.add))
                    link(v.tensor_reduce(kmax_b[:], ksum[:, 0:NG].rearrange("p g c -> p c g"), AX, ALU.add))
                    v.sem_inc(k_sum, 1)
                    v.wait_ge(den_mm, 1)
                    v.wait_ge(hm, 1 + P // HD)
                    for m in range(KC):
                        link(v.tensor_tensor(KVm[:, m], bank[m][:, 0:P], hmask[:], ALU.mult))
                        link(v.reciprocal(rden[:, m:m + 1], bank[2][:, m:m + 1]))
                    v.sem_inc(kv_ready, 1)
                    for m in range(KC):
                        v.wait_ge(M_mm, m + 1)
                        link(v.tensor_scalar(M[:, m, :], bank[4 + m][:, 0:C], rden[:, m:m + 1], None, ALU.mult))
                    v.sem_inc(M_ready, 1)

                    def front(n, s, laps, nt=2):
                        v.wait_ge(h_mm, n + 1)
                        v.wait_ge(pair_in[s], 48 * laps)
                        hs = h[:, s, 0:nt]
                        flat = lambda a: a.rearrange("p t c -> p (t c)")
                        link(v.tensor_tensor(flat(hs), bank[1][:, 0:nt * C], flat(xnp[:, s, 0:nt]), ALU.add))
                        link(v.tensor_tensor(hs, hs, bob[:].unsqueeze(1).broadcast_to([P, nt, C]), ALU.add))
                        for t in range(2):
                            link(v.bn_stats(pst[:, t, :], h[:, s, t % nt, :]))
                        mean_var(v, link, pst, pm[:], pv[:], pa[:])
                        link(v.tensor_scalar(pa[:], pv[:], LN_EPS, None, ALU.add))
                        rsqrt(v, link, pr[:], pa[:], pb[:])
                        for t in range(2):
                            link(v.tensor_scalar(z2[:, t % nt], h[:, s, t % nt], pm[:, t:t + 1], pr[:, t:t + 1],
                                                 ALU.subtract, ALU.mult))
                        v.sem_inc(z2_ready, 1)
                        link(v.tensor_tensor(flat(hs), flat(hs), flat(xp[:, s, 0:nt]), ALU.add))
                        v.sem_inc(front_done, 1)
                        link(v.tensor_tensor(hs, hs, bsumb[:].unsqueeze(1).broadcast_to([P, nt, C]), ALU.add))

                    def back(n, s, nt=2):
                        v.wait_ge(y_mm, n + 1)
                        at_least(v, part_out, n * 16)
                        v.tensor_tensor(part[:, 0:nt].rearrange("p t c -> p (t c)"), bank[7][:, 0:nt * C],
                                        h[:, s, 0:nt].rearrange("p t c -> p (t c)"), ALU.add).then_inc(part_ready, 1)
                        v.wait_ge(part_ready, n + 1)

                    per = 2 + 2 + MEAN_VAR_LINKS + 1 + RSQRT_LINKS + 2 + 2

                    def lap2(i):
                        front(2 * i + 1, 1, i + 1)
                        back(2 * i, 0)
                        front(2 * i + 2, 0, i + 2)
                        back(2 * i + 1, 1)

                    front(0, 0, 1)
                    lap2(0)
                    with v.Fori(1, L2 - 1) as i:
                        ch.enter(i - 1, 2 * per)
                        lap2(i)
                        ch.leave(L2 - 2)
                    front(PAIRS - 1, 1, L2)
                    back(PAIRS - 2, 0)
                    front(PAIRS, 0, L2 + 1, 1)
                    back(PAIRS - 1, 1)
                    back(PAIRS, 0, 1)

                @block.scalar
                def _(a):
                    for dst, name in ((WxT, "mix_WxT"), (Wx, "mix_Wx"), (WoT, "mix_WoT"), (gW1T, "gnn_W1T"),
                                      (gW2, "gnn_W2"), (W1f, "mix_W1T"), (W2, "mix_W2T"), (WR, "ffn_Wr")):
                        a.dma_start(dst[:], w[name].rearrange("(k p) c -> p k c", p=P)).then_inc(weights_in, 16)
                    a.dma_start(cols[:], w["cols"]).then_inc(weights_in, 16)
                    for dst, name in ((rows[0:1, 0:C], "mix_bx"), (rows[0:1, C:2 * C], "gnn_b2"),
                                      (rows[0:1, 2 * C:3 * C], "mix_b2"), (bo[:], "mix_bo"), (br[:], "ffn_br")):
                        a.dma_start(dst, w[name]).then_inc(weights_in, 16)
                    a.wait_ge(zero_done, 2)
                    for hd in range(HEADS):
                        r, k = hd * HD % P, hd * HD // P
                        for dst, at, name in ((BD, 0, "mix_WqT"), (BD, C, "mix_WkT"), (WvBD, 0, "mix_Wv")):
                            a.dma_start(dst[r:r + HD, k, at + hd * HD:at + hd * HD + HD], w[name]).then_inc(diag_in, 16)
                    a.wait_ge(weights_in, 14 * 16)

                    def take(n, out_, f):
                        a.wait_ge(fold_mm, n + 1)
                        a.activation(out_, f, ACT.Copy).then_inc(fold_out, 1)

                    for m in range(KC):
                        a.wait_ge(fold_mm, m + 1)
                        a.activation(RA[:, m, 0:QK], bank[m][:, 0:QK], ACT.Identity, scale=ln1w[:, m:m + 1]).then_inc(fold_out, 1)
                    for m in range(KC):
                        a.activation(RA[:, m, QK:], WxT[:, m, :], ACT.Identity, scale=ln1w[:, m:m + 1]).then_inc(scaled, 1)
                    take(2, bxp[:], bank[0][:, 0:KC])
                    take(3, RB[0:1, 0:QK], bank[1][0:1, 0:QK])
                    take(4, RB[0:1, QK:], bank[0][0:1, 0:C])
                    take(5, G[:].rearrange("p k c -> p (k c)"), bank[1][:, 0:KC * C])
                    take(6, W12[:].rearrange("p k c -> p (k c)"), bank[0][:, 0:KC * C])
                    take(7, bsum[:], bank[1][0:1, 0:C])
                    take(8, b1f[:], bank[0][:, 0:HB])
                    for m in range(KC):
                        a.activation(W1f[:, m, :], W1f[:, m, :], ACT.Identity, scale=ln2w[:, m:m + 1]).then_inc(scaled, 1)
                    take(9, RBb[:, 0:QK], bank[1][:, 0:QK])
                    a.wait_ge(fold_mm, 11)
                    a.activation(RBb[:, QK:], bank[0][:, 0:C], ACT.Copy).then_inc(scaled, 1)
                    a.activation(bob[:], bank[0][:, C:2 * C], ACT.Copy).then_inc(fold_out, 1)
                    a.wait_ge(fold_mm, 12)
                    a.activation(bsumb[:], bank[1][:, 0:C], ACT.Copy).then_inc(scaled, 1)
                    a.activation(brb[:], bank[1][:, C:C + EXPERTS], ACT.Copy).then_inc(fold_out, 1)
                    a.wait_ge(stats_ready, 1)

                    def turn(i, c):
                        n, s = 4 * i + c, c % 2
                        a.wait_ge(zT_mm, n + 1)
                        at_least(a, qkx_mm, n - 1)
                        a.activation(zT[:, s], bank[s][:, 0:C], ACT.Copy).then_inc(zT_ready, 1)
                        a.wait_ge(x_in[c % 4], 16 * (i + c // 4 + 1))
                        at_least(a, xn_out[s], 16 * (2 * i + c // 2))
                        a.activation(xn[:, s], xt[:, c % 4], ACT.Identity, bias=stat_a[:, bass.ds(n, 1)],
                                     scale=rstd[:, bass.ds(n, 1)]).then_inc(xn_ready, 1)

                    def exp_q(i, c):
                        a.wait_ge(q_shift, 4 * i + c + 1)
                        a.activation(q[:, c % 2], q[:, c % 2], ACT.Exp).then_inc(q_exp, 1)

                    def lap(i):
                        for c in range(4):
                            turn(i, c + 1)
                            exp_q(i, c)

                    turn(0, 0)
                    lap(0)
                    with a.Fori(1, L4) as i:
                        lap(i)
                    exp_q(L4, 0)

                    for g in range(NG):
                        a.wait_ge(k_sub, g + 1)
                        a.activation(xg[:, g % 2], xg[:, g % 2], ACT.Exp).then_inc(k_exp, 1)

                    def copy_q(n, nt=2):
                        a.wait_ge(qT_mm, n + 1)
                        at_least(a, h_mm, n)
                        a.activation(qT[:, :, 0:nt * P], bank[0][:, 0:KC * nt * P].rearrange("p (k c) -> p k c", k=KC),
                                     ACT.Copy).then_inc(qT_ready, 1)

                    def copy_z(n, nt=2):
                        a.wait_ge(z2T_mm, n + 1)
                        a.activation(z2T[:, :, 0:nt * P], bank[2][:, 0:KC * nt * P].rearrange("p (k c) -> p k c", k=KC),
                                     ACT.Copy).then_inc(z2T_ready, 1)

                    def gelus(n, nt=2):
                        at_least(a, y_mm, n)
                        for j in range(HB):
                            a.wait_ge(up_mm, n * HB + j + 1)
                            a.activation(hT[:, j, 0:nt * P], bank[3 + j % 4][:, 0:nt * P], ACT.Gelu, bias=b1f[:, j:j + 1])\
                             .then_inc(gelu, 1)

                    def lap1(n, nt=2):
                        copy_q(n + 1, nt)
                        gelus(n)
                        copy_z(n + 1, nt)

                    copy_q(0)
                    copy_z(0)
                    lap1(0)
                    with a.Fori(1, PAIRS - 1) as n:
                        lap1(n)
                    lap1(PAIRS - 1, 1)
                    gelus(PAIRS, 1)

                @block.tensor
                def _(pe):
                    pe.wait_ge(weights_in, 14 * 16)
                    pe.wait_ge(diag_in, 3 * HEADS * 16)
                    pe.wait_ge(const_done, CONSTS)

                    def room(n):
                        if n >= 2:
                            pe.wait_ge(fold_out, n - 1)
                        return bank[n % 2]

                    for m in range(KC):
                        f = room(m)
                        for k in range(KC):
                            mm = pe.matmul(f[:, 0:QK], Wx[:, k, m * P:m * P + P], BD[:, k, :], start=(k == 0), stop=(k == KC - 1))
                        mm.then_inc(fold_mm, 1)
                    f = room(2)
                    pe.matmul(f[:, 0:KC], ident[:], bxc, start=True, stop=False)
                    for m in range(KC):
                        for k in range(KC):
                            mm = pe.matmul(f[:, m:m + 1], WxT[:, k, m * P:m * P + P], ln1b[:, k:k + 1],
                                           start=False, stop=(m == KC - 1 and k == KC - 1))
                    mm.then_inc(fold_mm, 1)
                    f = room(3)
                    pe.wait_ge(fold_out, 3)
                    for k in range(KC):
                        mm = pe.matmul(f[0:1, 0:QK], bxp[:, k:k + 1], BD[:, k, :], start=(k == 0), stop=(k == KC - 1))
                    mm.then_inc(fold_mm, 1)
                    f = room(4)
                    pe.matmul(f[0:1, 0:C], ones[0:1, 0:1], rows[0:1, 0:C], start=True, stop=False)
                    for k in range(KC):
                        mm = pe.matmul(f[0:1, 0:C], ln1b[:, k:k + 1], WxT[:, k, :], start=False, stop=(k == KC - 1))
                    mm.then_inc(fold_mm, 1)
                    f = room(5)
                    for m in range(KC):
                        for k in range(KC):
                            mm = pe.matmul(f[:, m * C:m * C + C], WvBD[:, k, m * P:m * P + P], WoT[:, k, :],
                                           start=(k == 0), stop=(k == KC - 1))
                    mm.then_inc(fold_mm, 1)
                    f = room(6)
                    for m in range(KC):
                        for k in range(GH):
                            mm = pe.matmul(f[:, m * C:m * C + C], gW1T[:, k, m * P:m * P + P], gW2[:, k, :],
                                           start=(k == 0), stop=(k == GH - 1))
                    mm.then_inc(fold_mm, 1)
                    f = room(7)
                    pe.matmul(f[0:1, 0:C], ones[0:1, 0:1], rows[0:1, C:2 * C], start=True, stop=False)
                    pe.matmul(f[0:1, 0:C], ones[0:1, 0:1], rows[0:1, 2 * C:3 * C], start=False, stop=False)
                    for k in range(GH):
                        mm = pe.matmul(f[0:1, 0:C], gb1c[:, k:k + 1], gW2[:, k, :], start=False, stop=(k == GH - 1))
                    mm.then_inc(fold_mm, 1)
                    f = room(8)
                    pe.matmul(f[:, 0:HB], ident[:], b1c, start=True, stop=False)
                    for j in range(HB):
                        for k in range(KC):
                            mm = pe.matmul(f[:, j:j + 1], W1f[:, k, j * P:j * P + P], ln2b[:, k:k + 1],
                                           start=False, stop=(j == HB - 1 and k == KC - 1))
                    mm.then_inc(fold_mm, 1)
                    f = room(9)
                    pe.matmul(f[:, 0:QK], ones[0:1, :], RB[0:1, 0:QK], start=True, stop=True).then_inc(fold_mm, 1)
                    f = room(10)
                    pe.matmul(f[:, 0:C], ones[0:1, :], RB[0:1, QK:], start=True, stop=True)
                    pe.matmul(f[:, C:2 * C], ones[0:1, :], bo[:], start=True, stop=True).then_inc(fold_mm, 1)
                    f = room(11)
                    pe.matmul(f[:, 0:C], ones[0:1, :], bsum[:], start=True, stop=True)
                    pe.matmul(f[:, C:C + EXPERTS], ones[0:1, :], br[:], start=True, stop=True).then_inc(fold_mm, 1)
                    pe.wait_ge(counted, 1)
                    pe.matmul(cnt_ps[:, 0:NT], tri[:], counts[:], start=True, stop=True)
                    pe.matmul(cnt_ps[:, NT:2 * NT], ones[:], counts[:], start=True, stop=True).then_inc(summed, 1)
                    pe.wait_ge(fold_out, 12)
                    pe.wait_ge(scaled, 2 * KC + 2)

                    def turn(i, c):
                        n, s = 4 * i + c, c % 2
                        pe.wait_ge(z_ready, n + 1)
                        at_least(pe, zT_ready, n - 1)
                        for k in range(KC):
                            mm = pe.transpose(bank[s][:, k * P:k * P + P], z[:, s, k * P:k * P + P], ident[:])
                        mm.then_inc(zT_mm, 1)

                    def project(i, c):
                        n, s = 4 * i + c, c % 2
                        pe.wait_ge(zT_ready, n + 1)
                        at_least(pe, kx_ready, n - 1)
                        for o, lo, hi in ((4 + s, 0, QK), (6 + s, QK, 3 * C)):
                            for k in range(KC):
                                mm = pe.matmul(bank[o][:, 0:hi - lo], zT[:, s, k * P:k * P + P], RA[:, k, lo:hi],
                                               start=(k == 0), stop=(k == KC - 1))
                        mm.then_inc(qkx_mm, 1)

                    def lap(i):
                        for c in range(4):
                            turn(i, c + 1)
                            project(i, c)

                    turn(0, 0)
                    lap(0)
                    with pe.Fori(1, L4) as i:
                        lap(i)
                    project(L4, 0)

                    pe.wait_ge(kmax_done, 1)
                    for m in range(KC):
                        mm = pe.transpose(bank[0][:, m * P:m * P + P], kmax[:, m * P:m * P + P], ident[:])
                    mm.then_inc(kT_mm, 1)
                    pe.wait_ge(kdiag, 1)
                    for m in range(KC):
                        mm = pe.matmul(bank[1][:, m * P:m * P + P], ones[:], diag[:, m], start=True, stop=True)
                    mm.then_inc(kmax_mm, 1)
                    for g in range(NG):
                        pe.wait_ge(k_exp, g + 1)
                        for t in range(7):
                            n = 7 * g + t
                            used = LAST if n == NT - 1 else P
                            for m in range(KC):
                                mm = pe.matmul(bank[m][:, 0:P], xg2[0:used, g % 2, t, m * P:m * P + P],
                                               xg[0:used, g % 2, t, m * P:m * P + P], start=(n == 0), stop=(n == NT - 1))
                        mm.then_inc(kv_mm, 1)
                    pe.wait_ge(k_sum, NG + 1)
                    for m in range(KC):
                        mm = pe.matmul(bank[2][:, m:m + 1], kmax_b[:, m * P:m * P + P], ones[:, 0:1], start=True, stop=True)
                    mm.then_inc(den_mm, 1)
                    pe.wait_ge(kv_ready, 1)
                    for m in range(KC):
                        pe.matmul(bank[4 + m][:, 0:C], KVm[:, m], G[:, m, :], start=True, stop=True).then_inc(M_mm, 1)
                    pe.wait_ge(M_ready, 1)

                    def turn_q(n, s, laps, nt=2):
                        pe.wait_ge(pair_in[s], 48 * laps)
                        at_least(pe, qT_ready, n)
                        for k in range(KC):
                            for t in range(nt):
                                mm = pe.transpose(bank[0][:, (k * nt + t) * P:(k * nt + t + 1) * P],
                                                  qx[:, s, t, k * P:k * P + P], ident[:])
                        mm.then_inc(qT_mm, 1)

                    def attend(n, nt=2):
                        pe.wait_ge(qT_ready, n + 1)
                        at_least(pe, z2_ready, n)
                        for t in range(nt):
                            for k in range(KC):
                                mm = pe.matmul(bank[1][:, t * C:t * C + C], qT[:, k, t * P:t * P + P], M[:, k, :],
                                               start=(k == 0), stop=(k == KC - 1))
                        mm.then_inc(h_mm, 1)

                    def turn_z(n, nt=2):
                        pe.wait_ge(z2_ready, n + 1)
                        at_least(pe, z2T_ready, n)
                        for k in range(KC):
                            for t in range(nt):
                                mm = pe.transpose(bank[2][:, (k * nt + t) * P:(k * nt + t + 1) * P],
                                                  z2[:, t, k * P:k * P + P], ident[:])
                        mm.then_inc(z2T_mm, 1)

                    def up(n, nt=2):
                        N = nt * P
                        pe.wait_ge(z2T_ready, n + 1)
                        for j in range(HB):
                            at_least(pe, gelu, n * HB + j - 3)
                            for k in range(KC):
                                mm = pe.matmul(bank[3 + j % 4][:, 0:N], W1f[:, k, j * P:j * P + P], z2T[:, k, 0:N],
                                               start=(k == 0), stop=(k == KC - 1))
                            mm.then_inc(up_mm, 1)

                    def down(n, nt=2):
                        pe.wait_ge(gelu, n * HB + HB)
                        at_least(pe, part_ready, n)
                        for t in range(nt):
                            for j in range(HB):
                                mm = pe.matmul(bank[7][:, t * C:t * C + C], hT[:, j, t * P:t * P + P], W2[:, j, :],
                                               start=(j == 0), stop=(j == HB - 1))
                        mm.then_inc(y_mm, 1)

                    def lap1(n, s, laps, nt=2):
                        turn_q(n + 1, s, laps, nt)
                        up(n)
                        attend(n + 1, nt)
                        down(n)
                        turn_z(n + 1, nt)

                    turn_q(0, 0, 1)
                    attend(0)
                    turn_z(0)
                    lap1(0, 1, 1)
                    lap1(1, 0, 2)
                    with pe.Fori(1, L2 - 1) as i:
                        lap1(2 * i, 1, i + 1)
                        lap1(2 * i + 1, 0, i + 2)
                    lap1(PAIRS - 2, 1, L2)
                    lap1(PAIRS - 1, 0, L2 + 1, 1)
                    up(PAIRS, 1)
                    down(PAIRS, 1)

        sb, _, _ = tools(outer, "r")
        acc = sb("acc", [P, NT, C])
        idx = sb("idx", [P, NT, 2], I32)
        wgt = sb("wgt", [P, 2, NT])
        key2 = sb("key2", [P, ACOLS])
        owner_row = sb("owner_row", [1, P], I32)

        part = sb("part", [P, NT, C])

        c3 = ExitStack()
        with c3:
            sb, ps, sem = tools(c3, "b3")
            zrow = sb("zrow", [P, 8, C])
            zeroed = sem("zeroed")
            xs_zero = sem("xs_zero")
            part_in = sem("part_in")
            elist = sb("elist", [P, NCHP], I32)
            low = sb("low", [P, NCHP])
            crow = sb("crow", [1, CCOLS * P], I32)
            hot = sb("hot", [P, 2, 8, P])
            src_ring = sb("src_ring", [P, 2, 8], I32)
            rows16 = sb("rows16", [P, 16, C])
            bank = [ps(f"bank{n}", [P, 512]) for n in range(8)]
            list_in = sem("list_in")
            acc_in = sem("acc_in")
            zero = sem("zero")
            ready = sem("ready")
            gathered = [sem(f"gathered{n}") for n in range(16)]
            free = sem("free")
            added = sem("added")
            hold = sem("hold")
            dve = sem("dve")
            block = c3.enter_context(nc.Block())

            @block.sync
            def _(sp):
                sp.dma_start(elist[:, 0:NCH], elist_d.rearrange("(p n) a -> p (n a)", p=P)).then_inc(list_in, 16)
                sp.dma_start(crow[:], chunk_d.rearrange("n a -> a n")).then_inc(list_in, 16)
                sp.dma_start(acc[:], xn_d.rearrange("(t p) c -> p t c", p=P)).then_inc(acc_in, 16)
                sp.dma_start(part[:], part_d.rearrange("(t p) c -> p t c", p=P)).then_inc(part_in, 16)
                sp.wait_ge(zeroed, 1)
                for g in range(ETILES // 4):
                    sp.dma_start(xs_d[g * 8 * P:(g + 1) * 8 * P, :].rearrange("(t p) c -> p t c", p=P), zrow[:])\
                      .then_inc(xs_zero, 16)
                if ETILES % 4:
                    sp.dma_start(xs_d[(ETILES - 2) * 2 * P:, :].rearrange("(t p) c -> p t c", p=P), zrow[:, 0:4])\
                      .then_inc(xs_zero, 16)
                sp.wait_ge(part_in, 16)
                sp.wait_ge(xs_zero, 16 * (-(-ETILES // 4)))

            @block.vector
            def _(v):
                ch = Chain(v, dve)
                v.memset(zrow[:], 0.0).then_inc(zeroed, 1)
                ch.link(v.memset(elist[:, NCH:], P))
                v.wait_ge(list_in, 32)
                low_i = rows16[:].rearrange("p a b -> p (a b)")[:, 0:NCHP].bitcast(I32)
                ch.link(v.tensor_scalar(low_i, elist[:], 255, None, ALU.bitwise_and))
                ch.link(v.tensor_copy(low[:], low_i))
                ch.link(v.tensor_scalar(elist[:], elist[:], 8, None, ALU.logical_shift_right))

                def prepare(at, s):
                    v.tensor_tensor(hot[:, s], low[:, bass.ds(at, 8)].unsqueeze(2).broadcast_to([P, 8, P]),
                                    node_ids.unsqueeze(1).broadcast_to([P, 8, P]), ALU.is_equal).then_inc(ready, 1)
                    v.tensor_copy(src_ring[:, s], elist[:, bass.ds(at, 8)]).then_inc(ready, 1)

                def add(i, s):
                    _, owner = nc.values_load_multi_w_load_instructions(
                        crow[0:1, bass.ds(i * 16 + s * 8, 8)], engines=[mybir.EngineType.DVE], min_val=0, max_val=NT - 1,
                        skip_runtime_bounds_check_because="the owners were clamped to the last tile")
                    for c in range(8):
                        v.wait_ge(free, i * 16 + s * 8 + c + 17)
                        v.wait_ge(added, i * 16 + s * 8 + c + 8)
                        tile = acc[:, bass.ds(owner[c], 1), :].rearrange("p a c -> p (a c)")
                        v.tensor_tensor(tile, tile, bank[c][:, 0:C], ALU.add).then_inc(added, 1)

                v.sem_inc(added, 8)
                prepare(0, 0)
                v.wait_ge(acc_in, 16)
                with v.Fori(0, NCH // 16) as i:
                    v.wait_ge(free, i * 16 + 16)
                    prepare(i * 16 + 8, 1)
                    add(i, 0)
                    v.wait_ge(free, i * 16 + 24)
                    prepare(i * 16 + 16, 0)
                    add(i, 1)

            @block.gpsimd
            def _(pool):
                with pool.Fori(0, NCH // 16) as i:
                    for s in range(2):
                        pool.wait_ge(ready, i * 4 + 2 * s + 2)
                        pool.sem_inc(hold, 1)
                        for c in range(8):
                            n = 8 * s + c
                            pool.wait_ge(free, i * 16 + n + 1)
                            pool.sem_inc(hold, 1)
                            pool.indirect_dma_start(
                                out=rows16[:, n, :], out_offset=None, in_=xn_d,
                                in_offset=bass.IndirectOffsetOnAxis(ap=src_ring[:, s, c:c + 1], axis=0))\
                                .then_inc(gathered[n], 16)

            @block.tensor
            def _(pe):
                pe.sem_inc(free, 16)
                with pe.Fori(0, NCH // 16) as i:
                    for s in range(2):
                        pe.wait_ge(ready, i * 4 + 2 * s + 2)
                        for c in range(8):
                            n = 8 * s + c
                            pe.wait_ge(gathered[n], i * 16 + 16)
                            pe.wait_ge(added, i * 16 + n + 1)
                            pe.matmul(bank[c][:, 0:C], hot[:, s, c], rows16[:, n, :], start=True, stop=True).then_inc(free, 1)

        LH = PAIRS // 2
        sb, _, _ = tools(outer, "w")
        E1 = sb("E1", [P, 2, KC, HID])
        E2 = sb("E2", [P, 2, HB, C])
        vec = sb("vec", [P, 2, 2 * KC + HB])
        b2e = sb("b2e", [P, 2, C])
        w1_d = w["ffn_W1"].rearrange("(e k p) h -> e p k h", p=P, k=KC)
        w2_d = w["ffn_W2"].rearrange("(e j p) c -> e p j c", p=P, j=HB)

        def expert_of(t):
            return nc.values_load(owner_row[0:1, bass.ds(t, 1)], engines=[mybir.EngineType.SP],
                                  min_val=0, max_val=EXPERTS - 1,
                                  skip_runtime_bounds_check_because="the owners were clamped to the last expert")

        def load_up(sp, e, s, landed): 
            sp.dma_start(E1[:, s], w1_d[bass.ds(e, 1)].rearrange("a p k h -> p (a k) h")).then_inc(landed, 16)
            sp.dma_start(vec[:, s], w["ffn_vec"][bass.ds(e, 1)].rearrange("a p k -> p (a k)")).then_inc(landed, 16)

        def load_down(sp, e, s, landed):
            sp.dma_start(E2[:, s], w2_d[bass.ds(e, 1)].rearrange("a p k h -> p (a k) h")).then_inc(landed, 16)
            sp.dma_start(b2e[:, s], w["ffn_b2"][bass.ds(e, 1)].broadcast_to([P, C])).then_inc(landed, 16)

        c4 = ExitStack()
        with c4:
            sb, ps, sem = tools(c4, "b4")
            a_s = sb("a_s", [P, 2, C])
            aT = sb("aT", [P, 2, C])
            u = sb("u", [P, 2, C])
            uT = sb("uT", [P, 2, C])
            lg = sb("lg", [P, NT, EXPERTS])
            eq = sb("eq", [P, NT, EXPERTS])
            rev = sb("rev", [P, EXPERTS])
            best = sb("best", [P, 2, NT])
            first = sb("first", [P, NT])
            second = sb("second", [P, NT])
            mask = sb("mask", [P, ACOLS])
            scan = sb("scan", [P, ACOLS])
            pos = sb("pos", [P, ACOLS])
            counts, size, cum, off = (sb(f"e{n}", [P, EXPERTS]) for n in range(4))
            t_int = sb("t_int", [P, EXPERTS], I32)
            ge = sb("ge", [P, 1, EXPERTS])
            own_f = sb("own_f", [P, 1])
            own_i = sb("own_i", [P, 1], I32)
            z3 = sb("z3", [P, 4, C])
            ring = sb("ring", [P, 2, 4], I32)
            bank = [ps(f"bank{n}", [P, 512]) for n in range(8)]
            a_ready = sem("a_ready")
            aT_mm = sem("aT_mm")
            aT_ready = sem("aT_ready")
            gnn_mm = sem("gnn_mm")
            x1_ready = sem("x1_ready")
            stat_ok = sem("stat_ok")
            u_ready = sem("u_ready")
            uT_mm = sem("uT_mm")
            uT_ready = sem("uT_ready")
            lg_mm = sem("lg_mm")
            lg_ready = sem("lg_ready")
            diff_ready = sem("diff_ready")
            exp_ready = sem("exp_ready")
            counted = sem("counted")
            summed = sem("summed")
            owners = sem("owners")
            own_out = sem("own_out")
            own_in = sem("own_in")
            ahead = sem("ahead")
            placed = sem("placed")
            z3_ready = sem("z3_ready")
            ring_ready = sem("ring_ready")
            sent = [sem(f"sent{n}") for n in range(4)]
            hold = sem("hold")
            dve = sem("dve")
            block = c4.enter_context(nc.Block())
            tile_of = lambda n: acc[:, bass.ds(n, 1), :].rearrange("p a c -> p (a c)")

            @block.sync
            def _(sp):
                sp.wait_ge(owners, 1)
                sp.dma_start(etile_d, own_i[:]).then_inc(own_out, 16)
                sp.wait_ge(own_out, 16)
                sp.dma_start(owner_row[:], etile_d.rearrange("n a -> a n")).then_inc(own_in, 16)
                sp.wait_ge(own_in, 16)
                for t in range(2):
                    e = expert_of(t)
                    load_up(sp, e, t, ahead)
                    load_down(sp, e, t, ahead)
                sp.wait_ge(ahead, 2 * 4 * 16)

            @block.tensor
            def _(pe):
                def turn(n, s, ready, emptied, mm_done, from_):
                    pe.wait_ge(ready, n + 1)
                    at_least(pe, emptied, n - 1)
                    for k in range(KC):
                        mm = pe.transpose(bank[s][:, k * P:k * P + P], from_[:, s, k * P:k * P + P], ident[:])
                    mm.then_inc(mm_done, 1)

                def product(n, s, ready, emptied, mm_done, lhs, rhs, out_):
                    pe.wait_ge(ready, n + 1)
                    at_least(pe, emptied, n - 1)
                    for k in range(KC):
                        mm = pe.matmul(out_, lhs[:, s, k * P:k * P + P], rhs[:, k, :], start=(k == 0), stop=(k == KC - 1))
                    mm.then_inc(mm_done, 1)

                def steps(turn_args, product_args, banks):
                    def lap(i):
                        for s in range(2):
                            turn(2 * i + s + 1, 1 - s, *turn_args)
                            product(2 * i + s, s, *product_args, banks[s])

                    turn(0, 0, *turn_args)
                    lap(0)
                    with pe.Fori(1, PAIRS) as i:
                        lap(i)
                    product(NT - 1, 0, *product_args, banks[0])

                steps((a_ready, aT_ready, aT_mm, a_s), (aT_ready, x1_ready, gnn_mm, aT, W12),
                      [bank[2 + s][:, 0:C] for s in range(2)])
                pe.wait_ge(aT_ready, NT)
                steps((u_ready, uT_ready, uT_mm, u), (uT_ready, lg_ready, lg_mm, uT, WR),
                      [bank[4 + s][:, 0:EXPERTS] for s in range(2)])
                pe.wait_ge(counted, 1)
                pe.matmul(bank[6][:, 0:EXPERTS], tri[:], counts[:], start=True, stop=True)
                pe.matmul(bank[6][:, EXPERTS:2 * EXPERTS], ones[:], counts[:], start=True, stop=True).then_inc(summed, 1)

            @block.scalar
            def _(a):
                def fetch(n, s):
                    at_least(a, aT_mm, n - 1)
                    a.activation(a_s[:, s], tile_of(n), ACT.Copy).then_inc(a_ready, 1)

                def turn(n, s):
                    a.wait_ge(aT_mm, n + 1)
                    at_least(a, gnn_mm, n - 1)
                    a.activation(aT[:, s], bank[s][:, 0:C], ACT.Copy).then_inc(aT_ready, 1)

                def lap(i):
                    for s in range(2):
                        fetch(2 * i + s + 1, 1 - s)
                        turn(2 * i + s, s)

                fetch(0, 0)
                lap(0)
                with a.Fori(1, PAIRS) as i:
                    lap(i)
                turn(NT - 1, 0)

                def turn_u(n, s):
                    a.wait_ge(uT_mm, n + 1)
                    at_least(a, lg_mm, n - 1)
                    a.activation(uT[:, s], bank[s][:, 0:C], ACT.Copy).then_inc(uT_ready, 1)

                for s in range(2):
                    turn_u(s, s)
                with a.Fori(1, PAIRS) as i:
                    for s in range(2):
                        turn_u(2 * i + s, s)
                turn_u(NT - 1, 0)
                a.wait_ge(diff_ready, 1)
                a.activation(second[:], second[:], ACT.Exp).then_inc(exp_ready, 1)

                def rows(i, c):
                    n = 4 * i + c
                    at_least(a, sent[c], i * 32)
                    a.activation(z3[:, c], tile_of(n), ACT.Identity,
                                 bias=var[:, bass.ds(n, 1)], scale=rstd2[:, bass.ds(n, 1)]).then_inc(z3_ready, 1)

                for c in range(4):
                    rows(0, c)
                with a.Fori(1, LH) as i:
                    for c in range(4):
                        rows(i, c)
                rows(LH, 0)

            @block.vector
            def _(v):
                ch = Chain(v, dve)
                link = ch.link

                def x1(n, s):
                    v.wait_ge(gnn_mm, n + 1)
                    tile = tile_of(n)
                    v.tensor_tensor(tile, bank[2 + s][:, 0:C], part[:, bass.ds(n, 1), :].rearrange("p a c -> p (a c)"),
                                    ALU.add).then_inc(x1_ready, 1)

                def stat(n):
                    v.wait_ge(x1_ready, n + 1)
                    v.sem_inc(hold, 1)
                    v.bn_stats(stats[:, bass.ds(n, 1), :].rearrange("p a c -> p (a c)"), tile_of(n)).then_inc(stat_ok, 1)

                x1(0, 0)
                with v.Fori(0, PAIRS) as i:
                    for s in range(2):
                        x1(2 * i + s + 1, 1 - s)
                        stat(2 * i + s)
                stat(NT - 1)
                v.wait_ge(stat_ok, NT)
                mean_var(v, link, stats, stat_mean[:], var[:], stat_a[:])
                double_norm(v, link, var[:], rstd[:], rstd2[:], stat_a[:], stat_b[:])
                link(v.scalar_tensor_tensor(var[:], stat_mean[:], -1.0, rstd2[:], ALU.mult, ALU.mult))

                def norm(n, s):
                    at_least(v, uT_mm, n - 1)
                    v.tensor_scalar(u[:, s], tile_of(n), stat_mean[:, bass.ds(n, 1)], rstd[:, bass.ds(n, 1)],
                                    ALU.subtract, ALU.mult).then_inc(u_ready, 1)

                def logits(n, s):
                    v.wait_ge(lg_mm, n + 1)
                    v.tensor_tensor(lg[:, bass.ds(n, 1), :].rearrange("p a e -> p (a e)"), bank[4 + s][:, 0:EXPERTS], brb[:],
                                    ALU.add).then_inc(lg_ready, 1)

                norm(0, 0)
                norm(1, 1)
                for s in range(2):
                    norm(s + 2, s)
                    logits(s, s)
                with v.Fori(1, PAIRS - 1) as i:
                    for s in range(2):
                        norm(2 * i + s + 2, s)
                        logits(2 * i + s, s)
                norm(NT - 1, 0)
                for n in range(NT - 3, NT):
                    logits(n, n % 2)
                v.wait_ge(lg_ready, NT)

                link(v.tensor_scalar(rev[:], ids[:, 0:EXPERTS], -1.0, float(EXPERTS), ALU.mult, ALU.add))
                spread = lambda a: a.unsqueeze(2).broadcast_to([P, NT, EXPERTS])
                rev_b = rev[:].unsqueeze(1).broadcast_to([P, NT, EXPERTS])
                for c, best_c in enumerate((best[:, 0, :], best[:, 1, :])):
                    choice = key2[:, c * NT:c * NT + NT]
                    link(v.tensor_reduce(best_c, lg[:], AX, ALU.max))
                    link(v.tensor_tensor(eq[:], lg[:], spread(best_c), ALU.is_equal))
                    link(v.tensor_tensor(eq[:], eq[:], rev_b, ALU.mult))
                    link(v.tensor_reduce(choice, eq[:], AX, ALU.max))
                    if c == 0:
                        link(v.tensor_tensor(eq[:], rev_b, spread(choice), ALU.is_equal))
                        link(v.scalar_tensor_tensor(lg[:], eq[:], -3.0e38, lg[:], ALU.mult, ALU.add))
                    link(v.tensor_scalar(choice, choice, -1.0, float(EXPERTS), ALU.mult, ALU.add))
                    link(v.tensor_scalar(choice, choice, float(EXPERTS - 1), None, ALU.min))
                link(v.tensor_tensor(second[:], best[:, 1, :], best[:, 0, :], ALU.subtract))
                v.sem_inc(diff_ready, 1)

                link(v.memset(pos[:], 0.0))
                count_keys(v, ch, key2[:], mask[:], ids, counts[:], EXPERTS)
                v.sem_inc(counted, 1)
                v.wait_ge(summed, 1)
                bucket_starts(v, ch, bank[6], EXPERTS, TILE_TOKENS, cum[:], size[:], off[:], t_int[:], ones[:, 0:EXPERTS])
                tile_owner(v, ch, cum[:], EXPERTS, part_ids[:], ge[:], own_f[:], own_i[:], 1)
                v.sem_inc(owners, 1)
                place_keys(v, ch, key2[:], mask[:], scan[:], pos[:], ids, off[:], EXPERTS, hold)
                link(v.tensor_scalar(pos[:], pos[:], -1.0, None, ALU.add))
                link(v.tensor_copy(idx[:].rearrange("p n a -> p a n"), pos[:].rearrange("p (a n) -> p a n", a=2)))
                v.sem_inc(placed, 1)
                v.wait_ge(exp_ready, 1)
                link(v.tensor_scalar(first[:], second[:], 1.0, None, ALU.add))
                link(v.reciprocal(wgt[:, 0, :], first[:]))
                link(v.tensor_tensor(wgt[:, 1, :], wgt[:, 0, :], second[:], ALU.mult))

            @block.gpsimd
            def _(pool):
                def send(i, s, tiles=2):
                    for c in range(2 * s, 2 * s + tiles):
                        at_least(pool, sent[c], i * 32)
                    pool.sem_inc(hold, 1)
                    n = 4 * i + 2 * s
                    pool.tensor_copy(ring[:, s, 0:2 * tiles], idx[:, bass.ds(n, tiles), :].rearrange("p n a -> p (n a)"))\
                        .then_inc(ring_ready, 1)
                    pool.wait_ge(ring_ready, 2 * i + s + 1)
                    pool.sem_inc(hold, 1)
                    for c in range(tiles):
                        pool.wait_ge(z3_ready, n + c + 1)
                        pool.sem_inc(hold, 1)
                        for j in range(2):
                            at = 2 * c + j
                            pool.indirect_dma_start(
                                out=xs_d, out_offset=bass.IndirectOffsetOnAxis(ap=ring[:, s, at:at + 1], axis=0),
                                in_=z3[:, 2 * s + c, :], in_offset=None).then_inc(sent[2 * s + c], 16)

                pool.wait_ge(placed, 1)
                for s in range(2):
                    send(0, s)
                with pool.Fori(1, LH) as i:
                    for s in range(2):
                        send(i, s)
                send(LH, 0, 1)
                for c in range(4):
                    pool.wait_ge(sent[c], 32 * (LH + (c == 0)))

        c5 = ExitStack()
        with c5:
            sb, ps, sem = tools(c5, "b5")
            xs = sb("xs", [P, 2, 2, C])
            xeT = sb("xeT", [P, 2, KC, TILE_TOKENS])
            hT = sb("hT", [P, 2, HB, TILE_TOKENS])
            ys = sb("ys", [P, 2, 2, C])
            bank = [ps(f"bank{n}", [P, 512]) for n in range(8)]
            xs_in = [sem(f"xs_in{n}") for n in range(2)]
            up_in = [sem(f"up_in{n}") for n in range(2)]
            down_in = [sem(f"down_in{n}") for n in range(2)]
            xsT_mm = sem("xsT_mm")
            xeT_ready = sem("xeT_ready")
            up_mm = sem("up_mm")
            gelu = sem("gelu")
            y_mm = sem("y_mm")
            y_half = sem("y_half")
            y_out = [sem(f"y_out{n}") for n in range(2)]
            block = c5.enter_context(nc.Block())
            rows_at = lambda d, t: d[bass.ds(t * TILE_TOKENS, TILE_TOKENS), :].rearrange("(t p) c -> p t c", p=P)
            HALF = ETILES // 2

            @block.sync
            def _(sp):
                def load_rows(t, s):
                    at_least(sp, xsT_mm, t - 1)
                    sp.dma_start(xs[:, s], rows_at(xs_d, t)).then_inc(xs_in[s], 16)

                def store(t, s):
                    sp.wait_ge(y_half, 2 * t + 2)
                    sp.dma_start(rows_at(ys_d, t), ys[:, s]).then_inc(y_out[s], 16)

                def ahead(t, s):
                    load_rows(t + 2, s)
                    e = expert_of(t + 2)
                    sp.wait_ge(gelu, t * HB + HB)
                    load_up(sp, e, s, up_in[s])
                    sp.wait_ge(y_half, 2 * t + 2)
                    load_down(sp, e, s, down_in[s])
                    store(t, s)

                for t in range(2):
                    load_rows(t, t)
                with sp.Fori(0, HALF - 1) as i:
                    for s in range(2):
                        ahead(2 * i + s, s)
                for s in range(2):
                    store(ETILES - 2 + s, s)
                for s in range(2):
                    sp.wait_ge(y_out[s], 16 * HALF)

            @block.tensor
            def _(pe):
                def turn(i, s):
                    t, h = 2 * i + s, s % 2
                    pe.wait_ge(xs_in[h], (i + s // 2) * 16 + 16)
                    at_least(pe, xeT_ready, 2 * t)
                    for k in range(KC):
                        for j in range(2):
                            mm = pe.transpose(bank[0][:, k * C + j * P:k * C + j * P + P], xs[:, h, j, k * P:k * P + P], ident[:])
                    mm.then_inc(xsT_mm, 1)

                def up(i, s):
                    t = 2 * i + s
                    pe.wait_ge(xeT_ready, 2 * t + 2)
                    at_least(pe, up_in[s], i * 32)
                    for j in range(HB):
                        at_least(pe, gelu, t * HB + j - 3)
                        for k in range(KC):
                            mm = pe.matmul(bank[1 + j % 4][:, 0:TILE_TOKENS], E1[:, s, k, j * P:j * P + P], xeT[:, s, k, :],
                                           start=(k == 0), stop=(k == KC - 1))
                        mm.then_inc(up_mm, 1)

                def down(i, s):
                    t = 2 * i + s
                    at_least(pe, down_in[s], i * 32)
                    for n in range(2):
                        at_least(pe, y_half, 2 * t - 1 + n)
                        for j in range(HB):
                            if n == 0:
                                pe.wait_ge(gelu, t * HB + j + 1)
                            mm = pe.matmul(bank[5 + n][:, 0:C], hT[:, s, j, n * P:n * P + P], E2[:, s, j, :],
                                           start=(j == 0), stop=(j == HB - 1))
                        mm.then_inc(y_mm, 1)

                def lap(i):
                    for s in range(2):
                        up(i, s)
                        turn(i, s + 1)
                        down(i, s)

                turn(0, 0)
                lap(0)
                with pe.Fori(1, HALF - 1) as i:
                    lap(i)
                up(HALF - 1, 0)
                turn(HALF - 1, 1)
                down(HALF - 1, 0)
                up(HALF - 1, 1)
                down(HALF - 1, 1)

            @block.scalar
            def _(a):
                def scale(i, s):
                    t, h = 2 * i + s, s % 2
                    a.wait_ge(xsT_mm, t + 1)
                    at_least(a, up_in[h], (i + s // 2) * 32)
                    for k in range(KC):
                        a.activation(xeT[:, h, k, :], bank[0][:, k * C:k * C + TILE_TOKENS], ACT.Identity,
                                     bias=vec[:, h, KC + k:KC + k + 1], scale=vec[:, h, k:k + 1]).then_inc(xeT_ready, 1)

                def gelus(i, s):
                    t = 2 * i + s
                    for j in range(HB):
                        a.wait_ge(up_mm, t * HB + j + 1)
                        a.activation(hT[:, s, j, :], bank[1 + j % 4][:, 0:TILE_TOKENS], ACT.Gelu,
                                     bias=vec[:, s, 2 * KC + j:2 * KC + j + 1]).then_inc(gelu, 1)

                def lap(i):
                    for s in range(2):
                        gelus(i, s)
                        scale(i, s + 1)

                scale(0, 0)
                lap(0)
                with a.Fori(1, HALF - 1) as i:
                    lap(i)
                gelus(HALF - 1, 0)
                scale(HALF - 1, 1)
                gelus(HALF - 1, 1)

            @block.vector
            def _(v):
                def take(i, s):
                    t = 2 * i + s
                    at_least(v, down_in[s], i * 32)
                    at_least(v, y_out[s], i * 16)
                    for n in range(2):
                        v.wait_ge(y_mm, 2 * t + n + 1)
                        v.tensor_tensor(ys[:, s, n, :], bank[5 + n][:, 0:C], b2e[:, s, :], ALU.add).then_inc(y_half, 1)

                for s in range(2):
                    take(0, s)
                with v.Fori(1, HALF) as i:
                    for s in range(2):
                        take(i, s)

        c6 = ExitStack()
        with c6:
            sb, ps, sem = tools(c6, "b6")
            y1 = sb("y1", [P, 4, 2, C])
            o = sb("o", [P, 4, C])
            ring = sb("ring", [P, 2, 4], I32)
            got = [sem(f"got{n}") for n in range(4)]
            ring_ready = sem("ring_ready")
            hold = sem("hold")
            used = sem("used")
            dve = sem("dve")
            out_done = [sem(f"out_done{n}") for n in range(4)]
            block = c6.enter_context(nc.Block())

            @block.gpsimd
            def _(pool):
                def fetch(i, s, tiles=2):
                    n = 4 * i + 2 * s
                    at_least(pool, used, n + tiles - 4)
                    pool.sem_inc(hold, 1)
                    pool.tensor_copy(ring[:, s, 0:2 * tiles], idx[:, bass.ds(n, tiles), :].rearrange("p n a -> p (n a)"))\
                        .then_inc(ring_ready, 1)
                    pool.wait_ge(ring_ready, 2 * i + s + 1)
                    pool.sem_inc(hold, 1)
                    for c in range(tiles):
                        for j in range(2):
                            at = 2 * c + j
                            pool.indirect_dma_start(
                                out=y1[:, 2 * s + c, j, :], out_offset=None, in_=ys_d,
                                in_offset=bass.IndirectOffsetOnAxis(ap=ring[:, s, at:at + 1], axis=0))\
                                .then_inc(got[2 * s + c], 16)

                for s in range(2):
                    fetch(0, s)
                with pool.Fori(1, LH) as i:
                    for s in range(2):
                        fetch(i, s)
                fetch(LH, 0, 1)

            @block.vector
            def _(v):
                ch = Chain(v, dve)

                def combine(i, c):
                    n = 4 * i + c
                    v.wait_ge(got[c], i * 32 + 32)
                    at_least(v, out_done[c], i * 16)
                    tile = acc[:, bass.ds(n, 1), :].rearrange("p a c -> p (a c)")
                    ch.link(v.scalar_tensor_tensor(o[:, c], y1[:, c, 0], wgt[:, 0, bass.ds(n, 1)], tile, ALU.mult, ALU.add))
                    v.scalar_tensor_tensor(o[:, c], y1[:, c, 1], wgt[:, 1, bass.ds(n, 1)], o[:, c], ALU.mult, ALU.add)\
                     .then_inc(used, 1)

                for c in range(4):
                    combine(0, c)
                with v.Fori(1, LH) as i:
                    ch.enter(i - 1, 4)
                    for c in range(4):
                        combine(i, c)
                    ch.leave(LH - 1)
                combine(LH, 0)

            @block.sync
            def _(sp):
                def store(i, c):
                    n = 4 * i + c
                    sp.wait_ge(used, n + 1)
                    sp.dma_start(out[bass.ds(n * P, P), :], o[:, c]).then_inc(out_done[c], 16)

                with sp.Fori(0, LH) as i:
                    for c in range(4):
                        store(i, c)
                store(LH, 0)
                for c in range(4):
                    sp.wait_ge(out_done[c], 16 * (LH + (c == 0)))


def kernel(x, src, dst, **weights):
    import numpy as np
    from concourse import bacc
    from concourse.bass_utils import run_bass_kernel_spmd

    x, src, dst = np.asarray(x), np.asarray(src), np.asarray(dst)
    g = {k: np.asarray(a) for k, a in weights.items()}
    nodes = x.shape[0]
    tiles = -(-nodes // P)
    xp = np.zeros((tiles * P, C), x.dtype)
    xp[:nodes] = x
    ecols = -(-src.shape[0] // P)
    ecols += -ecols % 32
    sp = np.full(ecols * P, tiles * P - 1, src.dtype)
    sp[:src.shape[0]] = src
    dp = np.zeros(ecols * P, dst.dtype)
    dp[:dst.shape[0]] = dst
    T = lambda a: np.ascontiguousarray(a.T)
    col = lambda a: a.reshape(-1, P).T
    row = lambda a: a.reshape(1, -1)
    m = lambda n: g["L0_mix_" + n]
    f = lambda n: g["L0_ffn_" + n]
    arrays = {
        "x": xp, "src": sp.reshape(P, ecols), "dst": dp.reshape(P, ecols),
        "mix_WxT": T(m("Wx")), "mix_Wx": m("Wx"), "mix_WoT": T(m("Wo")), "mix_WqT": T(m("Wq")), "mix_WkT": T(m("Wk")),
        "mix_Wv": m("Wv"), "mix_W1T": T(m("W1")), "mix_W2T": T(m("W2")),
        "gnn_W1T": T(g["L0_gnn_W1"]), "gnn_W2": g["L0_gnn_W2"],
        "cols": np.concatenate([col(a) for a in (m("ln1_w"), m("ln1_b"), m("bx"), m("ln2_w"), m("ln2_b"), m("b1"),
                                                 g["L0_gnn_b1"])], axis=1),
        "mix_bx": row(m("bx")), "gnn_b2": row(g["L0_gnn_b2"]), "mix_b2": row(m("b2")), "mix_bo": row(m("bo")),
        "ffn_Wr": f("Wr"), "ffn_br": row(f("br")),
        "ffn_W1": f("W1").reshape(-1, f("W1").shape[2]), "ffn_W2": f("W2").reshape(-1, C),
        "ffn_vec": np.concatenate([f(n).reshape(EXPERTS, -1, P).transpose(0, 2, 1) for n in ("ln_g", "ln_b", "b1")], axis=2),
        "ffn_b2": f("b2"),
    }
    nc = bacc.Bacc("TRN2", target_bir_lowering=False, num_devices=1)
    aps, maps = {}, {}
    for name, a in arrays.items():
        a = np.ascontiguousarray(a)
        maps[f"in_{name}"] = a
        aps[name] = nc.dram_tensor(f"in_{name}", a.shape, mybir.dt.from_np(a.dtype), kind="ExternalInput").ap()
    out = nc.dram_tensor("out", xp.shape, F32, kind="ExternalOutput").ap()
    gps_layer(nc, aps, out, nodes, ecols)
    r = run_bass_kernel_spmd(nc, [maps], core_ids=[0])
    return r.results[0]["out"][:nodes]
```

```python
from contextlib import ExitStack

import concourse.bass as bass
from concourse import mybir

P = 128
C = 256
KC = C // P
F32 = mybir.dt.float32
F32R = mybir.dt.float32r
I32 = mybir.dt.int32
U32 = mybir.dt.uint32
ALU = mybir.AluOpType
ACT = mybir.ActivationFunctionType
AX = mybir.AxisListType.X
LN_EPS = 1e-5
HEADS, HD = 8, 32
EXPERTS = 8
TILE_TOKENS = 256
RSQRT_SEED = 1597463007.0


class Chain:

    def __init__(self, eng, sem):
        self.eng, self.sem, self.base, self.k, self.i, self.per = eng, sem, 0, 0, None, 0

    def tick(self, ins):
        ins.then_inc(self.sem, 1)
        self.k += 1

    def settle(self, running=0):
        at = self.base + self.k - running
        self.eng.wait_ge(self.sem, at if self.i is None else self.i * self.per + at)

    def link(self, ins, running=0):
        self.tick(ins)
        self.settle(running)

    def enter(self, i, per):
        self.base += self.k
        self.k, self.i, self.per = 0, i, per

    def leave(self, times):
        assert self.k == self.per, (self.k, self.per)
        self.base += times * self.per
        self.k, self.i = 0, None


def at_least(eng, sem, value):
    if not isinstance(value, int) or value > 0:
        eng.wait_ge(sem, value)


def rsqrt(v, link, y, x, t):
    link(v.tensor_scalar(t.bitcast(I32), x.bitcast(I32), 1, None, ALU.logical_shift_right))
    link(v.tensor_scalar(y.bitcast(I32), t.bitcast(I32), -1.0, RSQRT_SEED, ALU.mult, ALU.add))
    for _ in range(3):
        link(v.tensor_tensor(t, y, y, ALU.mult))
        link(v.scalar_tensor_tensor(t, t, -0.5, x, ALU.mult, ALU.mult))
        link(v.scalar_tensor_tensor(y, t, 1.5, y, ALU.add, ALU.mult))


RSQRT_LINKS = 11


def mean_var(v, link, st, mean, var, t):
    link(v.tensor_tensor(mean, st[:, :, 1], st[:, :, 4], ALU.add))
    link(v.tensor_scalar(mean, mean, 0.5, None, ALU.mult))
    link(v.tensor_tensor(t, st[:, :, 1], st[:, :, 4], ALU.subtract))
    link(v.tensor_tensor(t, t, t, ALU.mult))
    link(v.tensor_tensor(var, st[:, :, 2], st[:, :, 5], ALU.add))
    link(v.tensor_scalar(var, var, 1.0 / C, None, ALU.mult))
    link(v.scalar_tensor_tensor(var, t, 0.25, var, ALU.mult, ALU.add))


MEAN_VAR_LINKS = 7


def double_norm(v, link, var, rstd, rstd2, a, t):
    link(v.tensor_scalar(a, var, LN_EPS, None, ALU.add))
    rsqrt(v, link, rstd, a, t)
    link(v.tensor_tensor(a, rstd, rstd, ALU.mult))
    link(v.tensor_tensor(a, a, var, ALU.mult))
    link(v.tensor_scalar(a, a, LN_EPS, None, ALU.add))
    rsqrt(v, link, rstd2, a, t)
    link(v.tensor_tensor(rstd2, rstd2, rstd, ALU.mult))


def count_keys(v, ch, key, masks, ids, counts, n, steps):
    with v.Fori(0, n // steps) as i:
        ch.enter(i, steps)
        for j in range(steps):
            b = bass.ds(i * steps + j, 1)
            ch.link(v.tensor_scalar(masks[j % 2], key, ids[:, b], 0.0, ALU.is_equal, ALU.add, accum_out=counts[:, b]),
                    running=0 if j == steps - 1 else 1)
        ch.leave(n // steps)


def bucket_starts(v, ch, base_total, n, align, cum, size, off, t_int, ones_row):
    shift = align.bit_length() - 1
    link = ch.link
    link(v.tensor_scalar(size, base_total[:, n:2 * n], float(align - 1), None, ALU.add))
    link(v.tensor_copy(t_int, size))
    link(v.tensor_scalar(t_int, t_int, shift, None, ALU.logical_shift_right))
    link(v.tensor_copy(size, t_int))
    link(v.tensor_tensor_scan(cum, ones_row, size, 0.0, ALU.mult, ALU.add))
    link(v.tensor_tensor(off, cum, size, ALU.subtract))
    link(v.scalar_tensor_tensor(off, off, float(align), base_total[:, 0:n], ALU.mult, ALU.add))


def place_keys(v, ch, key, masks, scans, pos, ids, off, n, steps, hold, more=False):
    with v.Fori(0, n // steps) as i:
        ch.enter(i, (4 if more else 3) * steps)
        at = lambda j: bass.ds(i * steps + j, 1)
        match = lambda j: v.tensor_scalar(masks[j % 2], key, ids[:, at(j)], None, ALU.is_equal)

        def go_on(j, running):
            v.sem_inc(hold, 1)
            ch.link(v.tensor_copy(off[:, at(j)], scans[j % 2][:, key.shape[1] - 1:key.shape[1]]), running)

        ch.link(match(0))
        for j in range(steps):
            ch.link(v.tensor_tensor_scan(scans[j % 2], masks[j % 2], masks[j % 2], off[:, at(j)], ALU.add, ALU.max), 1)
            if more and j:
                go_on(j - 1, 1)
            if j < steps - 1:
                ch.link(match(j + 1), 1)
            else:
                ch.settle()
            v.sem_inc(hold, 1)
            ch.link(v.copy_predicated(pos, masks[j % 2].bitcast(I32), scans[j % 2]), 1)
        if more:
            go_on(steps - 1, 0)
        else:
            ch.settle()
        ch.leave(n // steps)


def tile_owner(v, ch, cum, n, unit_ids, ge, owner, owner_int, cols):
    link = ch.link
    link(v.tensor_tensor(ge, unit_ids.unsqueeze(2).broadcast_to([P, cols, n]),
                         cum.unsqueeze(1).broadcast_to([P, cols, n]), ALU.is_ge))
    link(v.tensor_reduce(owner, ge, AX, ALU.add))
    link(v.tensor_scalar(owner, owner, float(n - 1), None, ALU.min))
    link(v.tensor_copy(owner_int, owner))


def gps_layer(nc, w, out, NODES, ECOLS):
    NT = w["x"].shape[0] // P
    LAST = NODES - (NT - 1) * P
    PAIRS = NT // 2
    assert NT == 2 * PAIRS + 1 and PAIRS % 2 == 0 and NT % 7 == 0
    NCH = (ECOLS * P + NT * (P - 1)) // P
    NCH += -NCH % 16
    NCHP = NCH + 16
    CCOLS = -(-NCH // P)
    SCAT = 32
    assert ECOLS % SCAT == 0
    ACOLS = 2 * NT
    ETILES = (ACOLS * P + EXPERTS * (TILE_TOKENS - 1)) // TILE_TOKENS
    ETILES += ETILES % 2
    assert ETILES <= P
    HID = w["mix_W1T"].shape[1]
    HB = HID // P
    GH = w["gnn_W2"].shape[0] // P
    QK = 2 * C
    INV_P = 1.0 / P

    def dram(name, shape, dt=F32):
        return nc.dram_tensor(name, shape, dt, kind="Internal").ap()

    xn_d = dram("xn_d", (NT * P, C))
    q_d = dram("q_d", (NT * P, C))
    k_d = dram("k_d", (NT * P, C))
    xm_d = dram("xm_d", (NT * P, C))
    part_d = dram("part_d", (NT * P, C))
    elist_d = dram("elist_d", (P * NCH, 1), I32)
    chunk_d = dram("chunk_d", (CCOLS * P, 1), I32)
    etile_d = dram("etile_d", (P, 1), I32)
    xs_d = dram("xs_d", (ETILES * TILE_TOKENS, C))
    ys_d = dram("ys_d", (ETILES * TILE_TOKENS, C))

    outer = ExitStack()
    with outer:
        def tools(ctx, tag):
            sb = lambda name, shape, dt=F32: ctx.enter_context(nc.sbuf_tensor(f"{tag}_{name}", shape, dt))
            ps = lambda name, shape: ctx.enter_context(nc.psum_tensor(f"{tag}_{name}", shape, F32))
            sem = lambda name: ctx.enter_context(nc.semaphore(f"{tag}_{name}"))
            return sb, ps, sem

        sb, _, _ = tools(outer, "g")
        ident = sb("ident", [P, P])
        ones = sb("ones", [P, P])
        tri = sb("tri", [P, P])
        iota_b = sb("iota_b", [P, max(P, NT)])
        ids = iota_b[:, 0:NT]
        node_ids = iota_b[:, 0:P]
        unit_ids = sb("unit_ids", [P, CCOLS])
        part_ids = sb("part_ids", [P, 1])
        W12 = sb("W12", [P, KC, C])
        stat_mean = sb("mean", [P, NT])
        stat_a = sb("stat_a", [P, NT])
        stat_b = sb("stat_b", [P, NT])
        stats = sb("stats", [P, NT, 6])
        var = sb("var", [P, NT])
        rstd = sb("rstd", [P, NT])
        rstd2 = sb("rstd2", [P, NT])
        WR = sb("WR", [P, KC, EXPERTS])
        br = sb("br", [1, EXPERTS])
        brb = sb("brb", [P, EXPERTS])
        chunk_owner = sb("chunk_owner", [P, CCOLS], I32)
        hold = outer.enter_context(nc.semaphore("hold"))
        acc = sb("acc", [P, NT, C])

        mixctx = ExitStack()
        with mixctx:
            sb, _, _ = tools(mixctx, "m")
            RA = sb("RA", [P, KC, 3 * C])
            RB = sb("RB", [1, QK])
            RBb = sb("RBb", [P, QK])
            bob = sb("bob", [P, C])
            bsumb = sb("bsumb", [P, C])
            G = sb("G", [P, KC, C])
            M = sb("M", [P, KC, C])
            bo = sb("bo", [1, C])
            bsum = sb("bsum", [1, C])
            W1f = sb("W1f", [P, KC, HID])
            b1f = sb("b1f", [P, HB])
            W2 = sb("W2", [P, HB, C])
            addr = sb("addr", [P, ECOLS], I32)
            rec = sb("rec", [P, ECOLS], I32)

            c1 = ExitStack()
            with c1:
                sb, ps, sem = tools(c1, "b1")
                groups = sb("groups", [P, 2 * 2 * 7 * C])
                g4 = groups[:].rearrange("p (a b t c) -> p a b t c", a=2, b=2, t=7)
                xg, xg2 = g4[:, 0], g4[:, 1]
                work = sb("work", [P, max(5 * ECOLS, 8 * C)])
                cut = lambda buf, at, width: buf[:, at:at + width]
                key, mask, scan, pos = (cut(work, n * ECOLS, ECOLS) for n in range(4))
                src = cut(work, 4 * ECOLS, ECOLS).bitcast(I32)
                mask2, scan2 = (cut(groups, 2 * 7 * C + n * ECOLS, ECOLS) for n in range(2))
                assert 2 * ECOLS <= 2 * 7 * C and NCH <= 4 * C
                posi = src
                counts = sb("counts", [P, NT])
                size = sb("size", [P, NT])
                cum = sb("cum", [P, NT])
                off = sb("off", [P, NT])
                t_int = sb("t_int", [P, NT], I32)
                ge = sb("ge", [P, CCOLS, NT])
                own_f = sb("own_f", [P, CCOLS])
                WxT = sb("WxT", [P, KC, C])
                Wx = sb("Wx", [P, KC, C])
                BD = sb("BD", [P, KC, QK])
                WvBD = sb("WvBD", [P, KC, C])
                WoT = sb("WoT", [P, KC, C])
                gW1T = sb("gW1T", [P, GH, C])
                gW2 = sb("gW2", [P, GH, C])
                cols = sb("cols", [P, 5 * KC + HB + GH])
                ln1w, ln1b, bxc, ln2w, ln2b = (cols[:, KC * n:KC * n + KC] for n in range(5))
                b1c = cols[:, 5 * KC:5 * KC + HB]
                gb1c = cols[:, 5 * KC + HB:]
                rows = sb("rows", [1, 3 * C])
                bxp = sb("bxp", [P, KC])
                xt = sb("xt", [P, 4, C])
                fill = xt[:].rearrange("p a c -> p (a c)")[:, 0:NCH].bitcast(I32)
                z = sb("z", [P, 2, C])
                zT = sb("zT", [P, 2, C])
                q = sb("q", [P, 2, C])
                lg = sb("lg", [P, 2, QK])
                xm = sb("xm", [P, 2, C])
                mx = sb("mx", [P, HEADS])
                sx = sb("sx", [P, HEADS])
                kmax = sb("kmax", [P, C])
                kmax_c = sb("kmax_c", [P, KC])
                diag = sb("diag", [P, KC, P])
                kmax_b = sb("kmax_b", [P, C])
                ksum = cut(work, 0, 8 * C).rearrange("p (g c) -> p g c", c=C)
                KVm = sb("KVm", [P, KC, P])
                hmask = sb("hmask", [P, P])
                rden = sb("rden", [P, KC])
                qx, xp, h = (cut(groups, n * 4 * C, 4 * C).rearrange("p (s t c) -> p s t c", s=2, t=2) for n in range(3))
                z2, part, qT, z2T = (cut(groups, (12 + 2 * n) * C, 2 * C).rearrange("p (k c) -> p k c", k=2) for n in range(4))
                hT = cut(groups, 20 * C, HB * C).rearrange("p (j c) -> p j c", j=HB)
                pst = sb("pst", [P, 2, 6])
                pm, pv, pr, pa, pb = (sb(f"pair{n}", [P, 2]) for n in range(5))
                half = SCAT // 2
                ring_a = sb("ring_a", [P, 2, half], I32)
                ring_r = sb("ring_r", [P, 2, half], I32)
                bank = [ps(f"bank{n}", [P, 512]) for n in range(8)]
                cnt_ps = bank[2]

                const_done = sem("const_done")
                zero_done = sem("zero_done")
                edges_in = sem("edges_in")
                xg_in = [sem(f"xg_in{n}") for n in range(2)]
                xg_used = sem("xg_used")
                weights_in = sem("weights_in")
                diag_in = sem("diag_in")
                fold_mm = sem("fold_mm")
                fold_out = sem("fold_out")
                scaled = sem("scaled")
                counted = sem("counted")
                summed = sem("summed")
                owners = sem("owners")
                placed = sem("placed")
                stats_ready = sem("stats_ready")
                filled = sem("filled")
                owners_out = sem("owners_out")
                ring_ready = sem("ring_ready")
                sent = [sem(f"sent{n}") for n in range(2)]
                hm = sem("hm")
                x_in = [sem(f"x_in{n}") for n in range(4)]
                z_ready = sem("z_ready")
                xn_ready = sem("xn_ready")
                xn_out = sem("xn_out")
                xm_ready = sem("xm_ready")
                xm_out = [sem(f"xm_out{n}") for n in range(2)]
                zT_mm = sem("zT_mm")
                zT_ready = sem("zT_ready")
                qkx_mm = sem("qkx_mm")
                q_shift = sem("q_shift")
                q_exp = sem("q_exp")
                kx_ready = sem("kx_ready")
                q_ready = sem("q_ready")
                kx_out = [sem(f"kx_out{n}") for n in range(2)]
                q_out = [sem(f"q_out{n}") for n in range(2)]
                kmax_done = sem("kmax_done")
                kT_mm = sem("kT_mm")
                kdiag = sem("kdiag")
                kmax_mm = sem("kmax_mm")
                kx_in = [sem(f"kx_in{n}") for n in range(2)]
                k_sub = sem("k_sub")
                k_exp = sem("k_exp")
                k_sum = sem("k_sum")
                kv_mm = sem("kv_mm")
                den_mm = sem("den_mm")
                kv_ready = sem("kv_ready")
                M_mm = sem("M_mm")
                M_ready = sem("M_ready")
                pair_in = [sem(f"pair_in{n}") for n in range(2)]
                qT_mm = sem("qT_mm")
                qT_ready = sem("qT_ready")
                h_mm = sem("h_mm")
                z2_ready = sem("z2_ready")
                front_done = sem("front_done")
                z2T_mm = sem("z2T_mm")
                z2T_ready = sem("z2T_ready")
                up_mm = sem("up_mm")
                gelu = sem("gelu")
                y_mm = sem("y_mm")
                part_ready = sem("part_ready")
                part_out = sem("part_out")
                dve = sem("dve")
                block = c1.enter_context(nc.Block())

                NG = NT // 7
                FIRST = 128 if ECOLS > 320 else 64
                CONSTS = 9
                FOLDS = 11
                rows_of = lambda d, i, n=1: d[bass.ds(i * P, n * P), :]
                L4 = NT // 4
                L2 = PAIRS // 2

                @block.gpsimd
                def _(pool):
                    pool.memset(ones[:], 1.0).then_inc(const_done, 1)
                    pool.memset(ident[:], 0.0).then_inc(const_done, 1)
                    pool.memset(tri[:], 1.0).then_inc(const_done, 1)
                    pool.wait_ge(const_done, 3)
                    pool.affine_select(out=ident[:], in_=ident[:], compare_op=ALU.not_equal, fill=1.0, base=0,
                                       pattern=[[-1, P]], channel_multiplier=1).then_inc(const_done, 1)
                    pool.affine_select(out=tri[:], in_=tri[:], compare_op=ALU.is_gt, fill=0.0, base=0,
                                       pattern=[[1, P]], channel_multiplier=-1).then_inc(const_done, 1)
                    pool.iota(iota_b[:], [[1, max(P, NT)]], base=0, channel_multiplier=0,
                              allow_small_or_imprecise_dtypes=True).then_inc(const_done, 1)
                    pool.iota(unit_ids[:], [[1, CCOLS]], base=0, channel_multiplier=CCOLS,
                              allow_small_or_imprecise_dtypes=True).then_inc(const_done, 1)
                    pool.iota(part_ids[:], [[1, 1]], base=0, channel_multiplier=1,
                              allow_small_or_imprecise_dtypes=True).then_inc(const_done, 1)
                    pool.memset(fill, P).then_inc(const_done, 1)
                    pool.memset(BD[:], 0.0).then_inc(zero_done, 1)
                    pool.memset(WvBD[:], 0.0).then_inc(zero_done, 1)
                    pool.memset(hmask[:], 0.0).then_inc(hm, 1)
                    pool.wait_ge(hm, 1)
                    for g in range(P // HD):
                        pool.memset(hmask[g * HD:g * HD + HD, g * HD:g * HD + HD], 1.0).then_inc(hm, 1)
                        pool.wait_ge(hm, g + 2)

                    def scatter(i):
                        for s in range(2):
                            at_least(pool, sent[s], i * (16 * half))
                            pool.sem_inc(hold, 1)
                            at = i * SCAT + s * half
                            pool.tensor_copy(ring_a[:, s, :], addr[:, bass.ds(at, half)]).then_inc(ring_ready, 1)
                            pool.tensor_copy(ring_r[:, s, :], rec[:, bass.ds(at, half)]).then_inc(ring_ready, 1)
                            pool.wait_ge(ring_ready, i * 4 + 2 * s + 2)
                            pool.sem_inc(hold, 1)
                            for c in range(half):
                                pool.indirect_dma_start(
                                    out=elist_d, out_offset=bass.IndirectOffsetOnAxis(ap=ring_a[:, s, c:c + 1], axis=0),
                                    in_=ring_r[:, s, c:c + 1], in_offset=None).then_inc(sent[s], 16)

                    pool.wait_ge(filled, 16)
                    pool.wait_ge(placed, 1)
                    scatter(0)
                    with pool.Fori(1, FIRST // SCAT) as i:
                        scatter(i)
                    pool.wait_ge(placed, 2)
                    with pool.Fori(FIRST // SCAT, ECOLS // SCAT) as i:
                        scatter(i)
                    for s in range(2):
                        pool.wait_ge(sent[s], ECOLS // SCAT * 16 * half)

                @block.sync
                def _(sp):
                    sp.dma_start(src, w["src"]).then_inc(edges_in, 16)
                    sp.dma_start(rec[:], w["dst"]).then_inc(edges_in, 16)
                    xgt = w["x"].rearrange("(g t p) c -> g p t c", p=P, t=7)
                    sp.dma_start(xg[:, 0], xgt[0]).then_inc(xg_in[0], 16)
                    sp.dma_start(xg[:, 1], xgt[1]).then_inc(xg_in[1], 16)
                    sp.wait_ge(const_done, CONSTS)
                    sp.dma_start(elist_d.rearrange("(p n) a -> p (n a)", p=P), fill).then_inc(filled, 16)
                    sp.wait_ge(owners, 1)
                    sp.dma_start(chunk_d.rearrange("(p n) a -> p (n a)", p=P), chunk_owner[:]).then_inc(owners_out, 16)
                    for g in range(2, NG):
                        sp.wait_ge(xg_used, g - 1)
                        sp.dma_start(xg[:, g % 2], xgt[g]).then_inc(xg_in[g % 2], 16)

                    sp.wait_ge(filled, 16)
                    def load_x(i, c):
                        n = 4 * i + c
                        at_least(sp, z_ready, n - 3)
                        at_least(sp, xn_ready, n - 3)
                        sp.dma_start(xt[:, c % 4], rows_of(w["x"], n)).then_inc(x_in[c % 4], 16)

                    def store(i, c):
                        n, s = 4 * i + c, c % 2
                        sp.wait_ge(xn_ready, n + 1)
                        sp.dma_start(rows_of(xn_d, n), acc[:, bass.ds(n, 1), :].rearrange("p a c -> p (a c)")).then_inc(xn_out, 16)
                        sp.wait_ge(kx_ready, n + 1)
                        sp.dma_start(rows_of(k_d, n), lg[:, s, C:QK]).then_inc(kx_out[s], 16)
                        sp.wait_ge(xm_ready, n + 1)
                        sp.dma_start(rows_of(xm_d, n), xm[:, s]).then_inc(xm_out[s], 16)

                    def store_q(n, s):
                        sp.wait_ge(q_ready, n + 1)
                        sp.dma_start(rows_of(q_d, n), q[:, s]).then_inc(q_out[s], 16)

                    def lap(i, first=False, last=False):
                        for c in range(4):
                            if not (last and c >= 2):
                                load_x(i, c + 3)
                            store(i, c)
                            if not (first and c == 0):
                                store_q(4 * i + c - 1, (c + 1) % 2)

                    for c in range(3):
                        load_x(0, c)
                    lap(0, first=True)
                    with sp.Fori(1, L4 - 1) as i:
                        lap(i)
                    lap(L4 - 1, last=True)
                    store(L4, 0)
                    store_q(NT - 2, 1)
                    store_q(NT - 1, 0)
                    sp.wait_ge(xn_out, 16 * NT)
                    for s, n in ((0, PAIRS + 1), (1, PAIRS)):
                        sp.wait_ge(kx_out[s], 16 * n)
                        sp.wait_ge(xm_out[s], 16 * n)
                        sp.wait_ge(q_out[s], 16 * n)

                    for g in range(NG):
                        if g >= 2:
                            sp.wait_ge(kv_mm, g - 1)
                            sp.wait_ge(k_sum, g - 1)
                        for dst, d in ((xg, k_d), (xg2, xm_d)):
                            sp.dma_start(dst[:, g % 2], d.rearrange("(g t p) c -> g p t c", p=P, t=7)[g]).then_inc(kx_in[g % 2], 16)

                    def load_pair(n, s, tiles=2):
                        at_least(sp, front_done, n - 1)
                        for dst, d in ((qx, q_d), (xp, w["x"])):
                            sp.dma_start(dst[:, s, 0:tiles, :], d[bass.ds(n * 2 * P, tiles * P), :].rearrange("(t p) c -> p t c", p=P))\
                              .then_inc(pair_in[s], 16)

                    def store_pair(n, tiles=2):
                        sp.wait_ge(part_ready, n + 1)
                        sp.dma_start(part_d[bass.ds(n * 2 * P, tiles * P), :].rearrange("(t p) c -> p t c", p=P), part[:, 0:tiles, :])\
                          .then_inc(part_out, 16)

                    sp.wait_ge(kv_mm, NG)
                    sp.wait_ge(k_sum, NG + 1)
                    load_pair(0, 0)
                    load_pair(1, 1)
                    for n in range(2):
                        load_pair(n + 2, n)
                        store_pair(n)
                    with sp.Fori(1, L2 - 1) as i:
                        for s in range(2):
                            load_pair(2 * i + s + 2, s)
                            store_pair(2 * i + s)
                    load_pair(PAIRS, 0, 1)
                    store_pair(PAIRS - 2)
                    store_pair(PAIRS - 1)
                    store_pair(PAIRS, 1)
                    sp.wait_ge(part_out, 16 * (PAIRS + 1))
                    sp.wait_ge(owners_out, 16)

                @block.vector
                def _(v):
                    ch = Chain(v, dve)
                    link = ch.link
                    v.wait_ge(edges_in, 32)
                    v.wait_ge(const_done, CONSTS)
                    link(v.tensor_scalar(rec[:], rec[:], 8, None, ALU.logical_shift_left))
                    link(v.tensor_scalar(scan.bitcast(I32), src, P - 1, None, ALU.bitwise_and))
                    link(v.tensor_tensor(rec[:], rec[:], scan.bitcast(I32), ALU.bitwise_or))
                    link(v.tensor_scalar(src, src, 7, None, ALU.logical_shift_right))
                    link(v.tensor_copy(key, src))
                    link(v.memset(pos, 0.0))
                    count_keys(v, ch, key, (mask, mask2), ids, counts[:], NT, 7)
                    v.sem_inc(counted, 1)
                    v.wait_ge(summed, 1)
                    bucket_starts(v, ch, cnt_ps, NT, P, cum[:], size[:], off[:], t_int[:], ones[:, 0:NT])
                    tile_owner(v, ch, cum[:], NT, unit_ids[:], ge[:], own_f[:], chunk_owner[:], CCOLS)
                    v.sem_inc(owners, 1)

                    def place(lo, hi, more):
                        c = slice(lo, hi)
                        place_keys(v, ch, key[:, c], (mask[:, c], mask2[:, c]), (scan[:, c], scan2[:, c]), pos[:, c],
                                   ids, off[:], NT, 7, hold, more)
                        link(v.tensor_scalar(pos[:, c], pos[:, c], -1.0, None, ALU.add))
                        link(v.tensor_copy(posi[:, c], pos[:, c]))
                        link(v.tensor_scalar(addr[:, c], posi[:, c], P - 1, None, ALU.bitwise_and))
                        link(v.tensor_scalar(posi[:, c], posi[:, c], 7, None, ALU.logical_shift_right))
                        link(v.tensor_copy(pos[:, c], addr[:, c]))
                        link(v.tensor_copy(scan[:, c], posi[:, c]))
                        link(v.scalar_tensor_tensor(pos[:, c], pos[:, c], float(NCH), scan[:, c], ALU.mult, ALU.add))
                        link(v.tensor_copy(addr[:, c], pos[:, c]))
                        v.sem_inc(placed, 1)

                    place(0, FIRST, True)
                    place(FIRST, ECOLS, False)
                    for g in range(NG):
                        v.wait_ge(xg_in[g % 2], 16 * (g // 2 + 1))
                        for t in range(7):
                            ins = v.bn_stats(stats[:, 7 * g + t, :], xg[:, g % 2, t, :])
                        ins.then_inc(xg_used, 1)
                    v.wait_ge(xg_used, NG)
                    mean_var(v, link, stats, stat_mean[:], var[:], stat_a[:])
                    double_norm(v, link, var[:], rstd[:], rstd2[:], stat_a[:], stat_b[:])
                    link(v.scalar_tensor_tensor(stat_a[:], stat_mean[:], -1.0, rstd[:], ALU.mult, ALU.mult))
                    v.sem_inc(stats_ready, 1)

                    link(v.memset(kmax[:], -3.0e38))
                    v.wait_ge(fold_out, FOLDS)

                    def norm(i, c):
                        n = 4 * i + c
                        v.wait_ge(x_in[c % 4], 16 * (i + c // 4 + 1))
                        at_least(v, zT_mm, n - 1)
                        v.tensor_scalar(z[:, c % 2], xt[:, c % 4], stat_mean[:, bass.ds(n, 1)], rstd2[:, bass.ds(n, 1)],
                                        ALU.subtract, ALU.mult).then_inc(z_ready, 1)

                    by_head = lambda a: a.rearrange("p (h s) -> p h s", s=HD)
                    spread = lambda a: a.unsqueeze(2).broadcast_to([P, HEADS, HD])

                    SOFT = 5

                    def soft(i, c, used=P, first=False, ahead=True):
                        n, s = 4 * i + c, c % 2
                        qn, qp = by_head(q[:, s]), by_head(q[:, 1 - s])
                        if ahead:
                            norm(i, c + 2)
                        v.wait_ge(qkx_mm, n + 1)
                        at_least(v, kx_out[s], 16 * (2 * i + c // 2))
                        ch.tick(v.tensor_tensor(lg[:, s], bank[4 + s][:], RBb[:], ALU.add))
                        if not first:
                            v.wait_ge(q_exp, n)
                            at_least(v, q_ready, n - 1)
                            ch.tick(v.tensor_reduce(sx[:], qp, AX, ALU.add))
                        ch.settle(0 if first else 1)
                        v.sem_inc(kx_ready, 1)
                        ch.tick(v.tensor_reduce(mx[:], by_head(lg[:, s, 0:C]), AX, ALU.max))
                        if not first:
                            ch.settle(1)
                            ch.tick(v.reciprocal(sx[:], sx[:]))
                        ch.settle(0 if first else 1)
                        at_least(v, q_out[s], 16 * (2 * i + c // 2))
                        v.tensor_tensor(qn, by_head(lg[:, s, 0:C]), spread(mx[:]), ALU.subtract).then_inc(q_shift, 1)
                        ch.tick(v.tensor_tensor(kmax[0:used, :], kmax[0:used, :], lg[0:used, s, C:QK], ALU.max))
                        if not first:
                            ch.settle(1)
                            v.tensor_tensor(qp, qp, spread(sx[:]), ALU.mult).then_inc(q_ready, 1)
                            v.wait_ge(q_shift, n + 1)

                    norm(0, 0)
                    norm(0, 1)
                    for c in range(4):
                        soft(0, c, first=c == 0)
                    with v.Fori(1, L4 - 1) as i:
                        ch.enter(i - 1, 4 * SOFT)
                        for c in range(4):
                            soft(i, c)
                        ch.leave(L4 - 2)
                    for c in range(4):
                        soft(L4 - 1, c, ahead=c < 3)
                    soft(L4, 0, LAST, ahead=False)
                    v.wait_ge(q_exp, NT)
                    v.wait_ge(q_ready, NT - 1)
                    link(v.tensor_reduce(sx[:], by_head(q[:, 0]), AX, ALU.add))
                    link(v.reciprocal(sx[:], sx[:]))
                    v.tensor_tensor(by_head(q[:, 0]), by_head(q[:, 0]), spread(sx[:]), ALU.mult).then_inc(q_ready, 1)

                    v.sem_inc(kmax_done, 1)
                    v.wait_ge(kT_mm, 1)
                    for m in range(KC):
                        link(v.tensor_reduce(kmax_c[:, m:m + 1], bank[0][:, m * P:m * P + P], AX, ALU.max))
                    for m in range(KC):
                        link(v.tensor_scalar(diag[:, m], ident[:], kmax_c[:, m:m + 1], None, ALU.mult))
                    v.sem_inc(kdiag, 1)
                    v.wait_ge(kmax_mm, 1)
                    link(v.tensor_copy(kmax_b[:], bank[1][:, 0:C]))

                    def shift_k(g):
                        v.wait_ge(kx_in[g % 2], 32 * (g // 2 + 1))
                        v.tensor_tensor(xg[:, g % 2], xg[:, g % 2], kmax_b[:].unsqueeze(1).broadcast_to([P, 7, C]),
                                        ALU.subtract).then_inc(k_sub, 1)

                    def sum_k(g, tiles):
                        v.wait_ge(k_exp, g + 1)
                        v.tensor_reduce(ksum[:, g], xg[:, g % 2, 0:tiles].rearrange("p t c -> p c t"), AX, ALU.add)\
                         .then_inc(k_sum, 1)

                    shift_k(0)
                    for g in range(NG - 1):
                        shift_k(g + 1)
                        sum_k(g, 7)
                    sum_k(NG - 1, 6)
                    v.wait_ge(k_sum, NG)
                    last = ksum[0:LAST, NG - 1]
                    link(v.tensor_tensor(last, last, xg[0:LAST, (NG - 1) % 2, 6], ALU.add))
                    link(v.tensor_reduce(kmax_b[:], ksum[:, 0:NG].rearrange("p g c -> p c g"), AX, ALU.add))
                    v.sem_inc(k_sum, 1)
                    v.wait_ge(den_mm, 1)
                    v.wait_ge(hm, 1 + P // HD)
                    for m in range(KC):
                        link(v.tensor_copy(diag[:, m], bank[3][:, m * P:m * P + P]))
                        link(v.scalar_tensor_tensor(KVm[:, m], diag[:, m], bxp[:, m:m + 1], bank[m][:, 0:P], ALU.mult, ALU.add))
                        link(v.tensor_tensor(KVm[:, m], KVm[:, m], hmask[:], ALU.mult))
                        link(v.reciprocal(rden[:, m:m + 1], bank[2][:, m:m + 1]))
                    v.sem_inc(kv_ready, 1)
                    for m in range(KC):
                        v.wait_ge(M_mm, m + 1)
                        link(v.tensor_scalar(M[:, m, :], bank[4 + m][:, 0:C], rden[:, m:m + 1], None, ALU.mult))
                    v.sem_inc(M_ready, 1)

                    v.wait_ge(xn_ready, NT)

                    def front(n, s, laps, nt=2):
                        v.wait_ge(h_mm, n + 1)
                        v.wait_ge(pair_in[s], 32 * laps)
                        hs = h[:, s, 0:nt]
                        flat = lambda a: a.rearrange("p t c -> p (t c)")
                        link(v.tensor_tensor(flat(hs), bank[1][:, 0:nt * C], flat(acc[:, bass.ds(2 * n, nt), :]), ALU.add))
                        link(v.tensor_tensor(hs, hs, bob[:].unsqueeze(1).broadcast_to([P, nt, C]), ALU.add))
                        for t in range(2):
                            link(v.bn_stats(pst[:, t, :], h[:, s, t % nt, :]))
                        mean_var(v, link, pst, pm[:], pv[:], pa[:])
                        link(v.tensor_scalar(pa[:], pv[:], LN_EPS, None, ALU.add))
                        rsqrt(v, link, pr[:], pa[:], pb[:])
                        for t in range(2):
                            link(v.tensor_scalar(z2[:, t % nt], h[:, s, t % nt], pm[:, t:t + 1], pr[:, t:t + 1],
                                                 ALU.subtract, ALU.mult))
                        v.sem_inc(z2_ready, 1)
                        link(v.tensor_tensor(flat(hs), flat(hs), flat(xp[:, s, 0:nt]), ALU.add))
                        v.sem_inc(front_done, 1)
                        link(v.tensor_tensor(hs, hs, bsumb[:].unsqueeze(1).broadcast_to([P, nt, C]), ALU.add))

                    def back(n, s, nt=2):
                        v.wait_ge(y_mm, n + 1)
                        at_least(v, part_out, n * 16)
                        v.tensor_tensor(part[:, 0:nt].rearrange("p t c -> p (t c)"), bank[7][:, 0:nt * C],
                                        h[:, s, 0:nt].rearrange("p t c -> p (t c)"), ALU.add).then_inc(part_ready, 1)
                        v.wait_ge(part_ready, n + 1)

                    per = 2 + 2 + MEAN_VAR_LINKS + 1 + RSQRT_LINKS + 2 + 2

                    def lap2(i):
                        front(2 * i + 1, 1, i + 1)
                        back(2 * i, 0)
                        front(2 * i + 2, 0, i + 2)
                        back(2 * i + 1, 1)

                    front(0, 0, 1)
                    lap2(0)
                    with v.Fori(1, L2 - 1) as i:
                        ch.enter(i - 1, 2 * per)
                        lap2(i)
                        ch.leave(L2 - 2)
                    front(PAIRS - 1, 1, L2)
                    back(PAIRS - 2, 0)
                    front(PAIRS, 0, L2 + 1, 1)
                    back(PAIRS - 1, 1)
                    back(PAIRS, 0, 1)

                @block.scalar
                def _(a):
                    for dst, name in ((WxT, "mix_WxT"), (Wx, "mix_Wx"), (WoT, "mix_WoT"), (gW1T, "gnn_W1T"),
                                      (gW2, "gnn_W2"), (W1f, "mix_W1T"), (W2, "mix_W2T"), (WR, "ffn_Wr")):
                        a.dma_start(dst[:], w[name].rearrange("(k p) c -> p k c", p=P)).then_inc(weights_in, 16)
                    a.dma_start(cols[:], w["cols"]).then_inc(weights_in, 16)
                    for dst, name in ((rows[0:1, 0:C], "mix_bx"), (rows[0:1, C:2 * C], "gnn_b2"),
                                      (rows[0:1, 2 * C:3 * C], "mix_b2"), (bo[:], "mix_bo"), (br[:], "ffn_br")):
                        a.dma_start(dst, w[name]).then_inc(weights_in, 16)
                    a.wait_ge(zero_done, 2)
                    for hd in range(HEADS):
                        r, k = hd * HD % P, hd * HD // P
                        for dst, at, name in ((BD, 0, "mix_WqT"), (BD, C, "mix_WkT"), (WvBD, 0, "mix_Wv")):
                            a.dma_start(dst[r:r + HD, k, at + hd * HD:at + hd * HD + HD], w[name]).then_inc(diag_in, 16)
                    a.wait_ge(weights_in, 14 * 16)

                    def take(n, out_, f):
                        a.wait_ge(fold_mm, n + 1)
                        a.activation(out_, f, ACT.Copy).then_inc(fold_out, 1)

                    for m in range(KC):
                        a.wait_ge(fold_mm, m + 1)
                        a.activation(RA[:, m, 0:QK], bank[m][:, 0:QK], ACT.Identity, scale=ln1w[:, m:m + 1]).then_inc(fold_out, 1)
                    for m in range(KC):
                        a.activation(RA[:, m, QK:], WxT[:, m, :], ACT.Identity, scale=ln1w[:, m:m + 1]).then_inc(scaled, 1)
                    take(2, bxp[:], bank[0][:, 0:KC])
                    take(3, RB[0:1, 0:QK], bank[1][0:1, 0:QK])
                    take(4, bsum[:], bank[0][0:1, 0:C])
                    take(5, G[:].rearrange("p k c -> p (k c)"), bank[1][:, 0:KC * C])
                    take(6, W12[:].rearrange("p k c -> p (k c)"), bank[0][:, 0:KC * C])
                    take(7, b1f[:], bank[1][:, 0:HB])
                    for m in range(KC):
                        a.activation(W1f[:, m, :], W1f[:, m, :], ACT.Identity, scale=ln2w[:, m:m + 1]).then_inc(scaled, 1)
                    take(8, RBb[:], bank[0][:, 0:QK])
                    take(9, bob[:], bank[1][:, 0:C])
                    take(10, brb[:], bank[0][:, C:C + EXPERTS])
                    a.activation(bsumb[:], bank[0][:, 0:C], ACT.Copy).then_inc(scaled, 1)
                    a.wait_ge(stats_ready, 1)

                    def turn(i, c):
                        n, s = 4 * i + c, c % 2
                        a.wait_ge(zT_mm, n + 1)
                        at_least(a, qkx_mm, n - 1)
                        a.activation(zT[:, s], bank[s][:, 0:C], ACT.Copy).then_inc(zT_ready, 1)
                        a.wait_ge(x_in[c % 4], 16 * (i + c // 4 + 1))
                        a.activation(acc[:, bass.ds(n, 1), :].rearrange("p a c -> p (a c)"), xt[:, c % 4], ACT.Identity, bias=stat_a[:, bass.ds(n, 1)],
                                     scale=rstd[:, bass.ds(n, 1)]).then_inc(xn_ready, 1)

                    def exp_q(i, c):
                        s = c % 2
                        a.wait_ge(qkx_mm, 4 * i + c + 1)
                        at_least(a, xm_out[s], 16 * (2 * i + c // 2))
                        a.activation(xm[:, s], bank[6 + s][:, 0:C], ACT.Copy).then_inc(xm_ready, 1)
                        a.wait_ge(q_shift, 4 * i + c + 1)
                        a.activation(q[:, c % 2], q[:, c % 2], ACT.Exp).then_inc(q_exp, 1)

                    def lap(i):
                        for c in range(4):
                            turn(i, c + 1)
                            exp_q(i, c)

                    turn(0, 0)
                    lap(0)
                    with a.Fori(1, L4) as i:
                        lap(i)
                    exp_q(L4, 0)

                    for g in range(NG):
                        a.wait_ge(k_sub, g + 1)
                        a.activation(xg[:, g % 2], xg[:, g % 2], ACT.Exp).then_inc(k_exp, 1)

                    def copy_q(n, nt=2):
                        a.wait_ge(qT_mm, n + 1)
                        at_least(a, h_mm, n)
                        a.activation(qT[:, :, 0:nt * P], bank[0][:, 0:KC * nt * P].rearrange("p (k c) -> p k c", k=KC),
                                     ACT.Copy).then_inc(qT_ready, 1)

                    def copy_z(n, nt=2):
                        a.wait_ge(z2T_mm, n + 1)
                        a.activation(z2T[:, :, 0:nt * P], bank[2][:, 0:KC * nt * P].rearrange("p (k c) -> p k c", k=KC),
                                     ACT.Copy).then_inc(z2T_ready, 1)

                    def gelus(n, nt=2):
                        at_least(a, y_mm, n)
                        for j in range(HB):
                            a.wait_ge(up_mm, n * HB + j + 1)
                            a.activation(hT[:, j, 0:nt * P], bank[3 + j % 4][:, 0:nt * P], ACT.Gelu, bias=b1f[:, j:j + 1])\
                             .then_inc(gelu, 1)

                    def lap1(n, nt=2):
                        copy_q(n + 1, nt)
                        gelus(n)
                        copy_z(n + 1, nt)

                    copy_q(0)
                    copy_z(0)
                    lap1(0)
                    with a.Fori(1, PAIRS - 1) as n:
                        lap1(n)
                    lap1(PAIRS - 1, 1)
                    gelus(PAIRS, 1)

                @block.tensor
                def _(pe):
                    pe.wait_ge(weights_in, 14 * 16)
                    pe.wait_ge(diag_in, 3 * HEADS * 16)
                    pe.wait_ge(const_done, CONSTS)

                    def room(n):
                        if n >= 2:
                            pe.wait_ge(fold_out, n - 1)
                        return bank[n % 2]

                    for m in range(KC):
                        f = room(m)
                        for k in range(KC):
                            mm = pe.matmul(f[:, 0:QK], Wx[:, k, m * P:m * P + P], BD[:, k, :], start=(k == 0), stop=(k == KC - 1))
                        mm.then_inc(fold_mm, 1)
                    f = room(2)
                    pe.matmul(f[:, 0:KC], ident[:], bxc, start=True, stop=False)
                    for m in range(KC):
                        for k in range(KC):
                            mm = pe.matmul(f[:, m:m + 1], WxT[:, k, m * P:m * P + P], ln1b[:, k:k + 1],
                                           start=False, stop=(m == KC - 1 and k == KC - 1))
                    mm.then_inc(fold_mm, 1)
                    f = room(3)
                    pe.wait_ge(fold_out, 3)
                    for k in range(KC):
                        mm = pe.matmul(f[0:1, 0:QK], bxp[:, k:k + 1], BD[:, k, :], start=(k == 0), stop=(k == KC - 1))
                    mm.then_inc(fold_mm, 1)
                    f = room(4)
                    pe.matmul(f[0:1, 0:C], ones[0:1, 0:1], rows[0:1, C:2 * C], start=True, stop=False)
                    pe.matmul(f[0:1, 0:C], ones[0:1, 0:1], rows[0:1, 2 * C:3 * C], start=False, stop=False)
                    for k in range(GH):
                        mm = pe.matmul(f[0:1, 0:C], gb1c[:, k:k + 1], gW2[:, k, :], start=False, stop=(k == GH - 1))
                    mm.then_inc(fold_mm, 1)
                    f = room(5)
                    for m in range(KC):
                        for k in range(KC):
                            mm = pe.matmul(f[:, m * C:m * C + C], WvBD[:, k, m * P:m * P + P], WoT[:, k, :],
                                           start=(k == 0), stop=(k == KC - 1))
                    mm.then_inc(fold_mm, 1)
                    f = room(6)
                    for m in range(KC):
                        for k in range(GH):
                            mm = pe.matmul(f[:, m * C:m * C + C], gW1T[:, k, m * P:m * P + P], gW2[:, k, :],
                                           start=(k == 0), stop=(k == GH - 1))
                    mm.then_inc(fold_mm, 1)
                    f = room(7)
                    pe.matmul(f[:, 0:HB], ident[:], b1c, start=True, stop=False)
                    for j in range(HB):
                        for k in range(KC):
                            mm = pe.matmul(f[:, j:j + 1], W1f[:, k, j * P:j * P + P], ln2b[:, k:k + 1],
                                           start=False, stop=(j == HB - 1 and k == KC - 1))
                    mm.then_inc(fold_mm, 1)
                    f = room(8)
                    pe.matmul(f[:, 0:QK], ones[0:1, :], RB[0:1, 0:QK], start=True, stop=True).then_inc(fold_mm, 1)
                    f = room(9)
                    pe.matmul(f[:, 0:C], ones[0:1, :], bo[:], start=True, stop=True).then_inc(fold_mm, 1)
                    f = room(10)
                    pe.matmul(f[:, 0:C], ones[0:1, :], bsum[:], start=True, stop=True)
                    pe.matmul(f[:, C:C + EXPERTS], ones[0:1, :], br[:], start=True, stop=True).then_inc(fold_mm, 1)
                    pe.wait_ge(counted, 1)
                    pe.matmul(cnt_ps[:, 0:NT], tri[:], counts[:], start=True, stop=True)
                    pe.matmul(cnt_ps[:, NT:2 * NT], ones[:], counts[:], start=True, stop=True).then_inc(summed, 1)
                    pe.wait_ge(fold_out, FOLDS)
                    pe.wait_ge(scaled, 2 * KC + 1)

                    def turn(i, c):
                        n, s = 4 * i + c, c % 2
                        pe.wait_ge(z_ready, n + 1)
                        at_least(pe, zT_ready, n - 1)
                        for k in range(KC):
                            mm = pe.transpose(bank[s][:, k * P:k * P + P], z[:, s, k * P:k * P + P], ident[:])
                        mm.then_inc(zT_mm, 1)

                    def project(i, c):
                        n, s = 4 * i + c, c % 2
                        pe.wait_ge(zT_ready, n + 1)
                        at_least(pe, kx_ready, n - 1)
                        at_least(pe, xm_ready, n - 1)
                        for o, lo, hi in ((4 + s, 0, QK), (6 + s, QK, 3 * C)):
                            for k in range(KC):
                                mm = pe.matmul(bank[o][:, 0:hi - lo], zT[:, s, k * P:k * P + P], RA[:, k, lo:hi],
                                               start=(k == 0), stop=(k == KC - 1))
                        mm.then_inc(qkx_mm, 1)

                    def lap(i):
                        for c in range(4):
                            turn(i, c + 1)
                            project(i, c)

                    turn(0, 0)
                    lap(0)
                    with pe.Fori(1, L4) as i:
                        lap(i)
                    project(L4, 0)

                    pe.wait_ge(kmax_done, 1)
                    for m in range(KC):
                        mm = pe.transpose(bank[0][:, m * P:m * P + P], kmax[:, m * P:m * P + P], ident[:])
                    mm.then_inc(kT_mm, 1)
                    pe.wait_ge(kdiag, 1)
                    for m in range(KC):
                        mm = pe.matmul(bank[1][:, m * P:m * P + P], ones[:], diag[:, m], start=True, stop=True)
                    mm.then_inc(kmax_mm, 1)
                    for g in range(NG):
                        pe.wait_ge(k_exp, g + 1)
                        for t in range(7):
                            n = 7 * g + t
                            used = LAST if n == NT - 1 else P
                            for m in range(KC):
                                mm = pe.matmul(bank[m][:, 0:P], xg2[0:used, g % 2, t, m * P:m * P + P],
                                               xg[0:used, g % 2, t, m * P:m * P + P], start=(n == 0), stop=(n == NT - 1))
                        mm.then_inc(kv_mm, 1)
                    pe.wait_ge(k_sum, NG + 1)
                    for m in range(KC):
                        pe.matmul(bank[3][:, m * P:m * P + P], ones[:], kmax_b[:, m * P:m * P + P], start=True, stop=True)
                    for m in range(KC):
                        mm = pe.matmul(bank[2][:, m:m + 1], kmax_b[:, m * P:m * P + P], ones[:, 0:1], start=True, stop=True)
                    mm.then_inc(den_mm, 1)
                    pe.wait_ge(kv_ready, 1)
                    for m in range(KC):
                        pe.matmul(bank[4 + m][:, 0:C], KVm[:, m], G[:, m, :], start=True, stop=True).then_inc(M_mm, 1)
                    pe.wait_ge(M_ready, 1)

                    def turn_q(n, s, laps, nt=2):
                        pe.wait_ge(pair_in[s], 32 * laps)
                        at_least(pe, qT_ready, n)
                        for k in range(KC):
                            for t in range(nt):
                                mm = pe.transpose(bank[0][:, (k * nt + t) * P:(k * nt + t + 1) * P],
                                                  qx[:, s, t, k * P:k * P + P], ident[:])
                        mm.then_inc(qT_mm, 1)

                    def attend(n, nt=2):
                        pe.wait_ge(qT_ready, n + 1)
                        at_least(pe, z2_ready, n)
                        for t in range(nt):
                            for k in range(KC):
                                mm = pe.matmul(bank[1][:, t * C:t * C + C], qT[:, k, t * P:t * P + P], M[:, k, :],
                                               start=(k == 0), stop=(k == KC - 1))
                        mm.then_inc(h_mm, 1)

                    def turn_z(n, nt=2):
                        pe.wait_ge(z2_ready, n + 1)
                        at_least(pe, z2T_ready, n)
                        for k in range(KC):
                            for t in range(nt):
                                mm = pe.transpose(bank[2][:, (k * nt + t) * P:(k * nt + t + 1) * P],
                                                  z2[:, t, k * P:k * P + P], ident[:])
                        mm.then_inc(z2T_mm, 1)

                    def up(n, nt=2):
                        N = nt * P
                        pe.wait_ge(z2T_ready, n + 1)
                        for j in range(HB):
                            at_least(pe, gelu, n * HB + j - 3)
                            for k in range(KC):
                                mm = pe.matmul(bank[3 + j % 4][:, 0:N], W1f[:, k, j * P:j * P + P], z2T[:, k, 0:N],
                                               start=(k == 0), stop=(k == KC - 1))
                            mm.then_inc(up_mm, 1)

                    def down(n, nt=2):
                        pe.wait_ge(gelu, n * HB + HB)
                        at_least(pe, part_ready, n)
                        for t in range(nt):
                            for j in range(HB):
                                mm = pe.matmul(bank[7][:, t * C:t * C + C], hT[:, j, t * P:t * P + P], W2[:, j, :],
                                               start=(j == 0), stop=(j == HB - 1))
                        mm.then_inc(y_mm, 1)

                    def lap1(n, s, laps, nt=2):
                        turn_q(n + 1, s, laps, nt)
                        up(n)
                        attend(n + 1, nt)
                        down(n)
                        turn_z(n + 1, nt)

                    turn_q(0, 0, 1)
                    attend(0)
                    turn_z(0)
                    lap1(0, 1, 1)
                    lap1(1, 0, 2)
                    with pe.Fori(1, L2 - 1) as i:
                        lap1(2 * i, 1, i + 1)
                        lap1(2 * i + 1, 0, i + 2)
                    lap1(PAIRS - 2, 1, L2)
                    lap1(PAIRS - 1, 0, L2 + 1, 1)
                    up(PAIRS, 1)
                    down(PAIRS, 1)

        sb, _, _ = tools(outer, "r")
        idx = sb("idx", [P, NT, 2], I32)
        wgt = sb("wgt", [P, 2, NT])
        key2 = sb("key2", [P, ACOLS])
        owner_row = sb("owner_row", [1, P], I32)

        SPLIT = 2 * 2 * KC * (HID + TILE_TOKENS) + HB * TILE_TOKENS
        part_mem = sb("part", [P, max(NT * C, SPLIT)])
        part = part_mem[:, 0:NT * C].rearrange("p (n c) -> p n c", c=C)

        c3 = ExitStack()
        with c3:
            sb, ps, sem = tools(c3, "b3")
            zrow = sb("zrow", [P, 4, C])
            zeroed = sem("zeroed")
            xs_zero = sem("xs_zero")
            part_in = sem("part_in")
            elist = sb("elist", [P, NCHP], I32)
            low = sb("low", [P, NCHP])
            crow = sb("crow", [1, CCOLS * P], I32)
            hot = sb("hot", [P, 2, 8, P])
            src_ring = sb("src_ring", [P, 2, 8], I32)
            rows16 = sb("rows16", [P, 16, C])
            bank = [ps(f"bank{n}", [P, 512]) for n in range(8)]
            list_in = sem("list_in")
            ready = sem("ready")
            gathered = [sem(f"gathered{n}") for n in range(16)]
            free = sem("free")
            added = sem("added")
            dve = sem("dve")
            block = c3.enter_context(nc.Block())

            @block.sync
            def _(sp):
                sp.dma_start(elist[:, 0:NCH], elist_d.rearrange("(p n) a -> p (n a)", p=P)).then_inc(list_in, 16)
                sp.dma_start(crow[:], chunk_d.rearrange("n a -> a n")).then_inc(list_in, 16)
                for g in range(NT // 7):
                    sp.wait_ge(free, 16 + 16 * g + 16)
                    sp.dma_start(part[:, 7 * g:7 * g + 7], part_d.rearrange("(g t p) c -> g p t c", p=P, t=7)[g]).then_inc(part_in, 16)
                sp.wait_ge(zeroed, 1)
                for g in range(0, ETILES, 2):
                    sp.wait_ge(free, 16 + min(NCH, 16 * (NT // 7) + 8 * g))
                    sp.dma_start(xs_d[g * 2 * P:(g + 2) * 2 * P, :].rearrange("(t p) c -> p t c", p=P), zrow[:, 0:4])\
                      .then_inc(xs_zero, 16)
                sp.wait_ge(part_in, 16 * (NT // 7))
                sp.wait_ge(xs_zero, 16 * (ETILES // 2))

            @block.vector
            def _(v):
                ch = Chain(v, dve)
                ch.link(v.memset(elist[:, NCH:], P))
                v.wait_ge(list_in, 32)
                low_i = rows16[:].rearrange("p a b -> p (a b)")[:, 0:NCHP].bitcast(I32)
                ch.link(v.tensor_scalar(low_i, elist[:], 255, None, ALU.bitwise_and))
                ch.link(v.tensor_copy(low[:], low_i))
                ch.link(v.tensor_scalar(elist[:], elist[:], 8, None, ALU.logical_shift_right))

                def prepare(at, s):
                    v.tensor_tensor(hot[:, s], low[:, bass.ds(at, 8)].unsqueeze(2).broadcast_to([P, 8, P]),
                                    node_ids.unsqueeze(1).broadcast_to([P, 8, P]), ALU.is_equal).then_inc(ready, 1)
                    v.tensor_copy(src_ring[:, s], elist[:, bass.ds(at, 8)]).then_inc(ready, 1)

                def add(i, s):
                    _, owner = nc.values_load_multi_w_load_instructions(
                        crow[0:1, bass.ds(i * 16 + s * 8, 8)], engines=[mybir.EngineType.DVE], min_val=0, max_val=NT - 1,
                        skip_runtime_bounds_check_because="the owners were clamped to the last tile")
                    for c in range(8):
                        v.wait_ge(free, i * 16 + s * 8 + c + 17)
                        v.wait_ge(added, i * 16 + s * 8 + c + 8)
                        tile = acc[:, bass.ds(owner[c], 1), :].rearrange("p a c -> p (a c)")
                        v.tensor_tensor(tile, tile, bank[c][:, 0:C], ALU.add).then_inc(added, 1)

                v.sem_inc(added, 8)
                prepare(0, 0)
                v.memset(zrow[:], 0.0).then_inc(zeroed, 1)
                with v.Fori(0, NCH // 16) as i:
                    v.wait_ge(free, i * 16 + 16)
                    prepare(i * 16 + 8, 1)
                    add(i, 0)
                    v.wait_ge(free, i * 16 + 24)
                    prepare(i * 16 + 16, 0)
                    add(i, 1)

            @block.gpsimd
            def _(pool):
                with pool.Fori(0, NCH // 16) as i:
                    for s in range(2):
                        pool.wait_ge(ready, i * 4 + 2 * s + 2)
                        pool.sem_inc(hold, 1)
                        for c in range(8):
                            n = 8 * s + c
                            pool.wait_ge(free, i * 16 + n + 1)
                            pool.sem_inc(hold, 1)
                            pool.indirect_dma_start(
                                out=rows16[:, n, :], out_offset=None, in_=xn_d,
                                in_offset=bass.IndirectOffsetOnAxis(ap=src_ring[:, s, c:c + 1], axis=0))\
                                .then_inc(gathered[n], 16)

            @block.tensor
            def _(pe):
                pe.sem_inc(free, 16)
                with pe.Fori(0, NCH // 16) as i:
                    for s in range(2):
                        pe.wait_ge(ready, i * 4 + 2 * s + 2)
                        for c in range(8):
                            n = 8 * s + c
                            pe.wait_ge(gathered[n], i * 16 + 16)
                            pe.wait_ge(added, i * 16 + n + 1)
                            pe.matmul(bank[c][:, 0:C], hot[:, s, c], rows16[:, n, :], start=True, stop=True).then_inc(free, 1)

        LH = PAIRS // 2
        sb, _, _ = tools(outer, "w")
        E1 = sb("E1", [P, 2, KC, HID])
        E2 = sb("E2", [P, HB, C])
        vec = sb("vec", [P, 2, 2 * KC + HB])
        b2e = sb("b2e", [P, 2, C])
        w1_d = w["ffn_W1"].rearrange("(e k p) h -> e p k h", p=P, k=KC)
        w2_d = w["ffn_W2"].rearrange("(e j p) c -> e p j c", p=P, j=HB)

        def expert_of(t):
            return nc.values_load(owner_row[0:1, bass.ds(t, 1)], engines=[mybir.EngineType.SP],
                                  min_val=0, max_val=EXPERTS - 1,
                                  skip_runtime_bounds_check_because="the owners were clamped to the last expert")

        def load_up(sp, e, s, landed): 
            sp.dma_start(E1[:, s], w1_d[bass.ds(e, 1)].rearrange("a p k h -> p (a k) h")).then_inc(landed, 16)

        def load_down(sp, e, landed):
            sp.dma_start(E2[:], w2_d[bass.ds(e, 1)].rearrange("a p k h -> p (a k) h")).then_inc(landed, 16)

        def load_vectors(sp, e, s, landed):
            sp.dma_start(vec[:, s], w["ffn_vec"][bass.ds(e, 1)].rearrange("a p k -> p (a k)")).then_inc(landed, 16)
            sp.dma_start(b2e[:, s], w["ffn_b2"][bass.ds(e, 1)].broadcast_to([P, C])).then_inc(landed, 16)

        c4 = ExitStack()
        with c4:
            sb, ps, sem = tools(c4, "b4")
            a_s = sb("a_s", [P, 2, C])
            aT = sb("aT", [P, 2, C])
            u = sb("u", [P, 2, C])
            uT = sb("uT", [P, 2, C])
            lg = sb("lg", [P, NT, EXPERTS])
            eq = sb("eq", [P, NT, EXPERTS])
            rev = sb("rev", [P, EXPERTS])
            best = sb("best", [P, 2, NT])
            two = sb("two", [P, 2, 1])
            first = sb("first", [P, NT])
            second = sb("second", [P, NT])
            mask, mask2, scan, scan2 = (sb(f"place{n}", [P, ACOLS]) for n in range(4))
            pos = sb("pos", [P, ACOLS])
            counts, size, cum, off = (sb(f"e{n}", [P, EXPERTS]) for n in range(4))
            t_int = sb("t_int", [P, EXPERTS], I32)
            ge = sb("ge", [P, 1, EXPERTS])
            own_f = sb("own_f", [P, 1])
            own_i = sb("own_i", [P, 1], I32)
            z3 = sb("z3", [P, 4, C])
            ring = sb("ring", [P, 2, 4], I32)
            bank = [ps(f"bank{n}", [P, 512]) for n in range(8)]
            a_ready = sem("a_ready")
            aT_mm = sem("aT_mm")
            aT_ready = sem("aT_ready")
            gnn_mm = sem("gnn_mm")
            x1_ready = sem("x1_ready")
            stat_ok = sem("stat_ok")
            u_ready = sem("u_ready")
            norms_ready = sem("norms_ready")
            uT_mm = sem("uT_mm")
            uT_ready = sem("uT_ready")
            lg_mm = sem("lg_mm")
            lg_ready = sem("lg_ready")
            diff_ready = sem("diff_ready")
            exp_ready = sem("exp_ready")
            counted = sem("counted")
            summed = sem("summed")
            owners = sem("owners")
            own_moved = sem("own_moved")
            ahead = sem("ahead")
            placed = sem("placed")
            z3_ready = sem("z3_ready")
            ring_ready = sem("ring_ready")
            sent = [sem(f"sent{n}") for n in range(4)]
            dve = sem("dve")
            block = c4.enter_context(nc.Block())
            within = lambda n: not isinstance(n, int) or n < NT
            tile_of = lambda n: acc[:, bass.ds(n, 1), :].rearrange("p a c -> p (a c)")

            @block.sync
            def _(sp):
                sp.wait_ge(owners, 1)
                sp.dma_start(etile_d, own_i[:]).then_inc(own_moved, 16)
                sp.wait_ge(own_moved, 16)
                sp.dma_start(owner_row[:], etile_d.rearrange("n a -> a n")).then_inc(own_moved, 16)
                sp.wait_ge(own_moved, 32)
                for t in range(2):
                    e = expert_of(t)
                    load_up(sp, e, t, ahead)
                    load_vectors(sp, e, t, ahead)
                    if t == 0:
                        load_down(sp, e, ahead)
                sp.wait_ge(ahead, 7 * 16)

            @block.tensor
            def _(pe):
                def turn(n, s, ready, emptied, mm_done, from_, to):
                    pe.wait_ge(ready, n + 1)
                    at_least(pe, emptied, n - 1)
                    for k in range(KC):
                        mm = pe.transpose(bank[to + s][:, k * P:k * P + P], from_[:, s, k * P:k * P + P], ident[:])
                    mm.then_inc(mm_done, 1)

                def product(n, s, ready, emptied, mm_done, lhs, rhs, to, width):
                    pe.wait_ge(ready, n + 1)
                    at_least(pe, emptied, n - 1)
                    for k in range(KC):
                        mm = pe.matmul(bank[to + s][:, 0:width], lhs[:, s, k * P:k * P + P], rhs[:, k, :],
                                       start=(k == 0), stop=(k == KC - 1))
                    mm.then_inc(mm_done, 1)

                turn_a, gnn = (a_ready, aT_ready, aT_mm, a_s, 0), (aT_ready, x1_ready, gnn_mm, aT, W12, 2, C)
                turn_u, route = (u_ready, uT_ready, uT_mm, u, 4), (uT_ready, lg_ready, lg_mm, uT, WR, 6, EXPERTS)

                def lap(i):
                    for s in range(2):
                        n = 2 * i + s
                        if within(n + 2):
                            product(n + 2, s, *gnn)
                        turn(n, s, *turn_u)
                        if within(n + 3):
                            turn(n + 3, 1 - s, *turn_a)
                        if not isinstance(n, int) or n > 0:
                            product(n - 1, 1 - s, *route)

                for n in range(2):
                    turn(n, n, *turn_a)
                for n in range(2):
                    product(n, n, *gnn)
                turn(2, 0, *turn_a)
                lap(0)
                with pe.Fori(1, PAIRS - 2) as i:
                    lap(i)
                lap(PAIRS - 2)
                lap(PAIRS - 1)
                turn(NT - 1, 0, *turn_u)
                product(NT - 2, 1, *route)
                product(NT - 1, 0, *route)
                pe.wait_ge(counted, 1)
                pe.matmul(bank[2][:, 0:EXPERTS], tri[:], counts[:], start=True, stop=True)
                pe.matmul(bank[2][:, EXPERTS:2 * EXPERTS], ones[:], counts[:], start=True, stop=True).then_inc(summed, 1)

            @block.scalar
            def _(a):
                def fetch(n, s):
                    at_least(a, aT_mm, n - 1)
                    a.activation(a_s[:, s], tile_of(n), ACT.Copy).then_inc(a_ready, 1)

                def turn(n, s):
                    a.wait_ge(aT_mm, n + 1)
                    at_least(a, gnn_mm, n - 1)
                    a.activation(aT[:, s], bank[s][:, 0:C], ACT.Copy).then_inc(aT_ready, 1)

                def turn_u(n, s):
                    a.wait_ge(uT_mm, n + 1)
                    at_least(a, lg_mm, n - 1)
                    a.activation(uT[:, s], bank[4 + s][:, 0:C], ACT.Copy).then_inc(uT_ready, 1)

                def lap(i):
                    for s in range(2):
                        n = 2 * i + s
                        turn_u(n, s)
                        if within(n + 3):
                            turn(n + 3, 1 - s)
                        if within(n + 4):
                            fetch(n + 4, s)

                fetch(0, 0)
                fetch(1, 1)
                for n in range(3):
                    turn(n, n % 2)
                    if n < 2:
                        fetch(n + 2, n)
                lap(0)
                with a.Fori(1, PAIRS - 2) as i:
                    lap(i)
                lap(PAIRS - 2)
                lap(PAIRS - 1)
                turn_u(NT - 1, 0)
                a.wait_ge(diff_ready, 1)
                a.activation(second[:], second[:], ACT.Exp).then_inc(exp_ready, 1)

                a.wait_ge(norms_ready, 1)

                def rows(i, c):
                    n = 4 * i + c
                    at_least(a, sent[c], i * 32)
                    a.activation(z3[:, c], tile_of(n), ACT.Identity,
                                 bias=var[:, bass.ds(n, 1)], scale=rstd2[:, bass.ds(n, 1)]).then_inc(z3_ready, 1)

                for c in range(4):
                    rows(0, c)
                with a.Fori(1, LH) as i:
                    for c in range(4):
                        rows(i, c)
                rows(LH, 0)

            @block.vector
            def _(v):
                ch = Chain(v, dve)
                link = ch.link

                def x1(n, s):
                    v.wait_ge(gnn_mm, n + 1)
                    v.tensor_tensor(tile_of(n), bank[2 + s][:, 0:C], part[:, bass.ds(n, 1), :].rearrange("p a c -> p (a c)"),
                                    ALU.add).then_inc(x1_ready, 1)

                def stat(n):
                    v.wait_ge(x1_ready, n + 1)
                    v.sem_inc(hold, 1)
                    v.bn_stats(stats[:, bass.ds(n, 1), :].rearrange("p a c -> p (a c)"), tile_of(n)).then_inc(stat_ok, 1)

                def twice_mean(n, s):
                    v.wait_ge(stat_ok, n + 1)
                    at_least(v, u_ready, n - 1)
                    ch.tick(v.tensor_tensor(two[:, s], stats[:, bass.ds(n, 1), 1:2].rearrange("p a c -> p (a c)"),
                                            stats[:, bass.ds(n, 1), 4:5].rearrange("p a c -> p (a c)"), ALU.add))

                def centre(n, s):
                    ch.settle()
                    at_least(v, uT_mm, n - 1)
                    v.tensor_scalar(u[:, s], tile_of(n), 2.0, two[:, s], ALU.mult, ALU.subtract).then_inc(u_ready, 1)

                def logits(n, s):
                    v.wait_ge(lg_mm, n + 1)
                    v.tensor_copy(lg[:, bass.ds(n, 1), :].rearrange("p a e -> p (a e)"), bank[6 + s][:, 0:EXPERTS])\
                     .then_inc(lg_ready, 1)

                def lap(i):
                    for s in range(2):
                        n = 2 * i + s
                        if within(n + 2):
                            x1(n + 2, s)
                        twice_mean(n + 1, 1 - s)
                        if within(n + 2):
                            stat(n + 2)
                        centre(n + 1, 1 - s)
                        if not isinstance(n, int) or n > 0:
                            logits(n - 1, 1 - s)

                x1(0, 0)
                stat(0)
                x1(1, 1)
                twice_mean(0, 0)
                stat(1)
                centre(0, 0)
                lap(0)
                with v.Fori(1, PAIRS - 1) as i:
                    ch.enter(i - 1, 2)
                    lap(i)
                    ch.leave(PAIRS - 2)
                lap(PAIRS - 1)
                logits(NT - 2, 1)
                logits(NT - 1, 0)
                mean_var(v, link, stats, stat_mean[:], var[:], stat_a[:])
                double_norm(v, link, var[:], rstd[:], rstd2[:], stat_a[:], stat_b[:])
                v.wait_ge(u_ready, NT)
                link(v.scalar_tensor_tensor(var[:], stat_mean[:], -1.0, rstd2[:], ALU.mult, ALU.mult))
                v.sem_inc(norms_ready, 1)
                v.wait_ge(lg_ready, NT)
                spread = lambda a: a.unsqueeze(2).broadcast_to([P, NT, EXPERTS])
                link(v.scalar_tensor_tensor(lg[:], lg[:], 0.5, spread(rstd[:]), ALU.mult, ALU.mult))
                link(v.tensor_tensor(lg[:], lg[:], brb[:].unsqueeze(1).broadcast_to([P, NT, EXPERTS]), ALU.add))

                link(v.tensor_scalar(rev[:], ids[:, 0:EXPERTS], -1.0, float(EXPERTS), ALU.mult, ALU.add))
                rev_b = rev[:].unsqueeze(1).broadcast_to([P, NT, EXPERTS])
                for c, best_c in enumerate((best[:, 0, :], best[:, 1, :])):
                    choice = key2[:, c * NT:c * NT + NT]
                    link(v.tensor_reduce(best_c, lg[:], AX, ALU.max))
                    link(v.tensor_tensor(eq[:], lg[:], spread(best_c), ALU.is_equal))
                    link(v.tensor_tensor(eq[:], eq[:], rev_b, ALU.mult))
                    link(v.tensor_reduce(choice, eq[:], AX, ALU.max))
                    if c == 0:
                        link(v.tensor_tensor(eq[:], rev_b, spread(choice), ALU.is_equal))
                        link(v.scalar_tensor_tensor(lg[:], eq[:], -3.0e38, lg[:], ALU.mult, ALU.add))
                    link(v.tensor_scalar(choice, choice, -1.0, float(EXPERTS), ALU.mult, ALU.add))
                    link(v.tensor_scalar(choice, choice, float(EXPERTS - 1), None, ALU.min))
                link(v.tensor_tensor(second[:], best[:, 1, :], best[:, 0, :], ALU.subtract))
                v.sem_inc(diff_ready, 1)

                link(v.memset(pos[:], 0.0))
                count_keys(v, ch, key2[:], (mask[:], mask2[:]), ids, counts[:], EXPERTS, EXPERTS)
                v.sem_inc(counted, 1)
                v.wait_ge(summed, 1)
                bucket_starts(v, ch, bank[2], EXPERTS, TILE_TOKENS, cum[:], size[:], off[:], t_int[:], ones[:, 0:EXPERTS])
                tile_owner(v, ch, cum[:], EXPERTS, part_ids[:], ge[:], own_f[:], own_i[:], 1)
                v.sem_inc(owners, 1)
                place_keys(v, ch, key2[:], (mask[:], mask2[:]), (scan[:], scan2[:]), pos[:], ids, off[:], EXPERTS, EXPERTS, hold)
                link(v.tensor_scalar(pos[:], pos[:], -1.0, None, ALU.add))
                link(v.tensor_copy(idx[:].rearrange("p n a -> p a n"), pos[:].rearrange("p (a n) -> p a n", a=2)))
                v.sem_inc(placed, 1)
                v.wait_ge(exp_ready, 1)
                link(v.tensor_scalar(first[:], second[:], 1.0, None, ALU.add))
                link(v.reciprocal(wgt[:, 0, :], first[:]))
                link(v.tensor_tensor(wgt[:, 1, :], wgt[:, 0, :], second[:], ALU.mult))

            @block.gpsimd
            def _(pool):
                def send(i, s, tiles=2):
                    for c in range(2 * s, 2 * s + tiles):
                        at_least(pool, sent[c], i * 32)
                    pool.sem_inc(hold, 1)
                    n = 4 * i + 2 * s
                    pool.tensor_copy(ring[:, s, 0:2 * tiles], idx[:, bass.ds(n, tiles), :].rearrange("p n a -> p (n a)"))\
                        .then_inc(ring_ready, 1)
                    pool.wait_ge(ring_ready, 2 * i + s + 1)
                    pool.sem_inc(hold, 1)
                    for c in range(tiles):
                        pool.wait_ge(z3_ready, n + c + 1)
                        pool.sem_inc(hold, 1)
                        for j in range(2):
                            at = 2 * c + j
                            pool.indirect_dma_start(
                                out=xs_d, out_offset=bass.IndirectOffsetOnAxis(ap=ring[:, s, at:at + 1], axis=0),
                                in_=z3[:, 2 * s + c, :], in_offset=None).then_inc(sent[2 * s + c], 16)

                pool.wait_ge(placed, 1)
                for s in range(2):
                    send(0, s)
                with pool.Fori(1, LH) as i:
                    for s in range(2):
                        send(i, s)
                send(LH, 0, 1)
                for c in range(4):
                    pool.wait_ge(sent[c], 32 * (LH + (c == 0)))

        c5 = ExitStack()
        with c5:
            sb, ps, sem = tools(c5, "b5")
            xs = sb("xs", [P, 2, 2, C])
            xeT = sb("xeT", [P, KC, TILE_TOKENS])
            W_SIZE, X_SIZE = 2 * KC * HID, 2 * KC * TILE_TOKENS
            w_hi, w_lo = (part_mem[:, n * W_SIZE:(n + 1) * W_SIZE].rearrange("p (s k h) -> p s k h", s=2, k=KC)
                          for n in range(2))
            x_hi, x_lo = (part_mem[:, 2 * W_SIZE + n * X_SIZE:2 * W_SIZE + (n + 1) * X_SIZE]
                          .rearrange("p (s k c) -> p s k c", s=2, k=KC) for n in range(2))
            h_hi = part_mem[:, SPLIT - HB * TILE_TOKENS:SPLIT].rearrange("p (j c) -> p j c", j=HB)
            h_lo = sb("h_lo", [P, HB, TILE_TOKENS])
            w2_hi = sb("w2_hi", [P, 2, HB, C])
            w2_lo = sb("w2_lo", [P, 2, HB, C])
            hT = sb("hT", [P, HB, TILE_TOKENS])
            ys = sb("ys", [P, 2, 2, C])
            bank = [ps(f"bank{n}", [P, 512]) for n in range(8)]
            xs_in = [sem(f"xs_in{n}") for n in range(2)]
            up_in = [sem(f"up_in{n}") for n in range(2)]
            vec_in = [sem(f"vec_in{n}") for n in range(2)]
            down_in = sem("down_in")
            w2_hi_ready = sem("w2_hi_ready")
            w2_split = sem("w2_split")
            h_split = sem("h_split")
            xsT_mm = sem("xsT_mm")
            xeT_ready = sem("xeT_ready")
            w_split = sem("w_split")
            x_split = sem("x_split")
            dve = sem("dve")
            up_mm = sem("up_mm")
            gelu = sem("gelu")
            gelu_hi = sem("gelu_hi")
            y_mm = sem("y_mm")
            y_half = sem("y_half")
            y_out = [sem(f"y_out{n}") for n in range(2)]
            block = c5.enter_context(nc.Block())
            rows_at = lambda d, t: d[bass.ds(t * TILE_TOKENS, TILE_TOKENS), :].rearrange("(t p) c -> p t c", p=P)
            HALF = ETILES // 2
            BY_ACT = (0, 1, 4, 5)

            def upper_until(j):
                return sum(b <= j for b in BY_ACT) if j >= 0 else -sum(b > j + HB for b in BY_ACT)

            @block.sync
            def _(sp):
                def load_rows(t, s):
                    at_least(sp, xsT_mm, t - 1)
                    sp.dma_start(xs[:, s], rows_at(xs_d, t)).then_inc(xs_in[s], 16)

                def store(t, s):
                    sp.wait_ge(y_half, 2 * t + 2)
                    sp.dma_start(rows_at(ys_d, t), ys[:, s]).then_inc(y_out[s], 16)

                def ahead(t, s):
                    load_rows(t + 2, s)
                    e = expert_of(t + 2)
                    sp.wait_ge(w_split, t + 1)
                    load_up(sp, e, s, up_in[s])
                    sp.wait_ge(gelu, t * HB + HB)
                    sp.wait_ge(y_half, 2 * t + 2)
                    load_vectors(sp, e, s, vec_in[s])
                    store(t, s)
                    sp.wait_ge(w2_split, t + 2)
                    load_down(sp, e, down_in)

                for t in range(2):
                    load_rows(t, t)
                sp.wait_ge(w2_split, 1)
                load_down(sp, expert_of(1), down_in)
                with sp.Fori(0, HALF - 1) as i:
                    for s in range(2):
                        ahead(2 * i + s, s)
                for s in range(2):
                    store(ETILES - 2 + s, s)
                for s in range(2):
                    sp.wait_ge(y_out[s], 16 * HALF)

            @block.tensor
            def _(pe):
                def turn(i, s):
                    t, h = 2 * i + s, s % 2
                    pe.wait_ge(xs_in[h], (i + s // 2) * 16 + 16)
                    at_least(pe, xeT_ready, 2 * t)
                    for k in range(KC):
                        for j in range(2):
                            mm = pe.transpose(bank[0][:, k * C + j * P:k * C + j * P + P], xs[:, h, j, k * P:k * P + P], ident[:])
                    mm.then_inc(xsT_mm, 1)

                def up(i, s):
                    t = 2 * i + s
                    pe.wait_ge(w_split, t + 1)
                    pe.wait_ge(x_split, t + 1)
                    for j in range(HB):
                        at_least(pe, gelu, t * HB + j - 3)
                        at_least(pe, gelu_hi, t * len(BY_ACT) + upper_until(j - 4))
                        for k in range(KC):
                            for n, (wp, xp_) in enumerate(((w_hi, x_hi), (w_hi, x_lo), (w_lo, x_hi))):
                                mm = pe.matmul(bank[1 + j % 4][:, 0:TILE_TOKENS],
                                               wp[:, s, k, j * P:j * P + P].bitcast(F32R), xp_[:, s, k, :].bitcast(F32R),
                                               start=(k == 0 and n == 0), stop=(k == KC - 1 and n == 2))
                        mm.then_inc(up_mm, 1)

                def down(i, s):
                    t = 2 * i + s
                    pe.wait_ge(w2_split, t + 1)
                    for n in range(2):
                        at_least(pe, y_half, 2 * t - 1 + n)
                        for j in range(HB):
                            if n == 0:
                                pe.wait_ge(h_split, t * (HB // 2) + j // 2 + 1)
                            for m, (hp, wp) in enumerate(((h_hi, w2_hi), (h_lo, w2_hi), (h_hi, w2_lo))):
                                mm = pe.matmul(bank[5 + n][:, 0:C], hp[:, j, n * P:n * P + P].bitcast(F32R),
                                               wp[:, s, j, :].bitcast(F32R),
                                               start=(j == 0 and m == 0), stop=(j == HB - 1 and m == 2))
                        mm.then_inc(y_mm, 1)

                def lap(i):
                    for s in range(2):
                        up(i, s)
                        turn(i, s + 1)
                        down(i, s)

                turn(0, 0)
                lap(0)
                with pe.Fori(1, HALF - 1) as i:
                    lap(i)
                up(HALF - 1, 0)
                turn(HALF - 1, 1)
                down(HALF - 1, 0)
                up(HALF - 1, 1)
                down(HALF - 1, 1)

            @block.scalar
            def _(a):
                def scale(i, s):
                    t, h = 2 * i + s, s % 2
                    a.wait_ge(xsT_mm, t + 1)
                    at_least(a, vec_in[h], (i + s // 2) * 32)
                    at_least(a, x_split, t)
                    for k in range(KC):
                        a.activation(xeT[:, k, :], bank[0][:, k * C:k * C + TILE_TOKENS], ACT.Identity,
                                     bias=vec[:, h, KC + k:KC + k + 1], scale=vec[:, h, k:k + 1]).then_inc(xeT_ready, 1)

                def gelus(i, s):
                    t = 2 * i + s
                    for j in range(HB):
                        a.wait_ge(up_mm, t * HB + j + 1)
                        at_least(a, h_split, (t - 1) * (HB // 2) + j // 2 + 1)
                        at_least(a, y_mm, 2 * t)
                        for to, done in ((hT[:, j, :], gelu), (h_hi[:, j, :].bitcast(F32R), gelu_hi))[:1 + (j in BY_ACT)]:
                            a.activation(to, bank[1 + j % 4][:, 0:TILE_TOKENS], ACT.Gelu,
                                         bias=vec[:, s, 2 * KC + j:2 * KC + j + 1]).then_inc(done, 1)

                def upper_w2(i, s):
                    t = 2 * i + s
                    at_least(a, down_in, t * 16)
                    at_least(a, y_mm, 2 * t - 2)
                    at_least(a, w2_split, t - 1)
                    a.activation(w2_hi[:, s % 2].bitcast(F32R), E2[:], ACT.Copy).then_inc(w2_hi_ready, 1)

                def lap(i):
                    for s in range(2):
                        gelus(i, s)
                        scale(i, s + 1)
                        upper_w2(i, s + 1)

                scale(0, 0)
                upper_w2(0, 0)
                lap(0)
                with a.Fori(1, HALF - 1) as i:
                    lap(i)
                gelus(HALF - 1, 0)
                scale(HALF - 1, 1)
                upper_w2(HALF - 1, 1)
                gelus(HALF - 1, 1)

            @block.vector
            def _(v):
                ch = Chain(v, dve)

                def take(i, s):
                    t = 2 * i + s
                    at_least(v, vec_in[s], i * 32)
                    at_least(v, y_out[s], i * 16)
                    for n in range(2):
                        v.wait_ge(y_mm, 2 * t + n + 1)
                        v.tensor_tensor(ys[:, s, n, :], bank[5 + n][:, 0:C], b2e[:, s, :], ALU.add).then_inc(y_half, 1)

                def lower(x, hi, lo, done):
                    v.tensor_tensor(lo.bitcast(F32R), x, hi, ALU.subtract).then_inc(done, 1)

                def split(x, hi, lo, done):
                    ch.link(v.tensor_copy(hi.bitcast(F32R), x))
                    lower(x, hi, lo, done)

                def split_w(i, s):
                    t, h = 2 * i + s, s % 2
                    at_least(v, up_in[h], (i + s // 2) * 16)
                    at_least(v, up_mm, (t - 1) * HB)
                    split(E1[:, h], w_hi[:, h], w_lo[:, h], w_split)

                def split_x(i, s):
                    t, h = 2 * i + s, s % 2
                    v.wait_ge(xeT_ready, 2 * t + 2)
                    at_least(v, up_mm, (t - 1) * HB)
                    split(xeT[:], x_hi[:, h], x_lo[:, h], x_split)

                def split_h(i, s):
                    t = 2 * i + s
                    at_least(v, y_mm, 2 * t)
                    for j in range(0, HB, 2):
                        v.wait_ge(gelu, t * HB + j + 2)
                        if j in BY_ACT:
                            v.wait_ge(gelu_hi, t * len(BY_ACT) + upper_until(j + 1))
                        parts = lower if j in BY_ACT else split
                        parts(hT[:, j:j + 2], h_hi[:, j:j + 2], h_lo[:, j:j + 2], h_split)

                def lower_w2(i, s):
                    t = 2 * i + s
                    v.wait_ge(w2_hi_ready, t + 1)
                    at_least(v, down_in, t * 16)
                    at_least(v, y_mm, 2 * t - 2)
                    lower(E2[:], w2_hi[:, s % 2], w2_lo[:, s % 2], w2_split)

                def step(i, s):
                    split_h(i, s)
                    split_x(i, s + 1)
                    split_w(i, s + 1)
                    lower_w2(i, s + 1)
                    take(i, s)

                split_w(0, 0)
                split_x(0, 0)
                lower_w2(0, 0)
                step(0, 0)
                step(0, 1)
                with v.Fori(1, HALF - 1) as i:
                    ch.enter(i - 1, 2 * (2 + (HB - len(BY_ACT)) // 2))
                    step(i, 0)
                    step(i, 1)
                    ch.leave(HALF - 2)
                split_h(HALF - 1, 0)
                split_x(HALF - 1, 1)
                split_w(HALF - 1, 1)
                lower_w2(HALF - 1, 1)
                take(HALF - 1, 0)
                split_h(HALF - 1, 1)
                take(HALF - 1, 1)

        c6 = ExitStack()
        with c6:
            sb, ps, sem = tools(c6, "b6")
            y1 = sb("y1", [P, 4, 2, C])
            o = sb("o", [P, 4, C])
            ring = sb("ring", [P, 2, 4], I32)
            got = [sem(f"got{n}") for n in range(4)]
            ring_ready = sem("ring_ready")
            used = sem("used")
            dve = sem("dve")
            out_done = [sem(f"out_done{n}") for n in range(4)]
            block = c6.enter_context(nc.Block())

            @block.gpsimd
            def _(pool):
                def fetch(i, s, tiles=2):
                    n = 4 * i + 2 * s
                    at_least(pool, used, n + tiles - 4)
                    pool.sem_inc(hold, 1)
                    pool.tensor_copy(ring[:, s, 0:2 * tiles], idx[:, bass.ds(n, tiles), :].rearrange("p n a -> p (n a)"))\
                        .then_inc(ring_ready, 1)
                    pool.wait_ge(ring_ready, 2 * i + s + 1)
                    pool.sem_inc(hold, 1)
                    for c in range(tiles):
                        for j in range(2):
                            at = 2 * c + j
                            pool.indirect_dma_start(
                                out=y1[:, 2 * s + c, j, :], out_offset=None, in_=ys_d,
                                in_offset=bass.IndirectOffsetOnAxis(ap=ring[:, s, at:at + 1], axis=0))\
                                .then_inc(got[2 * s + c], 16)

                for s in range(2):
                    fetch(0, s)
                with pool.Fori(1, LH) as i:
                    for s in range(2):
                        fetch(i, s)
                fetch(LH, 0, 1)

            @block.vector
            def _(v):
                ch = Chain(v, dve)

                def combine(i, c):
                    n = 4 * i + c
                    v.wait_ge(got[c], i * 32 + 32)
                    at_least(v, out_done[c], i * 16)
                    tile = acc[:, bass.ds(n, 1), :].rearrange("p a c -> p (a c)")
                    ch.link(v.scalar_tensor_tensor(o[:, c], y1[:, c, 0], wgt[:, 0, bass.ds(n, 1)], tile, ALU.mult, ALU.add))
                    v.scalar_tensor_tensor(o[:, c], y1[:, c, 1], wgt[:, 1, bass.ds(n, 1)], o[:, c], ALU.mult, ALU.add)\
                     .then_inc(used, 1)

                for c in range(4):
                    combine(0, c)
                with v.Fori(1, LH) as i:
                    ch.enter(i - 1, 4)
                    for c in range(4):
                        combine(i, c)
                    ch.leave(LH - 1)
                combine(LH, 0)

            @block.sync
            def _(sp):
                def store(i, c):
                    n = 4 * i + c
                    sp.wait_ge(used, n + 1)
                    sp.dma_start(out[bass.ds(n * P, P), :], o[:, c]).then_inc(out_done[c], 16)

                with sp.Fori(0, LH) as i:
                    for c in range(4):
                        store(i, c)
                store(LH, 0)
                for c in range(4):
                    sp.wait_ge(out_done[c], 16 * (LH + (c == 0)))


def kernel(x, src, dst, **weights):
    import numpy as np
    from concourse import bacc
    from concourse.bass_utils import run_bass_kernel_spmd

    x, src, dst = np.asarray(x), np.asarray(src), np.asarray(dst)
    g = {k: np.asarray(a) for k, a in weights.items()}
    nodes = x.shape[0]
    tiles = -(-nodes // P)
    xp = np.zeros((tiles * P, C), x.dtype)
    xp[:nodes] = x
    ecols = -(-src.shape[0] // P)
    ecols += -ecols % 32
    sp = np.full(ecols * P, tiles * P - 1, src.dtype)
    sp[:src.shape[0]] = src
    dp = np.zeros(ecols * P, dst.dtype)
    dp[:dst.shape[0]] = dst
    T = lambda a: np.ascontiguousarray(a.T)
    col = lambda a: a.reshape(-1, P).T
    row = lambda a: a.reshape(1, -1)
    m = lambda n: g["L0_mix_" + n]
    f = lambda n: g["L0_ffn_" + n]
    arrays = {
        "x": xp, "src": sp.reshape(P, ecols), "dst": dp.reshape(P, ecols),
        "mix_WxT": T(m("Wx")), "mix_Wx": m("Wx"), "mix_WoT": T(m("Wo")), "mix_WqT": T(m("Wq")), "mix_WkT": T(m("Wk")),
        "mix_Wv": m("Wv"), "mix_W1T": T(m("W1")), "mix_W2T": T(m("W2")),
        "gnn_W1T": T(g["L0_gnn_W1"]), "gnn_W2": g["L0_gnn_W2"],
        "cols": np.concatenate([col(a) for a in (m("ln1_w"), m("ln1_b"), m("bx"), m("ln2_w"), m("ln2_b"), m("b1"),
                                                 g["L0_gnn_b1"])], axis=1),
        "mix_bx": row(m("bx")), "gnn_b2": row(g["L0_gnn_b2"]), "mix_b2": row(m("b2")), "mix_bo": row(m("bo")),
        "ffn_Wr": f("Wr"), "ffn_br": row(f("br")),
        "ffn_W1": f("W1").reshape(-1, f("W1").shape[2]), "ffn_W2": f("W2").reshape(-1, C),
        "ffn_vec": np.concatenate([f(n).reshape(EXPERTS, -1, P).transpose(0, 2, 1) for n in ("ln_g", "ln_b", "b1")], axis=2),
        "ffn_b2": f("b2"),
    }
    nc = bacc.Bacc("TRN2", target_bir_lowering=False, num_devices=1)
    aps, maps = {}, {}
    for name, a in arrays.items():
        a = np.ascontiguousarray(a)
        maps[f"in_{name}"] = a
        aps[name] = nc.dram_tensor(f"in_{name}", a.shape, mybir.dt.from_np(a.dtype), kind="ExternalInput").ap()
    out = nc.dram_tensor("out", xp.shape, F32, kind="ExternalOutput").ap()
    gps_layer(nc, aps, out, nodes, ecols)
    r = run_bass_kernel_spmd(nc, [maps], core_ids=[0])
    return r.results[0]["out"][:nodes]
```
